# Optimizing a Trainium2 kernel written in Bass

```python
import numpy as np
import jax
import jax.numpy as jnp

def _softmax(x, axis=-1):
    return jax.nn.softmax(x, axis=axis)

def _gelu(x):
    return jax.nn.gelu(x, approximate=True)

def _silu(x):
    return jax.nn.silu(x)

def _sigmoid(x):
    return jax.nn.sigmoid(x)

def _layernorm(x, axis=-1, eps=1e-05):
    m = jnp.mean(x, axis=axis, keepdims=True)
    v = jnp.var(x, axis=axis, keepdims=True)
    return (x - m) / jnp.sqrt(v + eps)

def _scatter_add(tgt, idx, src, axis=0):
    return tgt.at[idx].add(src)

def _segment_sum(src, seg, n):
    return jax.ops.segment_sum(src, seg, n)
kernel_name = 'mk_seq_preln_d4_jaxref_r8_fa8135'

def setup_inputs(seed: int=0):
    np.random.seed(seed)
    _w = jnp.asarray

    def _L0_attn_setup():
        import jax, jax.numpy as jnp
        import numpy as np
        B, S, E, H = (4, 256, 256, 16)
        D = E // H
        ROPE_BASE = 10000.0

        def rope(x, base=ROPE_BASE, offset=0):
            d = x.shape[-1]
            s = x.shape[-2]
            inv_freq = base ** (-jnp.arange(0, d, 2, dtype=jnp.float32) / d)
            pos = jnp.arange(offset, s + offset, dtype=jnp.float32)
            ang = pos[:, None] * inv_freq
            sin, cos = (jnp.sin(ang), jnp.cos(ang))
            xe, xo = (x[..., 0::2], x[..., 1::2])
            re = xe * cos - xo * sin
            ro = xe * sin + xo * cos
            return jnp.stack([re, ro], axis=-1).reshape(x.shape)
        key = jax.random.key(seed)
        ks = jax.random.split(key, 9)
        w = lambda k, shp: jax.random.normal(k, shp, dtype=jnp.float32) * 0.02
        return {'x': jax.random.normal(ks[0], (B, S, E), dtype=jnp.float32), 'Wq': w(ks[1], (E, E)), 'bq': w(ks[2], (E,)), 'Wk': w(ks[3], (E, E)), 'bk': w(ks[4], (E,)), 'Wv': w(ks[5], (E, E)), 'bv': w(ks[6], (E,)), 'Wo': w(ks[7], (E, E)), 'bo': w(ks[8], (E,))}
    _L0_attn_in = _L0_attn_setup()

    def _L0_ffn_setup():
        import jax, jax.numpy as jnp
        import numpy as np
        E = 16
        D = 256
        H = 176
        HS = 2 * 176
        TOP_K = 6
        ROUTE_SCALE = 1.0
        key = jax.random.key(seed)
        ks = jax.random.split(key, 16)
        s = 0.02
        return {'x': jax.random.normal(ks[0], (4, 128, D), dtype=jnp.float32), 'gate_w': jax.random.normal(ks[1], (E, D), dtype=jnp.float32) * s, 'gate_b': jax.random.normal(ks[2], (E,), dtype=jnp.float32) * s, 'w1': jax.random.normal(ks[3], (E, H, D), dtype=jnp.float32) * s, 'b1': jax.random.normal(ks[4], (E, H), dtype=jnp.float32) * s, 'w2': jax.random.normal(ks[5], (E, D, H), dtype=jnp.float32) * s, 'b2': jax.random.normal(ks[6], (E, D), dtype=jnp.float32) * s, 'w3': jax.random.normal(ks[7], (E, H, D), dtype=jnp.float32) * s, 'b3': jax.random.normal(ks[8], (E, H), dtype=jnp.float32) * s, 'ws1': jax.random.normal(ks[9], (HS, D), dtype=jnp.float32) * s, 'bs1': jax.random.normal(ks[10], (HS,), dtype=jnp.float32) * s, 'ws2': jax.random.normal(ks[11], (D, HS), dtype=jnp.float32) * s, 'bs2': jax.random.normal(ks[12], (D,), dtype=jnp.float32) * s, 'ws3': jax.random.normal(ks[13], (HS, D), dtype=jnp.float32) * s, 'bs3': jax.random.normal(ks[14], (HS,), dtype=jnp.float32) * s}
    _L0_ffn_in = _L0_ffn_setup()

    def _L1_attn_setup():
        import jax, jax.numpy as jnp
        import numpy as np
        NQ, NKV, HD, SW = (32, 8, 64, 64)
        QM = NQ // NKV

        def _rope_tables(L):
            inv_freq = (1.0 / 1024.0) ** jnp.linspace(0.0, 1.0, HD // 4)
            inv_freq = jnp.concatenate([inv_freq, jnp.zeros(HD // 4)])
            theta = jnp.arange(L, dtype=jnp.float32)[:, None] * inv_freq[None, :]
            return (jnp.cos(theta), jnp.sin(theta))

        def _apply_rope(x, cos, sin):
            x1, x2 = jnp.split(x, 2, axis=-1)
            return jnp.concatenate([x1 * cos + x2 * sin, -x1 * sin + x2 * cos], axis=-1)
        key = jax.random.key(seed)
        k1, k2, k3 = jax.random.split(key, 3)
        B, L, D = (1, 256, 256)
        x = jax.random.normal(k1, (B, L, D), jnp.float32)
        W_qkv = jax.random.normal(k2, (D, (NQ + 2 * NKV) * HD), jnp.float32) * 0.02
        W_out = jax.random.normal(k3, (NQ * HD, D), jnp.float32) * 0.02
        s = jnp.zeros((1, NKV, QM), jnp.float32)
        return {'x': x, 'W_qkv': W_qkv, 'W_out': W_out, 's': s}
    _L1_attn_in = _L1_attn_setup()

    def _L1_ffn_setup():
        import jax, jax.numpy as jnp
        import numpy as np
        B_, S, D = (2, 256, 256)
        F_ = 1024
        R = 16
        H = 16
        HD = D // H
        MOD_SCALE = 0.1
        EPS = 1e-06

        def _rmsnorm(x, w):
            v = jnp.mean(x * x, axis=-1, keepdims=True)
            return x * jax.lax.rsqrt(v + EPS) * w

        def _attention(x, Wq, Wk, Wv, Wo):
            b, s, d = x.shape
            q = (x @ Wq.T).reshape(b, s, H, HD)
            k = (x @ Wk.T).reshape(b, s, H, HD)
            v = (x @ Wv.T).reshape(b, s, H, HD)
            scores = jnp.einsum('bqhd,bkhd->bhqk', q, k) / np.sqrt(HD).astype(np.float32)
            causal = jnp.tril(jnp.ones((s, s), bool))
            scores = jnp.where(causal, scores, jnp.finfo(scores.dtype).min)
            probs = jax.nn.softmax(scores, axis=-1)
            out = jnp.einsum('bhqk,bkhd->bqhd', probs, v).reshape(b, s, d)
            return out @ Wo.T
        key = jax.random.key(seed)
        ks = jax.random.split(key, 12)
        sd = 0.02
        return {'hidden_states': jax.random.normal(ks[0], (B_, S, D), jnp.float32), 'ln1_w': jnp.ones((D,), jnp.float32), 'ln2_w': jnp.ones((D,), jnp.float32), 'Wq': jax.random.normal(ks[1], (D, D), jnp.float32) * sd, 'Wk': jax.random.normal(ks[2], (D, D), jnp.float32) * sd, 'Wv': jax.random.normal(ks[3], (D, D), jnp.float32) * sd, 'Wo': jax.random.normal(ks[4], (D, D), jnp.float32) * sd, 'A': jax.random.normal(ks[5], (D, R), jnp.float32) * (0.01 / np.sqrt(D)), 'B': jax.random.normal(ks[6], (R, F_), jnp.float32) * (0.01 / np.sqrt(R)), 'W_in_base': jax.random.normal(ks[7], (F_, D), jnp.float32) * sd, 'W_up_base': jax.random.normal(ks[8], (F_, D), jnp.float32) * sd, 'W_down': jax.random.normal(ks[9], (D, F_), jnp.float32) * sd}
    _L1_ffn_in = _L1_ffn_setup()

    def _L2_attn_setup():
        import jax, jax.numpy as jnp
        import numpy as np
        H = 16
        DK = 128
        DV = 128
        M = 64
        EPS = 1e-05
        CLAMP = 32.0
        ROPE_BASE = 10000.0

        def _rope(x, cos, sin):
            x1, x2 = jnp.split(x, 2, axis=-1)
            return jnp.concatenate([x1 * cos - x2 * sin, x2 * cos + x1 * sin], axis=-1)
        key = jax.random.key(seed)
        ks = jax.random.split(key, 9)
        B, T, D = (1, 256, 256)
        sc = 0.02
        return {'hidden_states': jax.random.normal(ks[0], (B, T, D), jnp.float32), 'Wq': jax.random.normal(ks[1], (H * DK, D), jnp.float32) * sc, 'Wk': jax.random.normal(ks[2], (H * DK, D), jnp.float32) * sc, 'Wv': jax.random.normal(ks[3], (H * DV, D), jnp.float32) * sc, 'Wg': jax.random.normal(ks[4], (H * DV, D), jnp.float32) * sc, 'Wo': jax.random.normal(ks[5], (D, H * DV), jnp.float32) * sc, 'Ws1': jax.random.normal(ks[6], (16, D), jnp.float32) * sc, 'Ws2': jax.random.normal(ks[7], (H * M, 16), jnp.float32) * sc, 'bs2': jnp.zeros((H * M,), jnp.float32), 'g_norm_weight': jnp.ones((DV,), jnp.float32)}
    _L2_attn_in = _L2_attn_setup()

    def _L2_ffn_setup():
        import jax, jax.numpy as jnp
        import numpy as np
        NUM_EXPERTS = 32
        TOP_K = 4
        HIDDEN = 256
        INTER = 96
        key = jax.random.key(seed)
        k1, k2, k3, k4 = jax.random.split(key, 4)
        hidden_states = jax.random.normal(k1, (4, 64, HIDDEN), dtype=jnp.float32)
        gate = jax.random.normal(k2, (HIDDEN, NUM_EXPERTS), dtype=jnp.float32) * 0.02
        gate_up_proj = jax.random.normal(k3, (NUM_EXPERTS, HIDDEN, 2 * INTER), dtype=jnp.float32) * 0.02
        down_proj = jax.random.normal(k4, (NUM_EXPERTS, INTER, HIDDEN), dtype=jnp.float32) * 0.02
        return {'hidden_states': hidden_states, 'gate': gate, 'gate_up_proj': gate_up_proj, 'down_proj': down_proj}
    _L2_ffn_in = _L2_ffn_setup()

    def _L3_attn_setup():
        import jax, jax.numpy as jnp
        import numpy as np
        D_MODEL = 256
        NHEAD = 16
        LN_EPS = 1e-05
        key = jax.random.key(seed)
        ks = jax.random.split(key, 6)
        scale = 1.0 / np.sqrt(D_MODEL)
        return {'x': jax.random.normal(ks[0], (4, 512, D_MODEL), dtype=jnp.float32), 'Wq': jax.random.normal(ks[1], (D_MODEL, D_MODEL), dtype=jnp.float32) * scale, 'Wv': jax.random.normal(ks[2], (D_MODEL, D_MODEL), dtype=jnp.float32) * scale, 'Wg': jax.random.normal(ks[3], (D_MODEL, D_MODEL), dtype=jnp.float32) * scale, 'Wo': jax.random.normal(ks[4], (D_MODEL, D_MODEL), dtype=jnp.float32) * scale, 'beta': jnp.full((NHEAD,), -0.2, dtype=jnp.float32), 'ln_g': jnp.ones((D_MODEL,), dtype=jnp.float32), 'ln_b': jnp.zeros((D_MODEL,), dtype=jnp.float32)}
    _L3_attn_in = _L3_attn_setup()

    def _L3_ffn_setup():
        import jax, jax.numpy as jnp
        import numpy as np
        NUM_EXPERTS = 16
        TOP_K = 4
        N_GROUP = 4
        TOPK_GROUP = 2
        SCALING = 2.5

        def _route(x, gate_weight, expert_bias):
            logits = x @ gate_weight.T
            scores = jax.nn.sigmoid(logits)
            biased = scores + expert_bias[None, :]
            T = x.shape[0]
            gsz = NUM_EXPERTS // N_GROUP
            grp = biased.reshape(T, N_GROUP, gsz)
            top2, _ = jax.lax.top_k(grp, 2)
            group_scores = top2.sum(-1)
            _, gidx = jax.lax.top_k(group_scores, TOPK_GROUP)
            gmask = jax.nn.one_hot(gidx, N_GROUP, dtype=scores.dtype).sum(1)
            emask = jnp.repeat(gmask, gsz, axis=1)
            masked = jnp.where(emask > 0, biased, -jnp.inf)
            _, sel = jax.lax.top_k(masked, TOP_K)
            w = jnp.take_along_axis(scores, sel, axis=1)
            w = w / (w.sum(-1, keepdims=True) + 1e-20)
            return (w * SCALING, sel)

        def _moe(x, w, sel, gate_proj, up_proj, down_proj):
            cw = (jax.nn.one_hot(sel, NUM_EXPERTS, dtype=x.dtype) * w[..., None]).sum(1)

            def body(acc, inp):
                g, u, d, we = inp
                y = jax.nn.silu(x @ g.T) * (x @ u.T) @ d.T
                return (acc + we[:, None] * y, None)
            out, _ = jax.lax.scan(body, jnp.zeros_like(x), (gate_proj, up_proj, down_proj, cw.T))
            return out
        key = jax.random.key(seed)
        ks = jax.random.split(key, 9)
        B, S, H, I = (2, 128, 256, 128)
        w = lambda k, shape: jax.random.normal(k, shape, jnp.float32) * 0.02
        return {'hidden_states': jax.random.normal(ks[0], (B, S, H), jnp.float32), 'gate_weight': w(ks[1], (NUM_EXPERTS, H)), 'expert_bias': jnp.zeros((NUM_EXPERTS,), jnp.float32), 'gate_proj': w(ks[2], (NUM_EXPERTS, I, H)), 'up_proj': w(ks[3], (NUM_EXPERTS, I, H)), 'down_proj': w(ks[4], (NUM_EXPERTS, H, I)), 'shared_gate': w(ks[5], (I, H)), 'shared_up': w(ks[6], (I, H)), 'shared_down': w(ks[7], (H, I))}
    _L3_ffn_in = _L3_ffn_setup()
    _d = {'L0_attn_x': _L0_attn_in['x'], 'L0_attn_Wq': _L0_attn_in['Wq'], 'L0_attn_bq': _L0_attn_in['bq'], 'L0_attn_Wk': _L0_attn_in['Wk'], 'L0_attn_bk': _L0_attn_in['bk'], 'L0_attn_Wv': _L0_attn_in['Wv'], 'L0_attn_bv': _L0_attn_in['bv'], 'L0_attn_Wo': _L0_attn_in['Wo'], 'L0_attn_bo': _L0_attn_in['bo'], 'L0_ffn_gate_w': _L0_ffn_in['gate_w'], 'L0_ffn_gate_b': _L0_ffn_in['gate_b'], 'L0_ffn_w1': _L0_ffn_in['w1'], 'L0_ffn_b1': _L0_ffn_in['b1'], 'L0_ffn_w2': _L0_ffn_in['w2'], 'L0_ffn_b2': _L0_ffn_in['b2'], 'L0_ffn_w3': _L0_ffn_in['w3'], 'L0_ffn_b3': _L0_ffn_in['b3'], 'L0_ffn_ws1': _L0_ffn_in['ws1'], 'L0_ffn_bs1': _L0_ffn_in['bs1'], 'L0_ffn_ws2': _L0_ffn_in['ws2'], 'L0_ffn_bs2': _L0_ffn_in['bs2'], 'L0_ffn_ws3': _L0_ffn_in['ws3'], 'L0_ffn_bs3': _L0_ffn_in['bs3'], 'L1_attn_W_qkv': _L1_attn_in['W_qkv'], 'L1_attn_W_out': _L1_attn_in['W_out'], 'L1_attn_s': _L1_attn_in['s'], 'L1_ffn_ln1_w': _L1_ffn_in['ln1_w'], 'L1_ffn_ln2_w': _L1_ffn_in['ln2_w'], 'L1_ffn_Wq': _L1_ffn_in['Wq'], 'L1_ffn_Wk': _L1_ffn_in['Wk'], 'L1_ffn_Wv': _L1_ffn_in['Wv'], 'L1_ffn_Wo': _L1_ffn_in['Wo'], 'L1_ffn_A': _L1_ffn_in['A'], 'L1_ffn_B': _L1_ffn_in['B'], 'L1_ffn_W_in_base': _L1_ffn_in['W_in_base'], 'L1_ffn_W_up_base': _L1_ffn_in['W_up_base'], 'L1_ffn_W_down': _L1_ffn_in['W_down'], 'L2_attn_Wq': _L2_attn_in['Wq'], 'L2_attn_Wk': _L2_attn_in['Wk'], 'L2_attn_Wv': _L2_attn_in['Wv'], 'L2_attn_Wg': _L2_attn_in['Wg'], 'L2_attn_Wo': _L2_attn_in['Wo'], 'L2_attn_Ws1': _L2_attn_in['Ws1'], 'L2_attn_Ws2': _L2_attn_in['Ws2'], 'L2_attn_bs2': _L2_attn_in['bs2'], 'L2_attn_g_norm_weight': _L2_attn_in['g_norm_weight'], 'L2_ffn_gate': _L2_ffn_in['gate'], 'L2_ffn_gate_up_proj': _L2_ffn_in['gate_up_proj'], 'L2_ffn_down_proj': _L2_ffn_in['down_proj'], 'L3_attn_Wq': _L3_attn_in['Wq'], 'L3_attn_Wv': _L3_attn_in['Wv'], 'L3_attn_Wg': _L3_attn_in['Wg'], 'L3_attn_Wo': _L3_attn_in['Wo'], 'L3_attn_beta': _L3_attn_in['beta'], 'L3_attn_ln_g': _L3_attn_in['ln_g'], 'L3_attn_ln_b': _L3_attn_in['ln_b'], 'L3_ffn_gate_weight': _L3_ffn_in['gate_weight'], 'L3_ffn_expert_bias': _L3_ffn_in['expert_bias'], 'L3_ffn_gate_proj': _L3_ffn_in['gate_proj'], 'L3_ffn_up_proj': _L3_ffn_in['up_proj'], 'L3_ffn_down_proj': _L3_ffn_in['down_proj'], 'L3_ffn_shared_gate': _L3_ffn_in['shared_gate'], 'L3_ffn_shared_up': _L3_ffn_in['shared_up'], 'L3_ffn_shared_down': _L3_ffn_in['shared_down']}
    _x0 = _d['L0_attn_x']
    _d['L0_attn_x'] = jax.random.normal(jax.random.fold_in(jax.random.key(seed), 1), (1, 1024, 256), dtype=_x0.dtype)
    del _x0
    return _d

def reference(L0_attn_x, L0_attn_Wq, L0_attn_bq, L0_attn_Wk, L0_attn_bk, L0_attn_Wv, L0_attn_bv, L0_attn_Wo, L0_attn_bo, L0_ffn_gate_w, L0_ffn_gate_b, L0_ffn_w1, L0_ffn_b1, L0_ffn_w2, L0_ffn_b2, L0_ffn_w3, L0_ffn_b3, L0_ffn_ws1, L0_ffn_bs1, L0_ffn_ws2, L0_ffn_bs2, L0_ffn_ws3, L0_ffn_bs3, L1_attn_W_qkv, L1_attn_W_out, L1_attn_s, L1_ffn_ln1_w, L1_ffn_ln2_w, L1_ffn_Wq, L1_ffn_Wk, L1_ffn_Wv, L1_ffn_Wo, L1_ffn_A, L1_ffn_B, L1_ffn_W_in_base, L1_ffn_W_up_base, L1_ffn_W_down, L2_attn_Wq, L2_attn_Wk, L2_attn_Wv, L2_attn_Wg, L2_attn_Wo, L2_attn_Ws1, L2_attn_Ws2, L2_attn_bs2, L2_attn_g_norm_weight, L2_ffn_gate, L2_ffn_gate_up_proj, L2_ffn_down_proj, L3_attn_Wq, L3_attn_Wv, L3_attn_Wg, L3_attn_Wo, L3_attn_beta, L3_attn_ln_g, L3_attn_ln_b, L3_ffn_gate_weight, L3_ffn_expert_bias, L3_ffn_gate_proj, L3_ffn_up_proj, L3_ffn_down_proj, L3_ffn_shared_gate, L3_ffn_shared_up, L3_ffn_shared_down):

    def _L0_attn_ref(x, Wq, bq, Wk, bk, Wv, bv, Wo, bo):
        import jax, jax.numpy as jnp
        import numpy as np
        B, S, E, H = (4, 256, 256, 16)
        D = E // H
        ROPE_BASE = 10000.0

        def rope(x, base=ROPE_BASE, offset=0):
            d = x.shape[-1]
            s = x.shape[-2]
            inv_freq = base ** (-jnp.arange(0, d, 2, dtype=jnp.float32) / d)
            pos = jnp.arange(offset, s + offset, dtype=jnp.float32)
            ang = pos[:, None] * inv_freq
            sin, cos = (jnp.sin(ang), jnp.cos(ang))
            xe, xo = (x[..., 0::2], x[..., 1::2])
            re = xe * cos - xo * sin
            ro = xe * sin + xo * cos
            return jnp.stack([re, ro], axis=-1).reshape(x.shape)
        b, s, _ = x.shape
        scale = D ** (-0.5)

        def proj(W, bias):
            y = jnp.einsum('bse,fe->bsf', x, W) + bias
            return y.reshape(b, s, H, D).transpose(0, 2, 1, 3)
        q = rope(proj(Wq, bq))
        k = rope(proj(Wk, bk))
        v = proj(Wv, bv)
        attn = jnp.einsum('bhqd,bhkd->bhqk', q, k) * scale
        causal = jnp.triu(jnp.ones((s, s), dtype=bool), k=1)
        attn = jnp.where(causal, -jnp.inf, attn)
        attn_weights = jax.nn.softmax(attn, axis=-1)
        out = jnp.einsum('bhqk,bhkd->bhqd', attn_weights, v)
        out = out.transpose(0, 2, 1, 3).reshape(b, s, E)
        return jnp.einsum('bse,fe->bsf', out, Wo) + bo

    def _L0_ffn_ref(x, gate_w, gate_b, w1, b1, w2, b2, w3, b3, ws1, bs1, ws2, bs2, ws3, bs3):
        import jax, jax.numpy as jnp
        import numpy as np
        E = 16
        D = 256
        H = 176
        HS = 2 * 176
        TOP_K = 6
        ROUTE_SCALE = 1.0
        shape = x.shape
        xf = x.reshape(-1, shape[-1])
        scores = xf @ gate_w.T
        probs = jax.nn.softmax(scores.astype(jnp.float32), axis=-1)
        biased = probs + gate_b
        _, idx = jax.lax.top_k(biased, TOP_K)
        weights = jnp.take_along_axis(probs, idx, axis=1) * ROUTE_SCALE
        weights = weights.astype(x.dtype)
        onehot = jax.nn.one_hot(idx, E, dtype=weights.dtype)
        cw = jnp.einsum('tk,tke->te', weights, onehot)

        def expert_step(y, params):
            W1, B1, W2, B2, W3, B3, c = params
            h = jax.nn.silu(xf @ W1.T + B1) * (xf @ W3.T + B3)
            out = h @ W2.T + B2
            return (y + c[:, None] * out, None)
        y0 = jnp.zeros_like(xf)
        y, _ = jax.lax.scan(expert_step, y0, (w1, b1, w2, b2, w3, b3, cw.T))
        z = jax.nn.silu(xf @ ws1.T + bs1) * (xf @ ws3.T + bs3) @ ws2.T + bs2
        return (y + z).reshape(shape)

    def _L1_attn_ref(x, W_qkv, W_out, s):
        import jax, jax.numpy as jnp
        import numpy as np
        NQ, NKV, HD, SW = (32, 8, 64, 64)
        QM = NQ // NKV

        def _rope_tables(L):
            inv_freq = (1.0 / 1024.0) ** jnp.linspace(0.0, 1.0, HD // 4)
            inv_freq = jnp.concatenate([inv_freq, jnp.zeros(HD // 4)])
            theta = jnp.arange(L, dtype=jnp.float32)[:, None] * inv_freq[None, :]
            return (jnp.cos(theta), jnp.sin(theta))

        def _apply_rope(x, cos, sin):
            x1, x2 = jnp.split(x, 2, axis=-1)
            return jnp.concatenate([x1 * cos + x2 * sin, -x1 * sin + x2 * cos], axis=-1)
        B, L, D = x.shape
        proj = x @ W_qkv
        q, k, v = jnp.split(proj, (NQ * HD, (NQ + NKV) * HD), axis=-1)
        cos, sin = _rope_tables(L)
        q = _apply_rope(q.reshape(B, L, NKV, QM, HD), cos[None, :, None, None, :], sin[None, :, None, None, :])
        k = _apply_rope(k.reshape(B, L, NKV, HD), cos[None, :, None, :], sin[None, :, None, :])
        v = v.reshape(B, L, NKV, HD)
        sm_scale = 1.0 / jnp.sqrt(jnp.float32(HD))
        attn = jnp.einsum('bqhmd,bkhd->bhmqk', q, k) * sm_scale
        q_pos = jnp.arange(L)[:, None]
        k_pos = jnp.arange(L)[None, :]
        mask = (q_pos >= k_pos) & (q_pos < k_pos + SW)
        attn = jnp.where(mask, -jnp.inf, attn)
        sink = jnp.broadcast_to(s[:, :, :, None, None], attn.shape[:-1] + (1,))
        w = jax.nn.softmax(jnp.concatenate([attn, sink], axis=-1), axis=-1)[..., :-1]
        out = jnp.einsum('bhmqk,bkhd->bqhmd', w, v).reshape(B, L, NQ * HD)
        return out @ W_out

    def _L1_ffn_ref(hidden_states, ln1_w, ln2_w, Wq, Wk, Wv, Wo, A, B, W_in_base, W_up_base, W_down):
        import jax, jax.numpy as jnp
        import numpy as np
        B_, S, D = (2, 256, 256)
        F_ = 1024
        R = 16
        H = 16
        HD = D // H
        MOD_SCALE = 0.1
        EPS = 1e-06

        def _rmsnorm(x, w):
            v = jnp.mean(x * x, axis=-1, keepdims=True)
            return x * jax.lax.rsqrt(v + EPS) * w

        def _attention(x, Wq, Wk, Wv, Wo):
            b, s, d = x.shape
            q = (x @ Wq.T).reshape(b, s, H, HD)
            k = (x @ Wk.T).reshape(b, s, H, HD)
            v = (x @ Wv.T).reshape(b, s, H, HD)
            scores = jnp.einsum('bqhd,bkhd->bhqk', q, k) / np.sqrt(HD).astype(np.float32)
            causal = jnp.tril(jnp.ones((s, s), bool))
            scores = jnp.where(causal, scores, jnp.finfo(scores.dtype).min)
            probs = jax.nn.softmax(scores, axis=-1)
            out = jnp.einsum('bhqk,bkhd->bqhd', probs, v).reshape(b, s, d)
            return out @ Wo.T
        residual = hidden_states
        x = _rmsnorm(hidden_states, ln1_w)
        attn = _attention(x, Wq, Wk, Wv, Wo)
        mod = MOD_SCALE * jnp.tanh(attn @ A)
        h = _rmsnorm(residual, ln2_w)
        gate_pre = h @ W_in_base.T + mod * (h @ A) @ B
        gate = jax.nn.silu(gate_pre)
        up = h @ W_up_base.T
        mlp_out = gate * up @ W_down.T
        return residual + mlp_out

    def _L2_attn_ref(hidden_states, Wq, Wk, Wv, Wg, Wo, Ws1, Ws2, bs2, g_norm_weight):
        import jax, jax.numpy as jnp
        import numpy as np
        H = 16
        DK = 128
        DV = 128
        M = 64
        EPS = 1e-05
        CLAMP = 32.0
        ROPE_BASE = 10000.0

        def _rope(x, cos, sin):
            x1, x2 = jnp.split(x, 2, axis=-1)
            return jnp.concatenate([x1 * cos - x2 * sin, x2 * cos + x1 * sin], axis=-1)
        B, T, D = hidden_states.shape
        hs = hidden_states
        q = (hs @ Wq.T).reshape(B, T, H, DK)
        k = (hs @ Wk.T).reshape(B, T, H, DK)
        pos = jnp.arange(T, dtype=jnp.float32)
        inv_freq = 1.0 / ROPE_BASE ** (jnp.arange(0, DK, 2, dtype=jnp.float32) / DK)
        ang = pos[:, None] * inv_freq[None, :]
        cos = jnp.cos(ang)[None, :, None, :]
        sin = jnp.sin(ang)[None, :, None, :]
        q = _rope(q, cos, sin).transpose(0, 2, 1, 3)
        k = _rope(k, cos, sin).transpose(0, 2, 1, 3)
        v = (hs @ Wv.T).reshape(B, T, H, DV).transpose(0, 2, 1, 3)
        s = hs @ Ws1.T @ Ws2.T + bs2
        s = jnp.clip(s, -CLAMP, CLAMP).reshape(B, T, H, M).transpose(0, 2, 1, 3)
        z = jax.lax.cumlogsumexp(s, axis=2)
        es = jnp.exp(s)
        enz = jnp.exp(-z)
        scale = DK ** (-0.5)
        mask = jnp.tril(jnp.ones((T, T), dtype=bool))
        A = jnp.einsum('bhtd,bhjd->bhtj', q, k) * scale
        A = jnp.where(mask, A, 0.0)
        ok = enz * jnp.einsum('bhtj,bhjm->bhtm', A, es)
        qv = jax.nn.softmax(ok, axis=-1)
        W2 = jnp.einsum('bhtm,bhjm->bhtj', qv * enz, es)
        W2 = jnp.where(mask, W2, 0.0)
        o = jnp.einsum('bhtj,bhjd->bhtd', W2, v)
        o = o.transpose(0, 2, 1, 3)
        g = (hs @ Wg.T).reshape(B, T, H, DV)
        o_n = o * jax.lax.rsqrt(jnp.mean(o * o, axis=-1, keepdims=True) + EPS) * g_norm_weight
        o_g = o_n * (g * jax.nn.sigmoid(g))
        return o_g.reshape(B, T, H * DV) @ Wo.T

    def _L2_ffn_ref(hidden_states, gate, gate_up_proj, down_proj):
        import jax, jax.numpy as jnp
        import numpy as np
        NUM_EXPERTS = 32
        TOP_K = 4
        HIDDEN = 256
        INTER = 96
        batch_size = hidden_states.shape[0]
        x = hidden_states.reshape(-1, HIDDEN)
        num_tokens = x.shape[0]
        router_logits = jnp.einsum('TD,DE->TE', x, gate)
        routing_weights = jax.nn.softmax(router_logits.astype(jnp.float32), axis=-1)
        top_k_weights, top_k_indices = jax.lax.top_k(routing_weights, TOP_K)
        top_k_weights = top_k_weights / top_k_weights.sum(axis=-1, keepdims=True)
        top_k_weights = top_k_weights.astype(x.dtype)
        router_weights = jnp.zeros((num_tokens, NUM_EXPERTS), dtype=x.dtype)
        token_indices = jnp.broadcast_to(jnp.arange(num_tokens)[:, None], top_k_indices.shape)
        router_weights = router_weights.at[token_indices, top_k_indices].set(top_k_weights)
        gate_up = jnp.einsum('TD,EDF->TEF', x, gate_up_proj)
        g, u = jnp.split(gate_up, 2, axis=-1)
        gated = u * jax.nn.silu(g)
        next_states = jnp.einsum('TEF,EFD->TED', gated, down_proj)
        next_states = (next_states * router_weights[..., None]).sum(axis=1)
        return next_states.reshape(batch_size, -1, HIDDEN)

    def _L3_attn_ref(x, Wq, Wv, Wg, Wo, beta, ln_g, ln_b):
        import jax, jax.numpy as jnp
        import numpy as np
        D_MODEL = 256
        NHEAD = 16
        LN_EPS = 1e-05
        B, S, D = x.shape
        H = NHEAD
        Dh = D // H
        q = (x @ Wq).reshape(B, S, H, Dh)
        v = (x @ Wv).reshape(B, S, H, Dh)
        lam = jax.nn.sigmoid(beta)[None, :, None]
        v_t = jnp.moveaxis(v, 1, 0)

        def step(prev, vt):
            new = lam * prev + vt
            return (new, new)
        _, rest = jax.lax.scan(step, v_t[0], v_t[1:])
        states = jnp.concatenate([v_t[:1], rest], axis=0)
        states = jnp.moveaxis(states, 0, 1)
        y = (q * states).reshape(B, S, D)
        mu = jnp.mean(y, axis=-1, keepdims=True)
        var = jnp.var(y, axis=-1, keepdims=True)
        y = (y - mu) * jax.lax.rsqrt(var + LN_EPS) * ln_g + ln_b
        gate = jax.nn.silu(x @ Wg)
        y = y * gate
        return y @ Wo

    def _L3_ffn_ref(hidden_states, gate_weight, expert_bias, gate_proj, up_proj, down_proj, shared_gate, shared_up, shared_down):
        import jax, jax.numpy as jnp
        import numpy as np
        NUM_EXPERTS = 16
        TOP_K = 4
        N_GROUP = 4
        TOPK_GROUP = 2
        SCALING = 2.5

        def _route(x, gate_weight, expert_bias):
            logits = x @ gate_weight.T
            scores = jax.nn.sigmoid(logits)
            biased = scores + expert_bias[None, :]
            T = x.shape[0]
            gsz = NUM_EXPERTS // N_GROUP
            grp = biased.reshape(T, N_GROUP, gsz)
            top2, _ = jax.lax.top_k(grp, 2)
            group_scores = top2.sum(-1)
            _, gidx = jax.lax.top_k(group_scores, TOPK_GROUP)
            gmask = jax.nn.one_hot(gidx, N_GROUP, dtype=scores.dtype).sum(1)
            emask = jnp.repeat(gmask, gsz, axis=1)
            masked = jnp.where(emask > 0, biased, -jnp.inf)
            _, sel = jax.lax.top_k(masked, TOP_K)
            w = jnp.take_along_axis(scores, sel, axis=1)
            w = w / (w.sum(-1, keepdims=True) + 1e-20)
            return (w * SCALING, sel)

        def _moe(x, w, sel, gate_proj, up_proj, down_proj):
            cw = (jax.nn.one_hot(sel, NUM_EXPERTS, dtype=x.dtype) * w[..., None]).sum(1)

            def body(acc, inp):
                g, u, d, we = inp
                y = jax.nn.silu(x @ g.T) * (x @ u.T) @ d.T
                return (acc + we[:, None] * y, None)
            out, _ = jax.lax.scan(body, jnp.zeros_like(x), (gate_proj, up_proj, down_proj, cw.T))
            return out
        B, S, H = hidden_states.shape
        x = hidden_states.reshape(-1, H)
        w, sel = _route(x, gate_weight, expert_bias)
        out = _moe(x, w, sel, gate_proj, up_proj, down_proj)
        shared = jax.nn.silu(x @ shared_gate.T) * (x @ shared_up.T) @ shared_down.T
        return (out + shared).reshape(B, S, H)
    x = L0_attn_x
    x = x + _L0_attn_ref(_layernorm(x, axis=-1), L0_attn_Wq, L0_attn_bq, L0_attn_Wk, L0_attn_bk, L0_attn_Wv, L0_attn_bv, L0_attn_Wo, L0_attn_bo)
    x = x + _L0_ffn_ref(_layernorm(x, axis=-1), L0_ffn_gate_w, L0_ffn_gate_b, L0_ffn_w1, L0_ffn_b1, L0_ffn_w2, L0_ffn_b2, L0_ffn_w3, L0_ffn_b3, L0_ffn_ws1, L0_ffn_bs1, L0_ffn_ws2, L0_ffn_bs2, L0_ffn_ws3, L0_ffn_bs3)
    x = x + _L1_attn_ref(_layernorm(x, axis=-1), L1_attn_W_qkv, L1_attn_W_out, L1_attn_s)
    x = x + _L1_ffn_ref(_layernorm(x, axis=-1), L1_ffn_ln1_w, L1_ffn_ln2_w, L1_ffn_Wq, L1_ffn_Wk, L1_ffn_Wv, L1_ffn_Wo, L1_ffn_A, L1_ffn_B, L1_ffn_W_in_base, L1_ffn_W_up_base, L1_ffn_W_down)
    x = x + _L2_attn_ref(_layernorm(x, axis=-1), L2_attn_Wq, L2_attn_Wk, L2_attn_Wv, L2_attn_Wg, L2_attn_Wo, L2_attn_Ws1, L2_attn_Ws2, L2_attn_bs2, L2_attn_g_norm_weight)
    x = x + _L2_ffn_ref(_layernorm(x, axis=-1), L2_ffn_gate, L2_ffn_gate_up_proj, L2_ffn_down_proj)
    x = x + _L3_attn_ref(_layernorm(x, axis=-1), L3_attn_Wq, L3_attn_Wv, L3_attn_Wg, L3_attn_Wo, L3_attn_beta, L3_attn_ln_g, L3_attn_ln_b)
    x = x + _L3_ffn_ref(_layernorm(x, axis=-1), L3_ffn_gate_weight, L3_ffn_expert_bias, L3_ffn_gate_proj, L3_ffn_up_proj, L3_ffn_down_proj, L3_ffn_shared_gate, L3_ffn_shared_up, L3_ffn_shared_down)
    return x

_drawn_inputs = setup_inputs


def setup_inputs(seed=0):
    import zlib

    import numpy as np

    out = dict(_drawn_inputs(seed))
    spreads = {'L1_attn_s': (0.0, 2.0),
     'L1_ffn_ln1_w': (1.0, 0.6),
     'L1_ffn_ln2_w': (1.0, 0.6),
     'L2_attn_bs2': (0.0, 2.0),
     'L2_attn_g_norm_weight': (1.0, 0.6),
     'L3_attn_beta': (-0.20000000298023224, 0.6),
     'L3_attn_ln_g': (1.0, 0.2),
     'L3_attn_ln_b': (0.0, 0.267),
     'L3_ffn_expert_bias': (0.0, 0.8)}
    factors = {'L0_attn_Wq': 8.0,
     'L0_attn_bq': 8.0,
     'L0_attn_Wk': 8.0,
     'L0_attn_bk': 8.0,
     'L0_attn_Wv': 4.059,
     'L0_attn_bv': 4.533,
     'L0_attn_Wo': 2.817,
     'L0_ffn_gate_w': 8.0,
     'L0_ffn_gate_b': 8.0,
     'L0_ffn_w1': 8.0,
     'L0_ffn_b1': 8.0,
     'L0_ffn_w2': 8.0,
     'L0_ffn_b2': 8.0,
     'L0_ffn_w3': 8.0,
     'L0_ffn_b3': 8.0,
     'L0_ffn_bs1': 8.0,
     'L0_ffn_bs3': 8.0,
     'L1_attn_W_qkv': 2.731,
     'L1_ffn_Wq': 64.0,
     'L1_ffn_Wk': 64.0,
     'L1_ffn_Wv': 64.0,
     'L1_ffn_Wo': 64.0,
     'L1_ffn_A': 64.0,
     'L1_ffn_B': 64.0,
     'L1_ffn_W_in_base': 2.929,
     'L1_ffn_W_up_base': 2.889,
     'L1_ffn_W_down': 2.9,
     'L2_attn_Wq': 8.0,
     'L2_attn_Wk': 8.0,
     'L2_attn_Ws1': 8.0,
     'L2_attn_Ws2': 8.0,
     'L2_ffn_gate': 8.0,
     'L2_ffn_gate_up_proj': 8.0,
     'L2_ffn_down_proj': 8.0,
     'L3_ffn_gate_weight': 8.0,
     'L3_ffn_gate_proj': 7.944,
     'L3_ffn_up_proj': 7.861,
     'L3_ffn_down_proj': 7.839,
     'L3_ffn_shared_gate': 8.0,
     'L3_ffn_shared_up': 8.0,
     'L3_ffn_shared_down': 8.0}
    for name, (base, spread) in spreads.items():
        noise = np.random.default_rng([zlib.crc32(name.encode()), seed]).standard_normal(out[name].shape)
        drawn = base * np.exp(spread * noise) if base else spread * noise
        out[name] = jnp.asarray(drawn.astype(out[name].dtype))
    for name, factor in factors.items():
        out[name] = (out[name] * factor).astype(out[name].dtype)
    return out
```

```python
import numpy as np
import concourse.bass as bass
from concourse import mybir
from contextlib import ExitStack

F32 = mybir.dt.float32
F32R = mybir.dt.float32r
BF16 = mybir.dt.bfloat16
ALU = mybir.AluOpType
ACT = mybir.ActivationFunctionType
AX = mybir.AxisListType

P = 128
T = 1024
D = 256
DC = D // P
HALF = 512
NH = T // HALF
TB = T // P
BIG = 3.0e38

C_ONES, C_IDENT, C_ZERO, C_ONE = 0, 128, 256, 384
C_MISC = 512
C_COLS = 1024


def half(h):
    return slice(h * HALF, (h + 1) * HALF)


class Core:

    def __init__(self, nc, ctx):
        self.nc = nc
        self.bank = [ctx.enter_context(nc.psum_tensor(f"bank{i}", [P, HALF], F32)) for i in range(8)]
        sb = lambda name, shape, dt=F32: ctx.enter_context(nc.sbuf_tensor(name, shape, dt))
        self.x = sb("x_resid", [P, DC, T])
        self.xn = sb("x_norm", [P, DC, T])
        self.xh = sb("x_norm_h", [P, DC, T], F32R)
        self.xl = sb("x_norm_l", [P, DC, T], F32R)
        self.mean_w = sb("mean_w", [P, P])
        self.ident = sb("ident", [P, P])
        self.zero_r = sb("zero_r", [P, P], F32R)
        self.ones_r = sb("ones_r", [P, P], F32R)
        self.ident_b = sb("ident_b", [P, P], BF16)
        self.eps5 = sb("eps5", [P, 1])
        self.eps6 = sb("eps6", [P, 1])

    def pool_copy(self, pool, dst, src):
        one = self.ones_r[:, 0:1].bitcast(F32)
        for _ in range(len(src.shape) - 2):
            one = one.unsqueeze(1)
        return pool.tensor_tensor(dst, src, one.to_broadcast(list(src.shape)), ALU.mult)


def load_inputs(nc, core, x_in, consts):
    x_loaded, c_loaded, made = map(nc.alloc_semaphore, ("x_loaded", "c_loaded", "c_made"))
    with nc.Block() as block:

        @block.sync
        def _(sp):
            sp.dma_start(core.x[:, :, :], x_in).then_inc(x_loaded, 16)
            sp.wait_ge(x_loaded, 16)

        @block.scalar
        def _(act):
            act.dma_start(core.mean_w[:, :], consts[:, C_ONES:C_ONES + P]).then_inc(c_loaded, 16)
            act.dma_start(core.ident[:, :], consts[:, C_IDENT:C_IDENT + P]).then_inc(c_loaded, 16)
            act.wait_ge(c_loaded, 32)

        @block.gpsimd
        def _(pool):
            pool.memset(core.eps5[:, :], 1e-5).then_inc(made, 1)
            pool.memset(core.eps6[:, :], 1e-6).then_inc(made, 1)
            pool.wait_ge(c_loaded, 32)
            pool.tensor_scalar(core.zero_r[:, :], core.ident[:, :], 0.0, None, ALU.mult).then_inc(made, 1)
            pool.tensor_scalar(core.ones_r[:, :], core.ident[:, :], 0.0, 1.0, ALU.mult, ALU.add).then_inc(made, 1)
            pool.tensor_copy(core.ident_b[:, :], core.ident[:, :]).then_inc(made, 1)
            pool.wait_ge(made, 5)


def store_output(nc, core, out):
    stored = nc.alloc_semaphore("stored")
    with nc.Block() as block:

        @block.sync
        def _(sp):
            sp.dma_start(out, core.x[:, :, :]).then_inc(stored, 16)
            sp.wait_ge(stored, 16)


def norm(nc, core, name, src, center, eps, dst=None, gain=None, split=True, shift=None):
    dst = core.xn if dst is None else dst
    with ExitStack() as ctx:
        sem = lambda n: nc.alloc_semaphore(f"{name}_{n}")
        sb = lambda n, shape, dt=F32: ctx.enter_context(nc.sbuf_tensor(f"{name}_{n}", shape, dt))
        mean_ready, xc_ready, sq_ready, var_ready, std_ready = map(sem, ("mean", "xc", "sq", "var", "std"))
        rstd_ready, xn_ready, hi_ready, lo_ready = map(sem, ("rstd", "xn", "hi", "lo"))
        sq = sb("sq", [P, DC, T])
        std = sb("std", [P, T])
        rstd = sb("rstdv", [P, T])
        xc = sb("xc_b", [P, DC, T]) if center else src
        block = ctx.enter_context(nc.Block())

        @block.tensor
        def _(pe):
            if center:
                for h in range(NH):
                    for c in range(DC):
                        mm = pe.matmul(core.bank[h][:, :], core.mean_w[:, :], src[:, c, half(h)],
                                       start=c == 0, stop=c == DC - 1)
                    mm.then_inc(mean_ready, 1)
            for h in range(NH):
                pe.wait_ge(sq_ready, h + 1)
                for c in range(DC):
                    mm = pe.matmul(core.bank[2 + h][:, :], core.mean_w[:, :], sq[:, c, half(h)],
                                   start=c == 0, stop=c == DC - 1)
                mm.then_inc(var_ready, 1)

        @block.vector
        def _(dve):
            if center:
                for h in range(NH):
                    dve.wait_ge(mean_ready, h + 1)
                    for c in range(DC):
                        dve.tensor_tensor(xc[:, c, half(h)], src[:, c, half(h)], core.bank[h][:, :],
                                          ALU.subtract).then_inc(xc_ready, 1)
            for h in range(NH):
                dve.wait_ge(std_ready, h + 1)
                if center:
                    dve.wait_ge(xc_ready, DC * (h + 1))
                dve.reciprocal(rstd[:, half(h)], std[:, half(h)]).then_inc(rstd_ready, 1)
                dve.wait_ge(rstd_ready, h + 1)
                for c in range(DC):
                    dve.tensor_tensor(dst[:, c, half(h)], xc[:, c, half(h)], rstd[:, half(h)],
                                      ALU.mult).then_inc(xn_ready, 1)
                if gain is not None and shift is not None:
                    for c in range(DC):
                        n = DC * h + c + 1
                        dve.wait_ge(xn_ready, DC * (h + 1))
                        dve.tensor_scalar(dst[:, c, half(h)], dst[:, c, half(h)], gain[:, c:c + 1],
                                          shift[:, c:c + 1], ALU.mult, ALU.add).then_inc(lo_ready, 1)
                if split:
                    for c in range(DC):
                        n = DC * h + c + 1
                        dve.wait_ge(hi_ready, n)
                        if gain is None:
                            dve.tensor_tensor(core.xl[:, c, half(h)], dst[:, c, half(h)],
                                              core.xh[:, c, half(h)].bitcast(F32), ALU.subtract).then_inc(lo_ready, 1)
                        else:
                            dve.scalar_tensor_tensor(core.xl[:, c, half(h)], dst[:, c, half(h)], gain[:, c:c + 1],
                                                     core.xh[:, c, half(h)].bitcast(F32), ALU.mult,
                                                     ALU.subtract).then_inc(lo_ready, 1)

        @block.scalar
        def _(act):
            for h in range(NH):
                if center:
                    act.wait_ge(xc_ready, DC * (h + 1))
                act.activation(sq[:, :, half(h)], xc[:, :, half(h)], ACT.Square).then_inc(sq_ready, 1)
            for h in range(NH):
                act.wait_ge(var_ready, h + 1)
                act.activation(std[:, half(h)], core.bank[2 + h][:, :], ACT.Sqrt,
                               bias=eps[:, :]).then_inc(std_ready, 1)
            if split:
                for h in range(NH):
                    for c in range(DC):
                        act.wait_ge(xn_ready, DC * h + c + 1)
                        act.activation(core.xh[:, c, half(h)], dst[:, c, half(h)], ACT.Copy,
                                       scale=1.0 if gain is None else gain[:, c:c + 1]).then_inc(hi_ready, 1)


def resplit(nc, core, name, gain):
    hi_ready, lo_ready = nc.alloc_semaphore(f"{name}_hi"), nc.alloc_semaphore(f"{name}_lo")
    with nc.Block() as block:

        @block.scalar
        def _(act):
            for h in range(NH):
                for c in range(DC):
                    act.activation(core.xh[:, c, half(h)], core.xn[:, c, half(h)], ACT.Copy,
                                   scale=gain[:, c:c + 1]).then_inc(hi_ready, 1)

        @block.vector
        def _(dve):
            for h in range(NH):
                for c in range(DC):
                    dve.wait_ge(hi_ready, DC * h + c + 1)
                    dve.scalar_tensor_tensor(core.xl[:, c, half(h)], core.xn[:, c, half(h)], gain[:, c:c + 1],
                                             core.xh[:, c, half(h)].bitcast(F32), ALU.mult,
                                             ALU.subtract).then_inc(lo_ready, 1)


def ffn_cols(kc):
    g = 0
    u = kc * P
    d = u + DC * P
    b = d + D
    s = b + 2
    return g, u, d, b, s, s + P


def gated_ffn(nc, core, name, w_dram, n_chunks, routed, cw_parts=None, cw_f32=None, b2=None, z_h=None, z_l=None,
              extra=None):
    kc = 3 if z_h is not None else DC
    G, U, DN, B, S, WCOLS = ffn_cols(kc)
    with ExitStack() as ctx:
        sem = lambda n: nc.alloc_semaphore(f"{name}_{n}")
        sb = lambda n, shape, dt=F32: ctx.enter_context(nc.sbuf_tensor(f"{name}_{n}", shape, dt))
        w_in = [sem("w_in0"), sem("w_in1")]
        raw_free, w_split, w_free = sem("raw_free"), sem("w_split"), sem("w_free")
        g_ready, u_ready, cwb_ready, y_done = sem("g"), sem("u"), sem("cwb"), sem("y")
        silu_ready, hh_ready, t_ready, h_ready, hl_ready = sem("silu"), sem("hh"), sem("t"), sem("h"), sem("hl")
        x_added = sem("x_added")
        zeroed = sem("zeroed")
        raw = sb("raw", [P, 2, WCOLS])
        wh = sb("wh", [P, 2, B], F32R)
        wl = sb("wl", [P, 2, B], F32R)
        bias = sb("bias", [P, 2, 2])
        sel = sb("sel", [P, 2, P], BF16)
        sg = sb("sg", [P, 2, HALF])
        tf = sb("tf", [P, 2, HALF])
        hf = sb("hf", [P, 2, HALF])
        hh = sb("hhi", [P, 2, HALF], F32R)
        hl = sb("hlo", [P, 2, HALF], F32R)
        acc = [[core.bank[2 * m + h] for h in range(NH)] for m in range(DC)]
        last = 2 * n_chunks
        block = ctx.enter_context(nc.Block())

        def chunks(eng, body):
            with eng.Fori(0, n_chunks // 2) as i:
                for slot in range(2):
                    body(i * 2 + slot, i, slot)
            if n_chunks % 2:
                body(n_chunks - 1, n_chunks // 2, 0)

        @block.sync
        def _(sp):
            def load(c, i, slot):
                sp.wait_ge(raw_free, c + 1)
                sp.dma_start(raw[:, slot, :], w_dram[c]).then_inc(w_in[slot], 16)
            chunks(sp, load)

        @block.gpsimd
        def _(pool):
            pool.tensor_scalar(wh[:, 1, :], core.xn[:, 0, 0:B], 0.0, None, ALU.mult).then_inc(zeroed, 1)
            pool.tensor_scalar(wl[:, 1, :], core.xn[:, 0, 0:B], 0.0, None, ALU.mult).then_inc(zeroed, 1)
            pool.tensor_scalar(hh[:, 1, :], core.xn[:, 0, 0:HALF], 0.0, None, ALU.mult).then_inc(zeroed, 1)
            pool.tensor_scalar(hl[:, 1, :], core.xn[:, 0, 0:HALF], 0.0, None, ALU.mult).then_inc(zeroed, 1)
            pool.wait_ge(zeroed, 4)
            pool.sem_inc(raw_free, 2)

            def split(c, i, slot):
                pool.wait_ge(w_in[slot], i * 16 + 16)
                pool.wait_ge(w_free, c + 1)
                core.pool_copy(pool, wh[:, slot, :], raw[:, slot, 0:B]).then_inc(w_split, 1)
                pool.tensor_copy(bias[:, slot, :], raw[:, slot, B:B + 2]).then_inc(w_split, 1)
                pool.tensor_copy(sel[:, slot, :], raw[:, slot, S:S + P]).then_inc(w_split, 1)
                pool.wait_ge(w_split, c * 4 + 3)
                pool.tensor_tensor(wl[:, slot, :], raw[:, slot, 0:B], wh[:, slot, :].bitcast(F32),
                                   ALU.subtract).then_inc(w_split, 1)
                pool.wait_ge(w_split, c * 4 + 4)
                pool.sem_inc(raw_free, 1)
            chunks(pool, split)

        @block.tensor
        def _(pe):
            def gemm(out, cols, n_k, slot, h, third):
                n = 0
                for k in range(n_k):
                    c0 = cols + k * P
                    xh = core.xh[:, k, half(h)] if k < DC else third[0][:, half(h)]
                    xl = core.xl[:, k, half(h)] if k < DC else third[1][:, half(h)]
                    for w, x in ((wh, xh), (wl, xh), (wh, xl)):
                        mm = pe.matmul(out[:, :], w[:, slot, c0:c0 + P], x, start=n == 0, stop=n == 3 * n_k - 1)
                        n += 1
                return mm

            def down(slot, h, par):
                for m in range(DC):
                    c0 = DN + m * P
                    for w, x in ((wh, hh), (wl, hh), (wh, hl)):
                        mm = pe.matmul(acc[m][h][:, :], w[:, slot, c0:c0 + P], x[:, par, :], start=False, stop=False,
                                       skip_group_check=True)
                return mm

            def products(c, i, slot):
                pe.wait_ge(w_split, c * 4 + 4)
                for h in range(NH):
                    k = c * 2 + h
                    gate, up = core.bank[4 + 2 * h], core.bank[5 + 2 * h]
                    pe.wait_ge(h_ready, k + 1)
                    gemm(gate, G, kc, slot, h, (z_h, z_l)).then_inc(g_ready, 1)
                    gemm(up, U, DC, slot, h, None).then_inc(u_ready, 1)
                    if routed:
                        pe.wait_ge(silu_ready, k + 1)
                        pe.matmul(gate[:, :], sel[:, slot, :], cw_parts[:, half(h)], start=True,
                                  stop=True).then_inc(cwb_ready, 1)
                    pe.wait_ge(hl_ready, k + 1)
                    down(slot if h else 1 - slot, 1 - h, 1 - h).then_inc(y_done, 1)
                    if h == 0:
                        pe.wait_ge(y_done, k + 2)
                        pe.sem_inc(w_free, 1)

            pe.wait_ge(zeroed, 4)
            for m in range(DC):
                for h in range(NH):
                    if b2 is None:
                        pe.matmul(acc[m][h][:, :], core.zero_r[:, :], core.xh[:, 0, half(h)], start=True, stop=False,
                                  skip_group_check=True)
                    else:
                        pe.matmul(acc[m][h][:, :], b2[:, m * P:(m + 1) * P], cw_f32[:, half(h)], start=True,
                                  stop=False, skip_group_check=True)
            pe.sem_inc(y_done, 1)
            pe.sem_inc(w_free, 1)
            chunks(pe, products)
            pe.wait_ge(hl_ready, last + 1)
            down((n_chunks - 1) % 2, 1, 1).then_inc(y_done, 1)

        @block.scalar
        def _(act):
            def rows(c, i, slot):
                act.wait_ge(w_split, c * 4 + 4)
                for h in range(NH):
                    k = c * 2 + h
                    act.wait_ge(g_ready, k + 1)
                    act.wait_ge(t_ready, k + 1)
                    act.activation(sg[:, h, :], core.bank[4 + 2 * h][:, :], ACT.Silu,
                                   bias=bias[:, slot, 0:1]).then_inc(silu_ready, 1)
                    act.wait_ge(h_ready, k + 3)
                    act.wait_ge(y_done, k + 1)
                    act.activation(hh[:, h, :], hf[:, h, :], ACT.Copy).then_inc(hh_ready, 1)
            act.wait_ge(zeroed, 4)
            chunks(act, rows)

        @block.vector
        def _(dve):
            dve.sem_inc(h_ready, 2)
            dve.sem_inc(t_ready, 2)
            dve.wait_ge(zeroed, 4)
            dve.sem_inc(hl_ready, 1)

            def rows(c, i, slot):
                for h in range(NH):
                    k = c * 2 + h
                    gate, up = core.bank[4 + 2 * h], core.bank[5 + 2 * h]
                    dve.wait_ge(u_ready, k + 1)
                    dve.wait_ge(silu_ready, k + 1)
                    if routed:
                        dve.wait_ge(h_ready, k + 1)
                        dve.scalar_tensor_tensor(tf[:, h, :], up[:, :], bias[:, slot, 1:2], sg[:, h, :], ALU.add,
                                                 ALU.mult).then_inc(t_ready, 1)
                        dve.wait_ge(t_ready, k + 3)
                        dve.wait_ge(cwb_ready, k + 1)
                        dve.wait_ge(y_done, k + 1)
                        dve.tensor_tensor(hf[:, h, :], tf[:, h, :], gate[:, :], ALU.mult).then_inc(h_ready, 1)
                    else:
                        dve.wait_ge(y_done, k + 1)
                        dve.scalar_tensor_tensor(hf[:, h, :], up[:, :], bias[:, slot, 1:2], sg[:, h, :], ALU.add,
                                                 ALU.mult).then_inc(h_ready, 1)
                        dve.sem_inc(t_ready, 1)
                    dve.wait_ge(hh_ready, k + 1)
                    dve.tensor_tensor(hl[:, h, :], hf[:, h, :], hh[:, h, :].bitcast(F32),
                                      ALU.subtract).then_inc(hl_ready, 1)
            chunks(dve, rows)
            dve.wait_ge(y_done, last + 2)
            n = 0
            for m in range(DC):
                for h in range(NH):
                    dve.tensor_tensor(core.x[:, m, half(h)], core.x[:, m, half(h)], acc[m][h][:, :],
                                      ALU.add).then_inc(x_added, 1)
                    n += 1
                    if extra is not None:
                        dve.wait_ge(x_added, n)
                        dve.tensor_tensor(core.x[:, m, half(h)], core.x[:, m, half(h)], extra[:, m, half(h)],
                                          ALU.add).then_inc(x_added, 1)
                        n += 1


def top_mask(dve, link, mask, work, top, values, n, k, tiles):
    for t in range(tiles):
        link(dve.max(top[:, t, :], work[:, t, 0:max(n, 8)]))
    if k < 8:
        link(dve.memset(top[:, :, k:8], -BIG))
    for t in range(tiles):
        link(dve.match_replace(work[:, t, :], top[:, t, :], work[:, t, :], BIG))
    link(dve.tensor_scalar(mask, work[:, :, 0:n], 2.9e38, None, ALU.is_ge))


def router(nc, core, name, kind, E, top_k, gate_w, bias_row, cw_parts, cw_f32=None):
    with ExitStack() as ctx:
        sem = lambda n: nc.alloc_semaphore(f"{name}_{n}")
        sb = lambda n, shape, dt=F32: ctx.enter_context(nc.sbuf_tensor(f"{name}_{n}", shape, dt))
        w_loaded, b_loaded = sem("w"), sem("b")
        logits_ready, shifted, exp_ready, cw_ready, cwt_ready, chain, zeroed = map(
            sem, ("lg", "sh", "ex", "cw", "cwt", "chain", "z"))
        gw = sb("gw", [P, DC, E])
        br = sb("br", [P, E])
        lg = sb("lg_s", [P, TB, E])
        pr = sb("pr", [P, TB, E])
        work = sb("work", [P, TB, E + 8])
        mask = sb("mask", [P, TB, E])
        col = sb("col", [P, TB])
        top = sb("top", [P, TB, 8])
        rest = sb("rest", [E, T])
        back = sb("back", [E, T])
        N_G = 4
        gs = sb("gs", [P, 4, TB, N_G])
        gwork = sb("gwork", [P, TB, 16])
        gmask = sb("gmask", [P, TB, N_G])
        block = ctx.enter_context(nc.Block())
        wide = lambda c: c.unsqueeze(2).to_broadcast([P, TB, E])
        logits = core.bank[0][:, 0:TB * E].rearrange("p (t e) -> p t e", e=E)

        @block.sync
        def _(sp):
            sp.dma_start(gw[:, :, :], gate_w).then_inc(w_loaded, 16)
            if bias_row is not None:
                sp.dma_start(br[:, :], bias_row.partition_broadcast(P)).then_inc(b_loaded, 16)

        @block.gpsimd
        def _(pool):
            pool.memset(cw_parts[:, :], 0.0).then_inc(zeroed, 1)
            if cw_f32 is not None:
                pool.memset(cw_f32[:, :], 0.0).then_inc(zeroed, 1)
                pool.wait_ge(zeroed, 2)
                pool.memset(cw_f32[96:97, :], 1.0).then_inc(zeroed, 1)
            else:
                pool.wait_ge(zeroed, 1)
                pool.sem_inc(zeroed, 2)
            pool.memset(cw_parts[96:97, :], 1.0).then_inc(zeroed, 1)
            pool.wait_ge(zeroed, 4)

        @block.tensor
        def _(pe):
            pe.wait_ge(w_loaded, 16)
            for t in range(TB):
                for c in range(DC):
                    mm = pe.matmul(logits[:, t, :], core.xn[:, c, t * P:(t + 1) * P], gw[:, c, :],
                                   start=c == 0, stop=c == DC - 1)
            mm.then_inc(logits_ready, 1)
            pe.wait_ge(cw_ready, 1)
            for t in range(TB):
                mm = pe.transpose(core.bank[2 + t // 4][0:E, (t % 4) * P:(t % 4 + 1) * P], pr[:, t, :],
                                  core.ident[:, :])
            mm.then_inc(cwt_ready, 1)

        @block.scalar
        def _(act):
            if kind == "groups":
                act.wait_ge(logits_ready, 1)
                act.activation(pr[:, :, :], logits, ACT.Sigmoid).then_inc(exp_ready, 1)
            else:
                act.wait_ge(shifted, 1)
                act.activation(pr[:, :, :], lg[:, :, :], ACT.Exp).then_inc(exp_ready, 1)

        @block.vector
        def _(dve):
            n = [0]

            def link(ins):
                ins.then_inc(chain, 1)
                n[0] += 1
                dve.wait_ge(chain, n[0])

            if kind != "groups":
                dve.wait_ge(logits_ready, 1)
                link(dve.tensor_reduce(col[:, :], logits, AX.X, ALU.max))
                dve.tensor_tensor(lg[:, :, :], logits, wide(col[:, :]), ALU.subtract).then_inc(shifted, 1)
            dve.wait_ge(exp_ready, 1)
            if kind != "groups":
                link(dve.tensor_reduce(col[:, :], pr[:, :, :], AX.X, ALU.add))
                link(dve.reciprocal(col[:, :], col[:, :]))
                link(dve.tensor_tensor(pr[:, :, :], pr[:, :, :], wide(col[:, :]), ALU.mult))
            link(dve.memset(work[:, :, E:E + 8], -BIG))
            if bias_row is not None:
                dve.wait_ge(b_loaded, 16)
                link(dve.tensor_tensor(work[:, :, 0:E], pr[:, :, :], br[:, :].unsqueeze(1).to_broadcast([P, TB, E]),
                                       ALU.add))
            else:
                link(dve.tensor_copy(work[:, :, 0:E], pr[:, :, :]))
            if kind == "groups":
                v = work[:, :, 0:E].rearrange("p t (g j) -> p t g j", j=E // N_G)
                big, small, big2, small2 = (gs[:, j, :, :] for j in range(4))
                link(dve.tensor_tensor(big, v[:, :, :, 0], v[:, :, :, 1], ALU.max))
                link(dve.tensor_tensor(small, v[:, :, :, 0], v[:, :, :, 1], ALU.min))
                link(dve.tensor_tensor(big2, v[:, :, :, 2], v[:, :, :, 3], ALU.max))
                link(dve.tensor_tensor(small2, v[:, :, :, 2], v[:, :, :, 3], ALU.min))
                link(dve.tensor_tensor(small, small, small2, ALU.max))
                link(dve.tensor_tensor(small2, big, big2, ALU.min))
                link(dve.tensor_tensor(small, small, small2, ALU.max))
                link(dve.tensor_tensor(big, big, big2, ALU.max))
                link(dve.memset(gwork[:, :, :], -BIG))
                link(dve.tensor_tensor(gwork[:, :, 0:N_G], big, small, ALU.add))
                top_mask(dve, link, gmask[:, :, :], gwork, top, None, N_G, 2, TB)
                gm = gmask[:, :, :].unsqueeze(3).to_broadcast([P, TB, N_G, E // N_G])
                m4 = mask[:, :, :].rearrange("p t (g j) -> p t g j", j=E // N_G)
                link(dve.tensor_scalar(gmask[:, :, :], gmask[:, :, :], -1.0, 1.0e30, ALU.add, ALU.mult))
                link(dve.tensor_copy(m4, gm))
                link(dve.tensor_tensor(work[:, :, 0:E], work[:, :, 0:E], mask[:, :, :], ALU.add))
            top_mask(dve, link, mask[:, :, :], work, top, None, E, top_k, TB)
            if kind == "softmax_bias":
                dve.tensor_tensor(pr[:, :, :], pr[:, :, :], mask[:, :, :], ALU.mult).then_inc(cw_ready, 1)
            else:
                link(dve.tensor_tensor(pr[:, :, :], pr[:, :, :], mask[:, :, :], ALU.mult))
                link(dve.tensor_reduce(col[:, :], pr[:, :, :], AX.X, ALU.add))
                if kind == "groups":
                    link(dve.tensor_scalar(col[:, :], col[:, :], 1e-20, None, ALU.add))
                link(dve.reciprocal(col[:, :], col[:, :]))
                if kind == "groups":
                    link(dve.tensor_scalar(col[:, :], col[:, :], 2.5, None, ALU.mult))
                dve.tensor_tensor(pr[:, :, :], pr[:, :, :], wide(col[:, :]), ALU.mult).then_inc(cw_ready, 1)
            dve.wait_ge(cwt_ready, 1)
            dve.wait_ge(zeroed, 4)
            for h in range(NH):
                if cw_f32 is not None:
                    link(dve.tensor_copy(cw_f32[0:E, half(h)], core.bank[2 + h][0:E, :]))
                link(dve.tensor_copy(rest[:, half(h)], core.bank[2 + h][0:E, :]))
            for j in range(3):
                link(dve.tensor_copy(cw_parts[32 * j:32 * j + E, :], rest[:, :]))
                if j < 2:
                    link(dve.tensor_copy(back[:, :], cw_parts[32 * j:32 * j + E, :]))
                    link(dve.tensor_tensor(rest[:, :], rest[:, :], back[:, :], ALU.subtract))


def load_split(block_engines, raw, wh, wl, srcs, in_sems, hi_sem, lo_sem, lo_engine):
    sp, act, low = block_engines
    if sp is not None:
        for j, (cols, src) in enumerate(srcs):
            sp.dma_start(raw[:, :, cols], src).then_inc(in_sems[j], 16)
    if act is not None:
        for j, (cols, src) in enumerate(srcs):
            act.wait_ge(in_sems[j], 16)
            act.activation(wh[:, :, cols], raw[:, :, cols], ACT.Copy).then_inc(hi_sem, 1)
    if low is not None:
        for j, (cols, src) in enumerate(srcs):
            low.wait_ge(hi_sem, j + 1)
            low.tensor_tensor(wl[:, :, cols], raw[:, :, cols], wh[:, :, cols].bitcast(F32),
                              ALU.subtract).then_inc(lo_sem, 1)


def gemm3(pe, out, wh, wl, xh, xl, first=True, last=True):
    n, total = 0, 3 * len(wh)
    for k in range(len(wh)):
        for w, x in ((wh[k], xh[k]), (wl[k], xh[k]), (wh[k], xl[k])):
            mm = pe.matmul(out, w, x, start=first and n == 0, stop=last and n == total - 1)
            n += 1
    return mm


def decay_attention(nc, core, w_dram, cols_dram):
    with ExitStack() as outer:
        sbo = lambda n, shape, dt=F32: outer.enter_context(nc.sbuf_tensor(f"l3a_{n}", shape, dt))
        wh = sbo("wh", [P, DC, 4 * D], F32R)
        wl = sbo("wl", [P, DC, 4 * D], F32R)
        cols = sbo("cols", [P, 3, DC])
        lam = sbo("lam", [P, DC])
        y = sbo("y", [P, DC, T])
        gate = sbo("gate", [P, DC, T])
        V, Q, G, O = (j * D for j in range(4))
        with ExitStack() as ctx:
            sem = lambda n: nc.alloc_semaphore(f"l3a_{n}")
            raw = ctx.enter_context(nc.sbuf_tensor("l3a_raw", [P, DC, 4 * D], F32))
            states = ctx.enter_context(nc.sbuf_tensor("l3a_states", [P, DC, T], F32))
            w_in = [sem(f"w_in{j}") for j in range(4)]
            hi, lo, cols_in, lam_ready, v_ready, q_ready, g_ready = map(
                sem, ("hi", "lo", "cols", "lam", "v", "q", "g"))
            state_ready, y_ready, gate_ready = sem("st"), sem("yr"), sem("gr")
            srcs = [(slice(j * D, (j + 1) * D), w_dram[:, :, j * D:(j + 1) * D]) for j in range(4)]
            block = ctx.enter_context(nc.Block())

            @block.sync
            def _(sp):
                load_split((sp, None, None), raw, wh, wl, srcs, w_in, hi, lo, None)
                sp.dma_start(cols[:, :, :], cols_dram).then_inc(cols_in, 16)

            @block.scalar
            def _(act):
                load_split((None, act, None), raw, wh, wl, srcs, w_in, hi, lo, None)
                act.wait_ge(cols_in, 16)
                act.activation(lam[:, :], cols[:, 0, :], ACT.Sigmoid).then_inc(lam_ready, 1)
                for n in range(DC * NH):
                    m, h = n // NH, n % NH
                    act.wait_ge(g_ready, n + 1)
                    act.activation(gate[:, m, half(h)], core.bank[4 + n][:, :], ACT.Silu).then_inc(gate_ready, 1)

            @block.gpsimd
            def _(pool):
                load_split((None, None, pool), raw, wh, wl, srcs, w_in, hi, lo, None)

            @block.tensor
            def _(pe):
                def project(part, banks, ready):
                    for n in range(DC * NH):
                        m, h = n // NH, n % NH
                        w = slice(part + m * P, part + (m + 1) * P)
                        gemm3(pe, core.bank[banks(n)][:, :], [wh[:, k, w] for k in range(DC)],
                              [wl[:, k, w] for k in range(DC)], [core.xh[:, k, half(h)] for k in range(DC)],
                              [core.xl[:, k, half(h)] for k in range(DC)]).then_inc(ready, 1)
                pe.wait_ge(lo, 1)
                project(V, lambda n: n, v_ready)
                pe.wait_ge(lo, 2)
                project(Q, lambda n: 4 + n, q_ready)
                pe.wait_ge(lo, 3)
                pe.wait_ge(y_ready, DC * NH)
                project(G, lambda n: 4 + n, g_ready)

            @block.vector
            def _(dve):
                dve.wait_ge(lam_ready, 1)
                for n in range(DC * NH):
                    m, h = n // NH, n % NH
                    dve.wait_ge(v_ready, n + 1)
                    if h:
                        dve.wait_ge(state_ready, n)
                    dve.tensor_tensor_scan(states[:, m, half(h)], lam[:, m:m + 1].to_broadcast([P, HALF]),
                                           core.bank[n][:, :],
                                           states[:, m, HALF - 1:HALF] if h else 0.0,
                                           ALU.mult, ALU.add).then_inc(state_ready, 1)
                for n in range(DC * NH):
                    m, h = n // NH, n % NH
                    dve.wait_ge(q_ready, n + 1)
                    dve.wait_ge(state_ready, n + 1)
                    dve.tensor_tensor(y[:, m, half(h)], core.bank[4 + n][:, :], states[:, m, half(h)],
                                      ALU.mult).then_inc(y_ready, 1)

        norm(nc, core, "l3a_ln", y, True, core.eps5, dst=y, gain=cols[:, 1, :], shift=cols[:, 2, :], split=False)

        with ExitStack() as ctx:
            sem = lambda n: nc.alloc_semaphore(f"l3o_{n}")
            yg, yh, yl, out_ready, added = map(sem, ("yg", "yh", "yl", "out", "add"))
            block = ctx.enter_context(nc.Block())

            @block.vector
            def _(dve):
                for h in range(NH):
                    for c in range(DC):
                        dve.tensor_tensor(y[:, c, half(h)], y[:, c, half(h)], gate[:, c, half(h)],
                                          ALU.mult).then_inc(yg, 1)
                    for c in range(DC):
                        dve.wait_ge(yh, DC * h + c + 1)
                        dve.tensor_tensor(core.xl[:, c, half(h)], y[:, c, half(h)], core.xh[:, c, half(h)].bitcast(F32),
                                          ALU.subtract).then_inc(yl, 1)
                add_banks(dve, core, out_ready, added)

            @block.scalar
            def _(act):
                for h in range(NH):
                    for c in range(DC):
                        act.wait_ge(yg, DC * h + c + 1)
                        act.activation(core.xh[:, c, half(h)], y[:, c, half(h)], ACT.Copy).then_inc(yh, 1)

            @block.tensor
            def _(pe):
                for h in range(NH):
                    pe.wait_ge(yl, DC * (h + 1))
                    for m in range(DC):
                        w = slice(O + m * P, O + (m + 1) * P)
                        gemm3(pe, core.bank[DC * h + m][:, :], [wh[:, k, w] for k in range(DC)],
                              [wl[:, k, w] for k in range(DC)], [core.xh[:, k, half(h)] for k in range(DC)],
                              [core.xl[:, k, half(h)] for k in range(DC)]).then_inc(out_ready, 1)


def add_banks(dve, core, ready, added):
    for h in range(NH):
        for m in range(DC):
            dve.wait_ge(ready, DC * h + m + 1)
            dve.tensor_tensor(core.x[:, m, half(h)], core.x[:, m, half(h)], core.bank[DC * h + m][:, :],
                              ALU.add).then_inc(added, 1)


def project(nc, core, name, n_chunks, w_dram, tables, out, bias, v_w, v_bias, v_out, v_heads, v_dim):
    rope = tables is not None
    WC = DC * P
    NV = v_heads * v_dim
    with ExitStack() as ctx:
        sem = lambda n: nc.alloc_semaphore(f"{name}_{n}")
        sb = lambda n, shape, dt=F32: ctx.enter_context(nc.sbuf_tensor(f"{name}_{n}", shape, dt))
        w_in = [sem("w_in0"), sem("w_in1")]
        vw_in, tab_in, vb_in = sem("vw_in"), sem("tab_in"), sem("vb_in")
        raw_free, w_split, v_split, ps_ready, swapped, turned, sin_done, out_done = map(
            sem, ("raw_free", "w_split", "v_split", "ps", "sw", "cos", "sin", "out"))
        v_ready, v_read = sem("v_ready"), sem("v_read")
        raw = sb("raw", [P, 2, WC + 2])
        wh = sb("wh", [P, 2, WC], F32R)
        wl = sb("wl", [P, 2, WC], F32R)
        bcol = sb("bcol", [P, 2, 2])
        vraw = sb("vraw", [P, DC, NV])
        vh = sb("vh", [P, DC, NV], F32R)
        vl = sb("vl", [P, DC, NV], F32R)
        if rope:
            tab = sb("tab", [P, 2, T])
            swap = sb("swap", [P, 2, HALF])
            t1 = sb("t1", [P, 2, HALF])
            t2 = sb("t2", [P, 2, HALF])
        if v_bias is not None:
            vb = sb("vb", [P, NV])
        block = ctx.enter_context(nc.Block())
        N2 = n_chunks // 2

        def chunks(eng, body):
            with eng.Fori(0, N2) as i:
                for slot in range(2):
                    body(i * 2 + slot, i, slot)

        @block.sync
        def _(sp):
            sp.dma_start(vraw[:, :, :], v_w).then_inc(vw_in, 16)
            if v_bias is not None:
                sp.dma_start(vb[:, :], v_bias.partition_broadcast(P)).then_inc(vb_in, 16)
            if rope:
                sp.dma_start(tab[:, :, :], tables).then_inc(tab_in, 16)

            def load(c, i, slot):
                sp.wait_ge(raw_free, c + 1)
                sp.dma_start(raw[:, slot, :], w_dram[c]).then_inc(w_in[slot], 16)
            chunks(sp, load)

        @block.gpsimd
        def _(pool):
            pool.sem_inc(raw_free, 2)
            pool.sem_inc(sin_done, 2)

            pool.wait_ge(vw_in, 16)
            if rope:
                pool.wait_ge(tab_in, 16)

            def split(c, i, slot):
                pool.wait_ge(ps_ready, c * 2 + 2)
                pool.wait_ge(out_done, c * 2 + 2)
                pool.wait_ge(w_in[slot], i * 16 + 16)
                pool.wait_ge(vw_in, 16)
                core.pool_copy(pool, wh[:, slot, :], raw[:, slot, 0:WC]).then_inc(w_split, 1)
                pool.tensor_copy(bcol[:, slot, :], raw[:, slot, WC:WC + 2]).then_inc(w_split, 1)
                pool.wait_ge(w_split, c * 3 + 2)
                pool.tensor_tensor(wl[:, slot, :], raw[:, slot, 0:WC], wh[:, slot, :].bitcast(F32),
                                   ALU.subtract).then_inc(w_split, 1)
                pool.wait_ge(w_split, c * 3 + 3)
                pool.sem_inc(raw_free, 1)

            def times_sin(c, slot):
                for h in range(NH):
                    k = c * 2 + h
                    pool.wait_ge(out_done, k + 3)
                    pool.wait_ge(swapped, k * 2 + 2)
                    pool.tensor_tensor(t2[:, h, :], swap[:, h, :], tab[:, 1, half(h)],
                                       ALU.mult).then_inc(sin_done, 1)

            if rope:
                split(0, 0, 0)
                with pool.Fori(0, N2 - 1) as i:
                    split(i * 2 + 1, i, 1)
                    times_sin(i * 2, 0)
                    split(i * 2 + 2, i + 1, 0)
                    times_sin(i * 2 + 1, 1)
                split(n_chunks - 1, N2 - 1, 1)
                times_sin(n_chunks - 2, 0)
                times_sin(n_chunks - 1, 1)
            else:
                chunks(pool, split)

        @block.tensor
        def _(pe):
            pe.sem_inc(ps_ready, 4)

            def product(c, i, slot):
                pe.wait_ge(w_split, c * 3 + 3)
                for h in range(NH):
                    k = c * 2 + h
                    pe.wait_ge(out_done, k + 1)
                    gemm3(pe, core.bank[2 * slot + h][:, :], [wh[:, slot, j * P:(j + 1) * P] for j in range(DC)],
                          [wl[:, slot, j * P:(j + 1) * P] for j in range(DC)],
                          [core.xh[:, j, half(h)] for j in range(DC)],
                          [core.xl[:, j, half(h)] for j in range(DC)]).then_inc(ps_ready, 1)
            chunks(pe, product)
            pe.wait_ge(v_split, 2)
            for t in range(TB):
                tok = slice(t * P, (t + 1) * P)
                if t >= 4:
                    pe.wait_ge(v_read, t - 3)
                gemm3(pe, core.bank[4 + t % 4][:, 0:NV], [core.xh[:, j, tok] for j in range(DC)],
                      [core.xl[:, j, tok] for j in range(DC)], [vh[:, j, :] for j in range(DC)],
                      [vl[:, j, :] for j in range(DC)]).then_inc(v_ready, 1)

        @block.scalar
        def _(act):
            def evacuate(c, i, slot):
                act.wait_ge(w_split, c * 3 + 3)
                for h in range(NH):
                    k = c * 2 + h
                    act.wait_ge(ps_ready, k + 5)
                    bank = core.bank[2 * slot + h]
                    if rope:
                        act.wait_ge(sin_done, k + 1)
                        act.activation(swap[0:64, h, :], bank[64:128, :], ACT.Identity,
                                       bias=bcol[0:64, slot, 1:2]).then_inc(swapped, 1)
                        act.activation(swap[64:128, h, :], bank[0:64, :], ACT.Identity,
                                       bias=bcol[64:128, slot, 1:2]).then_inc(swapped, 1)
                    else:
                        act.activation(out[:, c, half(h)], bank[:, :], ACT.Identity,
                                       bias=bcol[:, slot, 0:1]).then_inc(out_done, 1)
            if not rope:
                act.sem_inc(out_done, 4)
            act.wait_ge(vw_in, 16)
            act.activation(vh[:, :, :], vraw[:, :, :], ACT.Copy).then_inc(v_split, 1)
            chunks(act, evacuate)

        @block.vector
        def _(dve):
            dve.wait_ge(v_split, 1)
            dve.tensor_tensor(vl[:, :, :], vraw[:, :, :], vh[:, :, :].bitcast(F32), ALU.subtract).then_inc(v_split, 1)
            if rope:
                dve.sem_inc(out_done, 4)
                dve.wait_ge(tab_in, 16)

                def turn(c, i, slot):
                    dve.wait_ge(w_split, c * 3 + 3)
                    for h in range(NH):
                        k = c * 2 + h
                        dve.wait_ge(ps_ready, k + 5)
                        dve.wait_ge(swapped, k * 2 + 2)
                        dve.wait_ge(out_done, k + 3)
                        dve.scalar_tensor_tensor(t1[:, h, :], core.bank[2 * slot + h][:, :], bcol[:, slot, 0:1],
                                                 tab[:, 0, half(h)], ALU.add, ALU.mult).then_inc(turned, 1)
                        dve.wait_ge(turned, k + 1)
                        dve.wait_ge(sin_done, k + 3)
                        dve.tensor_tensor(out[:, c, half(h)], t1[:, h, :], t2[:, h, :], ALU.add).then_inc(out_done, 1)
                chunks(dve, turn)
            if v_bias is not None:
                dve.wait_ge(vb_in, 16)
            for t in range(TB):
                dve.wait_ge(v_ready, t + 1)
                ps = core.bank[4 + t % 4][:, 0:NV].rearrange("p (h d) -> p h d", d=v_dim)
                if v_bias is None:
                    dve.tensor_copy(v_out[:, t, :, 0:v_dim], ps).then_inc(v_read, 1)
                else:
                    dve.tensor_tensor(v_out[:, t, :, 0:v_dim], ps, vb[:, :].rearrange("p (h d) -> p h d", d=v_dim),
                                      ALU.add).then_inc(v_read, 1)


def attend(nc, core, name, qk, n_q, v, on, scale, causal, groups, head_masks, masks_dram, sink=None):
    HEADS = 8
    per_o = 4 if causal else 2
    vw = 32 if causal else 64
    n_tiles = [(h, kb) for h in range(NH) for kb in range(TB) if not causal or kb * P < (h + 1) * HALF]
    a_segs = [(qb, s) for qb in range(TB) for s in range(NH) if not causal or s * HALF < (qb + 1) * P]
    NS, NA = len(n_tiles), len(a_segs)
    NP = 6
    RC = 0 if causal else 5

    plan = [("A", 0, i) for i in range(NA)]
    for j in range(HEADS):
        for i in range(NS):
            plan.append(("S", j, i))
            if j + 1 < HEADS and i < NA:
                plan.append(("A", j + 1, i))
            if i:
                plan.append(("V", j, i - 1))
            if causal:
                if j % per_o == 0 and j and i == 2:
                    plan.append(("DEN", j // per_o - 1, 0))
                if j % per_o == 0 and j and i == 6:
                    plan += [("R", j // per_o - 1, h) for h in range(NH)]
            else:
                if j and i == 3:
                    plan.append(("DEN", j - 1, 0))
                if j and j % 2 == 0 and i == 8:
                    plan += [("R", j // 2 - 1, h) for h in range(NH)]
        plan.append(("V", j, NS - 1))
    n_o = HEADS // per_o
    plan.append(("DEN", n_o - 1 if causal else HEADS - 1, 0))
    plan += [("R", n_o - 1, h) for h in range(NH)]
    ring_index, uses = {}, 0
    for ev in plan:
        if ev[0] in ("A", "DEN", "R"):
            ring_index[ev] = uses
            uses += 1
    NU = uses + uses % 2

    with ExitStack() as ctx:
        sem = lambda n: nc.alloc_semaphore(f"{name}_{n}")
        sb = lambda n, shape, dt=F32: ctx.enter_context(nc.sbuf_tensor(f"{name}_{n}", shape, dt))
        c_in = sem("c_in")
        k_parts, v_copied, q_parts, a_ready, a_read, m_steps, d_ready = map(
            sem, ("k_parts", "v_copied", "q_parts", "a_ready", "a_read", "m_steps", "d_ready"))
        s_ready, p_ready, av_done, on_done, r_steps, prep = map(
            sem, ("s_ready", "p_ready", "av_done", "on_done", "r_steps", "prep"))
        sum_done, den_done, sink_ready, ou_done = sem("sum_done"), sem("den_done"), sem("sink"), sem("ou_done")
        n_mask = head_masks.shape[1]
        MW = P if causal else 2 * P
        hm = sb("hm", [P, n_mask])
        mk_raw = sb("mk_raw", [P, 2, MW])
        mk = sb("mk", [P, 2, MW], BF16)
        kh = sb("kh", [P, T], F32R)
        kl = sb("kl", [P, T], F32R)
        vs = sb("vs", [P, TB, HEADS * vw if causal else 2 * vw])
        qh = sb("qh", [P, 2, T], F32R)
        ql = sb("ql", [P, 2, T], F32R)
        mseg = sb("mseg", [P, 2, TB, NH])
        mrow = sb("mrow", [P, 2, TB])
        negm = sb("negm", [P, 2, TB], F32R)
        diag = sb("diag", [P, 2, T], F32R)
        prob = sb("prob", [P, NP, HALF])
        den = sb("den", [P, TB, per_o])
        rx = sb("rx", [P, TB, per_o, vw])
        ou = sb("ou", [P, T])
        if causal:
            pick = sb("pick", [P, per_o])
        else:
            psum_acc = sb("psum_acc", [P, 2, T])
            sk = sb("sk", [P, groups * HEADS])
            sk8 = sb("sk8", [P, groups * HEADS])
            esink = sb("esink", [P, 2, TB])
            one_col = sb("one_col", [P, 1])
        block = ctx.enter_context(nc.Block())

        def tile_cols(i):
            h, kb = n_tiles[i]
            q0 = max(kb * P, h * HALF) if causal else h * HALF
            return h, kb, q0, q0 - h * HALF, (h + 1) * HALF - q0

        def o_bank(o, h):
            return core.bank[4 + 2 * (o % 2) + h]

        @block.sync
        def _(sp):
            sp.dma_start(hm[:, :], head_masks).then_inc(c_in, 16)
            sp.dma_start(mk_raw[:, :, :], masks_dram[:, :, 0:MW]).then_inc(c_in, 16)
            if causal:
                sp.dma_start(pick[:, :], masks_dram[:, 0, MW:MW + per_o]).then_inc(c_in, 16)
            else:
                sp.dma_start(sk[:, :], sink.partition_broadcast(P)).then_inc(c_in, 16)
            sp.wait_ge(c_in, 48)

        @block.gpsimd
        def _(pool):
            pool.wait_ge(c_in, 48)
            pool.tensor_scalar(mk[:, :, :], mk_raw[:, :, :], 1.0, None, ALU.mult).then_inc(prep, 1)
            pool.memset(mseg[:, :, :, :], -BIG).then_inc(prep, 1)
            if not causal:
                pool.tensor_scalar(sk8[:, :], sk[:, :], 1.0 / scale, None, ALU.mult).then_inc(prep, 1)
                pool.memset(one_col[:, :], 1.0).then_inc(prep, 1)
                pool.sem_inc(sum_done, NP)
                with pool.Fori(0, groups) as g:
                    for j in range(HEADS):
                        for i in range(NS):
                            h, kb = n_tiles[i]
                            v_ = g * (HEADS * NS) + (j * NS + i)
                            if kb == 0:
                                continue
                            acc = psum_acc[:, j % 2, half(h)]
                            pt = lambda k: prob[:, (j * NS + k) % NP, :]
                            if kb == 1:
                                if h == 0:
                                    pool.wait_ge(den_done, g * HEADS + (j + 1))
                                pool.wait_ge(p_ready, v_ + 3)
                                pool.tensor_tensor(acc, pt(i - 1), pt(i), ALU.add).then_inc(sum_done, 2)
                            else:
                                pool.wait_ge(sum_done, v_ + NP)
                                pool.wait_ge(p_ready, v_ + 3)
                                pool.tensor_tensor(acc, acc, pt(i), ALU.add).then_inc(sum_done, 1)
            else:
                pool.sem_inc(prep, 2)

        @block.tensor
        def _(pe):
            pe.wait_ge(prep, 4)
            pe.wait_ge(c_in, 48)
            pe.sem_inc(s_ready, 2 * NS)
            pe.sem_inc(av_done, NP)
            pe.sem_inc(den_done, 2)
            with pe.Fori(0, groups) as g:
                for ev in plan:
                    kind, j, i = ev
                    if kind in ("A", "DEN", "R"):
                        u = ring_index[ev]
                        ring = core.bank[u % 2]
                        u_ = g * NU + u
                    if kind == "A":
                        qb, s = a_segs[i]
                        if i == 0:
                            pe.wait_ge(q_parts, g * (2 * HEADS) + (2 * j + 2))
                            if j == 0:
                                pe.wait_ge(k_parts, g * 2 + 2)
                        k1 = min((qb + 1) * P, (s + 1) * HALF) if causal else (s + 1) * HALF
                        w = k1 - s * HALF
                        m0 = qb * P if causal else (qb - 1) * P
                        lo, hi = max(m0, s * HALF), min((qb + 1) * P, k1)
                        pe.wait_ge(a_read, u_ + 1)
                        mm = pe.matmul(ring[:, 0:w], qh[:, j % 2, qb * P:(qb + 1) * P], kh[:, s * HALF:k1],
                                       start=True, stop=lo >= hi)
                        if lo < hi:
                            mm = pe.matmul(ring[:, lo - s * HALF:hi - s * HALF], core.ident_b[:, :],
                                           mk[:, 1, lo - m0:hi - m0], start=False, stop=True)
                        mm.then_inc(a_ready, 1)
                    elif kind == "S":
                        h, kb, q0, c0, w = tile_cols(i)
                        v_ = g * (HEADS * NS) + (j * NS + i)
                        bank = core.bank[2 + (j * NS + i) % 2]
                        keys = slice(kb * P, (kb + 1) * P)
                        if i == 0:
                            pe.wait_ge(d_ready, g * HEADS + (j + 1))
                        pe.wait_ge(p_ready, v_ + 1)
                        out = bank[:, c0:c0 + w]
                        pe.matmul(out, kh[:, keys], qh[:, j % 2, q0:q0 + w], start=True, stop=False)
                        pe.matmul(out, kl[:, keys], qh[:, j % 2, q0:q0 + w], start=False, stop=False)
                        pe.matmul(out, kh[:, keys], ql[:, j % 2, q0:q0 + w], start=False, stop=False)
                        lo, hi = max(kb * P, q0), min(kb * P + MW, q0 + w)
                        mm = pe.matmul(out, core.ones_r[:, :], diag[:, j % 2, q0:q0 + w], start=False, stop=lo >= hi)
                        if lo < hi:
                            mm = pe.matmul(bank[:, lo - h * HALF:hi - h * HALF], core.ident_b[:, :],
                                           mk[:, 0, lo - kb * P:hi - kb * P], start=False, stop=True)
                        mm.then_inc(s_ready, 1)
                    elif kind == "V":
                        h, kb, q0, c0, w = tile_cols(i)
                        n = j * NS + i
                        v_ = g * (HEADS * NS) + n
                        o, a = j // per_o, j % per_o
                        if j == 0 and i == 0:
                            pe.wait_ge(v_copied, g * 1 + 1)
                        if a == 0 and i == 0:
                            pe.wait_ge(ou_done, g * (2 * n_o) + (2 * o + 2))
                        pe.wait_ge(p_ready, v_ + 3)
                        vcol = (j if causal else j % 2) * vw
                        pe.matmul(o_bank(o, h)[vw * a:vw * a + vw, c0:c0 + w], vs[:, kb, vcol:vcol + vw],
                                  prob[:, n % NP, 0:w], start=kb == 0,
                                  stop=kb == (4 * h + 3 if causal else TB - 1), skip_group_check=True,
                                  tile_position=(0, vw * a)).then_inc(av_done, 1)
                    elif kind == "DEN":
                        pe.wait_ge(a_read, u_ + 1)
                        if causal:
                            pe.wait_ge(ou_done, g * (2 * n_o) + (2 * j + 6))
                            for qb in range(TB):
                                mm = pe.matmul(ring[:, qb * per_o:(qb + 1) * per_o], ou[:, qb * P:(qb + 1) * P],
                                               pick[:, :], start=True, stop=True)
                        else:
                            pe.wait_ge(sum_done, g * (HEADS * NS) + ((j + 1) * NS + NP))
                            for qb in range(TB):
                                mm = pe.matmul(ring[:, qb:qb + 1], psum_acc[:, j % 2, qb * P:(qb + 1) * P],
                                               one_col[:, :], start=True, stop=True)
                        mm.then_inc(a_ready, 1)
                        if not causal:
                            pe.wait_ge(a_ready, u_ + 1)
                            pe.sem_inc(den_done, 1)
                    elif kind == "R":
                        if i == 0:
                            steps = 2 if causal else 5
                            pe.wait_ge(r_steps, g * (steps * n_o) + (steps * (j + 1) + RC))
                        pe.wait_ge(a_read, u_ + 1)
                        for b in range(4):
                            qb = 4 * i + b
                            mm = pe.transpose(ring[:, b * P:(b + 1) * P],
                                              rx[:, qb, :, :].rearrange("p a d -> p (a d)"), core.ident[:, :])
                        mm.then_inc(a_ready, 1)
                if NU != uses:
                    pe.sem_inc(a_ready, 1)

        @block.scalar
        def _(act):
            act.sem_inc(p_ready, 2)
            act.sem_inc(ou_done, 4)
            if not causal:
                act.sem_inc(sink_ready, 2)
                act.wait_ge(c_in, 48)
            with act.Fori(0, groups) as g:
                act.wait_ge(av_done, g * (HEADS * NS) + NP)
                for t in range(TB):
                    src = (v[:, t, bass.ts(g, HEADS), :] if causal else v[:, t, bass.ts(g, 2), :])
                    ins = act.activation(vs[:, t, :].rearrange("p (a d) -> p a d", d=vw), src, ACT.Copy)
                ins.then_inc(v_copied, 1)
                for j in range(HEADS):
                    for i in range(NS):
                        h, kb, q0, c0, w = tile_cols(i)
                        n = j * NS + i
                        v_ = g * (HEADS * NS) + n
                        if not causal and i == 0:
                            act.wait_ge(m_steps, g * (2 * HEADS) + (2 * j + 2))
                            act.wait_ge(r_steps, g * (5 * n_o) + (5 * (j // 2) + 2 * (j % 2) + 1))
                            act.activation(esink[:, j % 2, :], negm[:, j % 2, :].bitcast(F32), ACT.Exp,
                                           bias=sk[:, bass.ds(g * HEADS + j, 1)], scale=scale).then_inc(sink_ready, 1)
                        act.wait_ge(av_done, v_ + 1)
                        if not causal:
                            act.wait_ge(sum_done, v_ + 1)
                        act.wait_ge(s_ready, v_ + (2 * NS + 1))
                        act.activation(prob[:, n % NP, 0:w], core.bank[2 + n % 2][:, c0:c0 + w], ACT.Exp,
                                       scale=scale).then_inc(p_ready, 1)
                    if j % per_o == per_o - 1:
                        o = j // per_o
                        act.wait_ge(av_done, g * (HEADS * NS) + ((j + 1) * NS + NP))
                        act.wait_ge(on_done, g * (2 * n_o) + (2 * o + 1))
                        for h in range(NH):
                            act.activation(ou[:, half(h)], o_bank(o, h)[:, :], ACT.Copy).then_inc(ou_done, 1)

        @block.vector
        def _(dve):
            dve.wait_ge(prep, 4)
            dve.wait_ge(c_in, 48)
            dve.sem_inc(a_read, 2)
            dve.sem_inc(on_done, 1)
            if not causal:
                dve.sem_inc(r_steps, RC)
            with dve.Fori(0, groups) as g:
                dve.wait_ge(s_ready, g * (HEADS * NS) + 2 * NS)
                key = qk[:, bass.ds(g + n_q, 1), :].rearrange("p a t -> p (a t)")
                dve.tensor_copy(kh[:, :], key).then_inc(k_parts, 1)
                dve.wait_ge(k_parts, g * 2 + 1)
                dve.tensor_tensor(kl[:, :], key, kh[:, :].bitcast(F32), ALU.subtract).then_inc(k_parts, 1)

                def split_q(j):
                    c = g if causal else g * 4 + j // 2
                    src = qk[:, bass.ds(c, 1), :].rearrange("p a t -> p (a t)")
                    row = hm[:, j:j + 1] if causal else hm[:, j % 2:j % 2 + 1]
                    dve.wait_ge(s_ready, g * (HEADS * NS) + (j + 1) * NS)
                    dve.tensor_scalar(qh[:, j % 2, :], src, row, None, ALU.mult).then_inc(q_parts, 1)
                    dve.wait_ge(q_parts, g * (2 * HEADS) + (2 * j + 1))
                    dve.scalar_tensor_tensor(ql[:, j % 2, :], src, row, qh[:, j % 2, :].bitcast(F32), ALU.mult,
                                             ALU.subtract).then_inc(q_parts, 1)

                def take_max(j, last_use):
                    r = j % 2
                    dve.wait_ge(a_read, g * NU + (last_use + 3))
                    dve.tensor_reduce(mrow[:, r, :], mseg[:, r, :, :], AX.X, ALU.max).then_inc(m_steps, 1)
                    dve.wait_ge(m_steps, g * (2 * HEADS) + (2 * j + 1))
                    if causal:
                        dve.tensor_scalar(negm[:, r, :], mrow[:, r, :], -1.0, None, ALU.mult).then_inc(m_steps, 1)
                    else:
                        dve.wait_ge(sink_ready, g * HEADS + (j + 1))
                        dve.tensor_scalar(negm[:, r, :], mrow[:, r, :], sk8[:, bass.ds(g * HEADS + j, 1)], -1.0,
                                          ALU.max, ALU.mult).then_inc(m_steps, 1)
                    dve.wait_ge(m_steps, g * (2 * HEADS) + (2 * j + 2))
                    dve.tensor_tensor(diag[:, r, :].rearrange("p (b k) -> p b k", k=P),
                                      core.ident[:, :].unsqueeze(1).to_broadcast([P, TB, P]),
                                      negm[:, r, :].bitcast(F32).unsqueeze(2).to_broadcast([P, TB, P]),
                                      ALU.mult).then_inc(d_ready, 1)

                split_q(0)
                for ev in plan:
                    kind, j, i = ev
                    if kind not in ("A", "DEN", "R"):
                        continue
                    u = ring_index[ev]
                    ring = core.bank[u % 2]
                    u_ = g * NU + u
                    if kind == "A":
                        qb, s = a_segs[i]
                        if i == 0 and j:
                            split_q(j)
                        k1 = min((qb + 1) * P, (s + 1) * HALF) if causal else (s + 1) * HALF
                        dve.wait_ge(a_ready, u_ + 1)
                        dve.tensor_reduce(mseg[:, j % 2, qb, s:s + 1], ring[:, 0:k1 - s * HALF], AX.X,
                                          ALU.max).then_inc(a_read, 1)
                        if i == NA - 1:
                            take_max(j, u)
                    elif kind == "DEN":
                        dve.wait_ge(a_ready, u_ + 1)
                        if causal:
                            base = g * (2 * n_o) + 2 * j
                            dve.reciprocal(den[:, :, :], ring[:, 0:TB * per_o].rearrange("p (b a) -> p b a", a=per_o)
                                           ).then_inc(r_steps, 1)
                            dve.wait_ge(r_steps, base + 1)
                            dve.tensor_copy(rx[:, :, :, :], den[:, :, :].unsqueeze(3).to_broadcast([P, TB, per_o, vw])
                                            ).then_inc(r_steps, 1)
                            dve.sem_inc(a_read, 1)
                        else:
                            base = g * (5 * n_o) + (5 * (j // 2) + 2 * (j % 2) + RC)
                            dve.wait_ge(sink_ready, g * HEADS + (j + 3))
                            dve.tensor_tensor(den[:, :, j % 2], ring[:, 0:TB], esink[:, j % 2, :],
                                              ALU.add).then_inc(r_steps, 1)
                            dve.wait_ge(r_steps, base + 1)
                            dve.sem_inc(a_read, 1)
                            dve.reciprocal(den[:, :, j % 2], den[:, :, j % 2]).then_inc(r_steps, 1)
                            if j % 2:
                                dve.wait_ge(r_steps, base + 2)
                                dve.tensor_copy(rx[:, :, :, :],
                                                den[:, :, :].unsqueeze(3).to_broadcast([P, TB, per_o, vw])
                                                ).then_inc(r_steps, 1)
                    elif kind == "R":
                        dve.wait_ge(a_ready, u_ + 1)
                        o = j
                        c = g * n_o + o
                        dst = on[:, bass.ds(c, 1), half(i)].rearrange("p a t -> p (a t)")
                        dve.wait_ge(ou_done, g * (2 * n_o) + (2 * o + i + 5))
                        dve.tensor_tensor(dst, ou[:, half(i)], ring[:, :], ALU.mult).then_inc(on_done, 1)
                        dve.wait_ge(on_done, g * (2 * n_o) + (2 * o + i + 2))
                        dve.sem_inc(a_read, 1)
                if NU != uses:
                    dve.sem_inc(a_read, 1)


def out_product(nc, core, name, on, n_chunks, w_dram, bias, dst, add_x):
    with ExitStack() as ctx:
        sem = lambda n: nc.alloc_semaphore(f"{name}_{n}")
        sb = lambda n, shape, dt=F32: ctx.enter_context(nc.sbuf_tensor(f"{name}_{n}", shape, dt))
        w_in = [sem("w_in0"), sem("w_in1")]
        raw_free, w_split, oh_ready, ol_ready, y_done, added, b_in = map(
            sem, ("raw_free", "w_split", "oh", "ol", "y", "added", "b_in"))
        raw = sb("raw", [P, 2, D])
        wh = sb("wh", [P, 2, D], F32R)
        wl = sb("wl", [P, 2, D], F32R)
        oh = sb("ohi", [P, 2, T], F32R)
        ol = sb("olo", [P, 2, T], F32R)
        bc = sb("bc", [P, DC])
        block = ctx.enter_context(nc.Block())

        def chunks(eng, body):
            with eng.Fori(0, n_chunks // 2) as i:
                for slot in range(2):
                    body(i * 2 + slot, i, slot)

        @block.sync
        def _(sp):
            sp.dma_start(bc[:, :], bias).then_inc(b_in, 16)

            def load(c, i, slot):
                sp.wait_ge(raw_free, c + 1)
                sp.dma_start(raw[:, slot, :], w_dram[c]).then_inc(w_in[slot], 16)
            chunks(sp, load)

        @block.gpsimd
        def _(pool):
            pool.sem_inc(raw_free, 2)

            def split(c, i, slot):
                pool.wait_ge(y_done, c + 1)
                pool.wait_ge(w_in[slot], i * 16 + 16)
                pool.wait_ge(b_in, 16)
                core.pool_copy(pool, wh[:, slot, :], raw[:, slot, :]).then_inc(w_split, 1)
                pool.wait_ge(w_split, c * 2 + 1)
                pool.tensor_tensor(wl[:, slot, :], raw[:, slot, :], wh[:, slot, :].bitcast(F32),
                                   ALU.subtract).then_inc(w_split, 1)
                pool.wait_ge(w_split, c * 2 + 2)
                pool.sem_inc(raw_free, 1)
            chunks(pool, split)

        @block.scalar
        def _(act):
            def high(c, i, slot):
                act.wait_ge(y_done, c + 1)
                src = on[:, bass.ds(c, 1), :].rearrange("p a t -> p (a t)")
                act.activation(oh[:, slot, :], src, ACT.Copy).then_inc(oh_ready, 1)
            chunks(act, high)

        @block.vector
        def _(dve):
            def low(c, i, slot):
                dve.wait_ge(oh_ready, c + 1)
                src = on[:, bass.ds(c, 1), :].rearrange("p a t -> p (a t)")
                dve.tensor_tensor(ol[:, slot, :], src, oh[:, slot, :].bitcast(F32), ALU.subtract).then_inc(ol_ready, 1)
            chunks(dve, low)
            dve.wait_ge(b_in, 16)
            dve.wait_ge(y_done, n_chunks + 2)
            for m in range(DC):
                for h in range(NH):
                    ps = core.bank[DC * h + m][:, :]
                    if add_x:
                        dve.scalar_tensor_tensor(dst[:, m, half(h)], ps, bc[:, m:m + 1], dst[:, m, half(h)], ALU.add,
                                                 ALU.add).then_inc(added, 1)
                    else:
                        dve.tensor_scalar(dst[:, m, half(h)], ps, bc[:, m:m + 1], None, ALU.add).then_inc(added, 1)

        @block.tensor
        def _(pe):
            for m in range(DC):
                for h in range(NH):
                    pe.matmul(core.bank[DC * h + m][:, :], core.zero_r[:, :], core.xh[:, 0, half(h)], start=True,
                              stop=False, skip_group_check=True)
            pe.sem_inc(y_done, 2)

            def product(c, i, slot):
                pe.wait_ge(w_split, c * 2 + 2)
                pe.wait_ge(ol_ready, c + 1)
                for m in range(DC):
                    for h in range(NH):
                        for w, x in ((wh, oh), (wl, oh), (wh, ol)):
                            mm = pe.matmul(core.bank[DC * h + m][:, :], w[:, slot, m * P:(m + 1) * P],
                                           x[:, slot, half(h)], start=False, stop=False, skip_group_check=True)
                mm.then_inc(y_done, 1)
            chunks(pe, product)


def low_state(nc, core, w_dram, t_h, t_l):
    with ExitStack() as ctx:
        sem = lambda n: nc.alloc_semaphore("ls_" + n)
        sb = lambda n, shape, dt=F32: ctx.enter_context(nc.sbuf_tensor("ls_" + n, shape, dt))
        w_in, split, ready, hi, lo = map(sem, ("w", "sp", "rd", "hi", "lo"))
        w = sb("wt", [P, DC, P])
        wh = sb("wth", [P, DC, P], F32R)
        wl = sb("wtl", [P, DC, P], F32R)
        block = ctx.enter_context(nc.Block())

        @block.sync
        def _(sp):
            sp.dma_start(w[:, :, :], w_dram).then_inc(w_in, 16)

        @block.tensor
        def _(pe):
            pe.wait_ge(split, 2)
            for h in range(NH):
                gemm3(pe, core.bank[h][:, :], [wh[:, k, :] for k in range(DC)], [wl[:, k, :] for k in range(DC)],
                      [core.xh[:, k, half(h)] for k in range(DC)],
                      [core.xl[:, k, half(h)] for k in range(DC)]).then_inc(ready, 1)

        @block.scalar
        def _(act):
            for h in range(NH):
                act.wait_ge(ready, h + 1)
                act.activation(t_h[:, half(h)], core.bank[h][:, :], ACT.Copy).then_inc(hi, 1)

        @block.vector
        def _(dve):
            dve.wait_ge(w_in, 16)
            dve.tensor_copy(wh[:, :, :], w[:, :, :]).then_inc(split, 1)
            dve.wait_ge(split, 1)
            dve.tensor_tensor(wl[:, :, :], w[:, :, :], wh[:, :, :].bitcast(F32), ALU.subtract).then_inc(split, 1)
            for h in range(NH):
                dve.wait_ge(hi, h + 1)
                dve.tensor_tensor(t_l[:, half(h)], core.bank[h][:, :], t_h[:, half(h)].bitcast(F32),
                                  ALU.subtract).then_inc(lo, 1)


def state_attention(nc, core, a):
    NQ = 4
    DK = 128
    uses = [(("v", t), t % 4) for t in range(TB)] + [(("g", t), t % 4) for t in range(TB)]
    for p in range(2):
        uses += [(("s", p, h), h) for h in range(NH)]
        uses += [(("qk", p, a_, w, h), 4 + 2 * w + h) for a_ in range(2) for w in range(2) for h in range(NH)]
        uses += [(("te", p, h), h) for h in range(NH)]
        uses += [(("tk", p, a_, h), (2, 4)[a_] + h) for a_ in range(2) for h in range(NH)]
        uses += [(("at", p, a_, h), (0, 6)[a_] + h) for a_ in range(2) for h in range(NH)]
        uses += [(("s1", p, h), 2 + h) for h in range(NH)]
        uses += [(("s2", p, h), 4 + h) for h in range(NH)]
        uses += [(("ok", p, h), h) for h in range(NH)]
        uses += [(("tok", p, h), 2 + h) for h in range(NH)]
        uses += [(("tq", p, h), 6 + h) for h in range(NH)]
        uses += [(("w2", p, i), (0, 1, 4, 5)[i]) for i in range(4)]
        uses += [(("o", p, i), (2, 3, 6, 7)[i]) for i in range(4)]
        uses += [(("to", p, a_, h), (0, 4)[a_] + h) for a_ in range(2) for h in range(NH)]
        uses += [(("wo", p, m, h), (2, 6)[m] + h) for m in range(DC) for h in range(NH)]
    bank_of = dict(uses)
    count = [0] * 8
    nth = {}
    for key, b in uses:
        nth[key] = count[b]
        count[b] += 1

    with ExitStack() as ctx:
        sem = lambda n: nc.alloc_semaphore("l2a_" + n)
        sb = lambda n, shape, dt=F32: ctx.enter_context(nc.sbuf_tensor("l2a_" + n, shape, dt))
        t_h = sb("t_h", [P, T], F32R)
        t_l = sb("t_l", [P, T], F32R)
        low_state(nc, core, a["l2a_ws1"], t_h, t_l)
        full = [sem(f"bank_full{b}") for b in range(8)]
        free = [sem(f"bank_free{b}") for b in range(8)]
        c_in, vw_in, gw_in, sw_in, wo_in = map(sem, ("c_in", "vw_in", "gw_in", "sw_in", "wo_in"))
        qkw_in = [sem("qkw_in0"), sem("qkw_in1")]
        vraw_free, qkraw_free, swraw_free, woraw_free = map(sem, ("vraw_free", "qkraw_free", "swraw_free", "woraw_free"))
        vg_hi, vg_lo, sw_split, qkw_split, wo_split = map(sem, ("vg_hi", "vg_lo", "sw_split", "qkw_split", "wo_split"))
        v_ready, g_silu, g_ready, clipped, es_ready, summed, enz_ready = map(
            sem, ("v_ready", "g_silu", "g_ready", "clipped", "es", "summed", "enz"))
        swapped, times_cos, times_sin, qk_ready = map(sem, ("swapped", "cos", "sin", "qk"))
        tm_ready, at_ready, s1_ready, s2_ready, oke_ready = map(sem, ("tm", "at", "s1", "s2", "oke"))
        shifted, exped, soft, pb_ready, w2_ready = map(sem, ("shifted", "exped", "soft", "pb", "w2"))
        squared, sumsq, rooted, scaled, gated = map(sem, ("squared", "sumsq", "rooted", "scaled", "gated"))
        oth, otl, pair_done, rooted_inv, zeroed = map(sem, ("oth", "otl", "pair_done", "rooted_inv", "zeroed"))

        tab = sb("tab", [P, 2, T])
        causal = sb("causal", [P, P])
        gnw = sb("gnw", [P, DK])
        vraw = sb("vraw", [P, DC, 512])
        vgh = sb("vgh", [P, 2, DC, 512], F32R)
        vgl = sb("vgl", [P, 2, DC, 512], F32R)
        swraw = sb("swraw", [P, 2, P + 1])
        swh = sb("swh", [P, 2, P], F32R)
        swl = sb("swl", [P, 2, P], F32R)
        sbias = sb("sbias", [P, 2])
        qkraw = sb("qkraw", [P, 2, DC * P])
        qkwh = sb("qkwh", [P, 2, DC * P], F32R)
        qkwl = sb("qkwl", [P, 2, DC * P], F32R)
        woraw = sb("woraw", [P, 2, D])
        woh = sb("woh", [P, 2, D], F32R)
        wol = sb("wol", [P, 2, D], F32R)
        vq = sb("vq", [P, TB, 4, DK])
        gq = sb("gq", [P, TB, 4, DK])
        qt = sb("qt", [P, 2, 2, T])
        ktm = sb("ktm", [P, 2, TB, P])
        es = sb("es_", [P, T])
        estm = sb("estm", [P, TB, P])
        enz = sb("enz_", [P, T])
        atw = sb("atw", [P, TB, 2, P])
        s1 = sb("s1_", [P, TB, 2, 64])
        s2 = sb("s2_", [P, TB, DK])
        pb = sb("pb_", [P, TB, 2, P])
        og = sb("og", [P, TB, 2, DK])
        cs = og[:, 0:4, :, :].rearrange("p t a d -> p (t a d)")
        sc = og[:, 4:8, :, :].rearrange("p t a d -> p (t a d)")
        oke = core.xn[:, 0, :]
        qv = core.xn[:, 1, :]
        swap = core.xn[:, 0, :].rearrange("p (h t) -> p h t", h=NH)
        t2 = core.xn[:, 1, :].rearrange("p (h t) -> p h t", h=NH)
        ogh = sb("ogh", [P, 2, T], F32R)
        ogl = sb("ogl", [P, 2, T], F32R)
        mx = sb("mx", [P, TB, 2])
        rs = sb("rs", [P, TB, 2])
        ss = sb("ss", [P, TB, 2])
        block = ctx.enter_context(nc.Block())

        def at(g, key):
            return g * count[bank_of[key]] + (nth[key] + 1)

        def bank(key):
            return core.bank[bank_of[key]]

        @block.sync
        def _(sp):
            sp.dma_start(tab[:, :, :], a["l2a_tab"]).then_inc(c_in, 16)
            sp.dma_start(causal[:, :], a["l2a_mask"]).then_inc(c_in, 16)
            sp.dma_start(gnw[:, :], a["l2a_gnw"].partition_broadcast(P)).then_inc(c_in, 16)
            with sp.Fori(0, NQ) as g:
                for j, s_in in ((0, vw_in), (1, gw_in)):
                    sp.wait_ge(vraw_free, g * 2 + (j + 1))
                    sp.dma_start(vraw[:, :, :], a["l2a_wvg"][g * 2 + j]).then_inc(s_in, 16)
                sp.wait_ge(swraw_free, g + 1)
                sp.dma_start(swraw[:, :, :], a["l2a_ws2"][g]).then_inc(sw_in, 16)
                for c in range(8):
                    sp.wait_ge(qkraw_free, g * 8 + (c + 1))
                    sp.dma_start(qkraw[:, c % 2, :], a["l2a_wqk"][g * 8 + c]).then_inc(qkw_in[c % 2], 16)
                    if c % 4 == 3:
                        sp.wait_ge(woraw_free, g * 2 + (c // 4 + 1))
                        sp.dma_start(woraw[:, :, :], a["l2a_wo"][g * 2 + c // 4]).then_inc(wo_in, 16)

        @block.gpsimd
        def _(pool):
            pool.sem_inc(vraw_free, 1)
            pool.sem_inc(swraw_free, 1)
            pool.sem_inc(qkraw_free, 2)
            pool.sem_inc(woraw_free, 1)
            pool.sem_inc(times_sin, 2)
            pool.memset(pb[:, :, :, :], 0.0).then_inc(zeroed, 1)
            pool.memset(s1[:, 0, :, :], 0.0).then_inc(zeroed, 1)
            pool.memset(s2[:, 0, :], 0.0).then_inc(zeroed, 1)
            pool.wait_ge(c_in, 48)
            with pool.Fori(0, NQ) as g:
                for j in range(2):
                    pool.wait_ge(vg_hi, g * 2 + (j + 1))
                    pool.tensor_tensor(vgl[:, j, :, :], vraw[:, :, :], vgh[:, j, :, :].bitcast(F32),
                                       ALU.subtract).then_inc(vg_lo, 1)
                    pool.wait_ge(vg_lo, g * 2 + (j + 1))
                    pool.sem_inc(vraw_free, 1)
                pool.wait_ge(sw_in, g * 16 + 16)
                pool.wait_ge(pair_done, g * 2 + 1)
                pool.wait_ge(c_in, 48)
                core.pool_copy(pool, swh[:, :, :], swraw[:, :, 0:P]).then_inc(sw_split, 1)
                pool.tensor_copy(sbias[:, :], swraw[:, :, P]).then_inc(sw_split, 1)
                pool.wait_ge(sw_split, g * 3 + 2)
                pool.tensor_tensor(swl[:, :, :], swraw[:, :, 0:P], swh[:, :, :].bitcast(F32),
                                   ALU.subtract).then_inc(sw_split, 1)
                pool.wait_ge(sw_split, g * 3 + 3)
                pool.sem_inc(swraw_free, 1)

                def split_qk(c):
                    p, a_, w = c // 4, c // 2 % 2, c % 2
                    if c >= 2:
                        last = ("qk", (c - 2) // 4, (c - 2) // 2 % 2, w, 1)
                        pool.wait_ge(full[bank_of[last]], at(g, last))
                    pool.wait_ge(qkw_in[c % 2], g * 64 + 16 * (c // 2 + 1))
                    pool.wait_ge(c_in, 48)
                    core.pool_copy(pool, qkwh[:, c % 2, :], qkraw[:, c % 2, :]).then_inc(qkw_split, 1)
                    pool.wait_ge(qkw_split, g * 16 + (2 * c + 1))
                    pool.tensor_tensor(qkwl[:, c % 2, :], qkraw[:, c % 2, :], qkwh[:, c % 2, :].bitcast(F32),
                                       ALU.subtract).then_inc(qkw_split, 1)
                    pool.wait_ge(qkw_split, g * 16 + (2 * c + 2))
                    pool.sem_inc(qkraw_free, 1)

                split_qk(0)
                for t in range(TB):
                    pool.wait_ge(g_silu, g * TB + (t + 1))
                    pool.tensor_tensor(gq[:, t, :, :], gq[:, t, :, :], gnw[:, :].unsqueeze(1).to_broadcast([P, 4, DK]),
                                       ALU.mult).then_inc(g_ready, 1)
                for c in range(8):
                    if c < 7:
                        split_qk(c + 1)
                    for h in range(NH):
                        k = 2 * c + h
                        pool.wait_ge(qk_ready, g * 16 + (k + 1))
                        pool.wait_ge(swapped, g * 32 + (2 * k + 2))
                        pool.tensor_tensor(t2[:, h, :], swap[:, h, :], tab[:, 1, half(h)],
                                           ALU.mult).then_inc(times_sin, 1)
                    if c % 4 == 3:
                        p = c // 4
                        pool.wait_ge(wo_in, g * 32 + 16 * (p + 1))
                        pool.wait_ge(pair_done, g * 2 + (p + 1))
                        pool.wait_ge(c_in, 48)
                        core.pool_copy(pool, woh[:, :, :], woraw[:, :, :]).then_inc(wo_split, 1)
                        pool.wait_ge(wo_split, g * 4 + (2 * p + 1))
                        pool.tensor_tensor(wol[:, :, :], woraw[:, :, :], woh[:, :, :].bitcast(F32),
                                           ALU.subtract).then_inc(wo_split, 1)
                        pool.wait_ge(wo_split, g * 4 + (2 * p + 2))
                        pool.sem_inc(woraw_free, 1)
                        for i in range(4):
                            t = slice(2 * i, 2 * i + 2)
                            pool.wait_ge(scaled, g * 8 + (4 * p + i + 1))
                            pool.tensor_tensor(og[:, t, :, :], og[:, t, :, :], gq[:, t, 2 * p:2 * p + 2, :],
                                               ALU.mult).then_inc(gated, 1)

        @block.tensor
        def _(pe):
            pe.sem_inc(pair_done, 1)
            pe.wait_ge(c_in, 48)
            pe.wait_ge(zeroed, 3)
            with pe.Fori(0, NQ) as g:
                for j, kind in enumerate("vg"):
                    pe.wait_ge(vg_lo, g * 2 + (j + 1))
                    for t in range(TB):
                        key = (kind, t)
                        tok = slice(t * P, (t + 1) * P)
                        pe.wait_ge(free[bank_of[key]], at(g, key))
                        gemm3(pe, bank(key)[:, :], [core.xh[:, k, tok] for k in range(DC)],
                              [core.xl[:, k, tok] for k in range(DC)], [vgh[:, j, k, :] for k in range(DC)],
                              [vgl[:, j, k, :] for k in range(DC)]).then_inc(full[bank_of[key]], 1)
                pe.wait_ge(sw_split, g * 3 + 3)
                for p in range(2):
                    for h in range(NH):
                        key = ("s", p, h)
                        pe.wait_ge(free[bank_of[key]], at(g, key))
                        gemm3(pe, bank(key)[:, :], [swh[:, p, :]], [swl[:, p, :]], [t_h[:, half(h)]],
                              [t_l[:, half(h)]]).then_inc(full[bank_of[key]], 1)
                    for c in range(4):
                        a_, w = c // 2, c % 2
                        pe.wait_ge(qkw_split, g * 16 + (8 * p + 2 * c + 2))
                        for h in range(NH):
                            key = ("qk", p, a_, w, h)
                            pe.wait_ge(free[bank_of[key]], at(g, key))
                            gemm3(pe, bank(key)[:, :], [qkwh[:, w, k * P:(k + 1) * P] for k in range(DC)],
                                  [qkwl[:, w, k * P:(k + 1) * P] for k in range(DC)],
                                  [core.xh[:, k, half(h)] for k in range(DC)],
                                  [core.xl[:, k, half(h)] for k in range(DC)]).then_inc(full[bank_of[key]], 1)
                    for h in range(NH):
                        key = ("te", p, h)
                        pe.wait_ge(es_ready, g * 4 + (2 * p + h + 1))
                        pe.wait_ge(free[bank_of[key]], at(g, key))
                        for b in range(4):
                            t = 4 * h + b
                            mm = pe.transpose(bank(key)[:, b * P:(b + 1) * P], es[:, t * P:(t + 1) * P],
                                              core.ident[:, :])
                        mm.then_inc(full[bank_of[key]], 1)
                    for a_ in range(2):
                        for h in range(NH):
                            key = ("tk", p, a_, h)
                            pe.wait_ge(qk_ready, g * 16 + (8 * p + 4 * a_ + 2 + h + 3))
                            pe.wait_ge(free[bank_of[key]], at(g, key))
                            for b in range(4):
                                t = 4 * h + b
                                mm = pe.transpose(bank(key)[:, b * P:(b + 1) * P],
                                                  qt[:, a_, 1, t * P:(t + 1) * P], core.ident[:, :])
                            mm.then_inc(full[bank_of[key]], 1)
                    for a_ in range(2):
                        for h in range(NH):
                            key = ("at", p, a_, h)
                            pe.wait_ge(free[bank_of[key]], at(g, key))
                            for b in range(4):
                                tok = slice((4 * h + b) * P, (4 * h + b + 1) * P)
                                mm = pe.matmul(bank(key)[:, b * P:(b + 1) * P], qt[:, a_, 1, tok], qt[:, a_, 0, tok],
                                               start=True, stop=True)
                            mm.then_inc(full[bank_of[key]], 1)
                    pe.wait_ge(tm_ready, g * 12 + (6 * p + 6))
                    for h in range(NH):
                        key = ("s1", p, h)
                        pe.wait_ge(free[bank_of[key]], at(g, key))
                        for t in range(4 * h, min(4 * h + 4, TB - 1)):
                            for a_ in range(2):
                                c0 = (t % 4) * P + 64 * a_
                                mm = pe.matmul(bank(key)[:, c0:c0 + 64], ktm[:, a_, t, :],
                                               estm[:, t, 64 * a_:64 * a_ + 64], start=True, stop=True)
                        mm.then_inc(full[bank_of[key]], 1)
                    for h in range(NH):
                        key = ("s2", p, h)
                        pe.wait_ge(v_ready, g * TB + TB)
                        pe.wait_ge(free[bank_of[key]], at(g, key))
                        for t in range(4 * h, min(4 * h + 4, TB - 1)):
                            for a_ in range(2):
                                mm = pe.matmul(bank(key)[64 * a_:64 * a_ + 64, (t % 4) * P:(t % 4 + 1) * P],
                                               estm[:, t, 64 * a_:64 * a_ + 64], vq[:, t, 2 * p + a_, :],
                                               start=True, stop=True, tile_position=(0, 64 * a_))
                        mm.then_inc(full[bank_of[key]], 1)
                    for h in range(NH):
                        key = ("ok", p, h)
                        pe.wait_ge(free[bank_of[key]], at(g, key))
                        pe.wait_ge(at_ready, g * 8 + (4 * p + 4))
                        pe.wait_ge(s1_ready, g * 14 + (7 * p + (3 if h == 0 else 7)))
                        for t in range(4 * h, 4 * h + 4):
                            for a_ in range(2):
                                out = bank(key)[64 * a_:64 * a_ + 64, (t % 4) * P:(t % 4 + 1) * P]
                                mm = pe.matmul(out, estm[:, t, 64 * a_:64 * a_ + 64], atw[:, t, a_, :],
                                               start=True, stop=t == 0, tile_position=(0, 64 * a_))
                                if t:
                                    mm = pe.matmul(out, s1[:, t, a_, :], qt[:, a_, 0, t * P:(t + 1) * P],
                                                   start=False, stop=True, tile_position=(0, 64 * a_))
                        mm.then_inc(full[bank_of[key]], 1)
                    for h in range(NH):
                        key = ("tok", p, h)
                        pe.wait_ge(oke_ready, g * 4 + (2 * p + h + 1))
                        pe.wait_ge(free[bank_of[key]], at(g, key))
                        for b in range(4):
                            t = 4 * h + b
                            mm = pe.transpose(bank(key)[:, b * P:(b + 1) * P], oke[:, t * P:(t + 1) * P],
                                              core.ident[:, :])
                        mm.then_inc(full[bank_of[key]], 1)
                    for h in range(NH):
                        key = ("tq", p, h)
                        pe.wait_ge(soft, g * 12 + (6 * p + 5 + h))
                        pe.wait_ge(free[bank_of[key]], at(g, key))
                        for b in range(4):
                            t = 4 * h + b
                            mm = pe.transpose(bank(key)[:, b * P:(b + 1) * P], qv[:, t * P:(t + 1) * P],
                                              core.ident[:, :])
                        mm.then_inc(full[bank_of[key]], 1)
                    for i in range(4):
                        key = ("w2", p, i)
                        pe.wait_ge(pb_ready, g * 8 + (4 * p + 2 * (i // 2) + 2))
                        pe.wait_ge(free[bank_of[key]], at(g, key))
                        for t in (2 * i, 2 * i + 1):
                            mm = pe.matmul(bank(key)[:, (t % 2) * 256:(t % 2 + 1) * 256], es[:, t * P:(t + 1) * P],
                                           pb[:, t, :, :].rearrange("p a t -> p (a t)"), start=True, stop=True)
                        mm.then_inc(full[bank_of[key]], 1)
                    for i in range(4):
                        key = ("o", p, i)
                        pe.wait_ge(w2_ready, g * 8 + (4 * p + i + 1))
                        pe.wait_ge(s2_ready, g * 14 + (7 * p + 7))
                        pe.wait_ge(free[bank_of[key]], at(g, key))
                        for t in (2 * i, 2 * i + 1):
                            for a_ in range(2):
                                out = bank(key)[:, (t % 2) * 256 + a_ * P:(t % 2) * 256 + (a_ + 1) * P]
                                mm = pe.matmul(out, atw[:, t, a_, :], vq[:, t, 2 * p + a_, :], start=True, stop=t == 0)
                                if t:
                                    mm = pe.matmul(out, pb[:, t, a_, :], s2[:, t, :], start=False, stop=True)
                        mm.then_inc(full[bank_of[key]], 1)
                    for a_ in range(2):
                        for h in range(NH):
                            key = ("to", p, a_, h)
                            pe.wait_ge(gated, g * 8 + (4 * p + 2 * h + 2))
                            pe.wait_ge(free[bank_of[key]], at(g, key))
                            for b in range(4):
                                mm = pe.transpose(bank(key)[:, b * P:(b + 1) * P], og[:, 4 * h + b, a_, :],
                                                  core.ident[:, :])
                            mm.then_inc(full[bank_of[key]], 1)
                    pe.wait_ge(wo_split, g * 4 + (2 * p + 2))
                    pe.wait_ge(otl, g * 8 + (4 * p + 4))
                    for m in range(DC):
                        for h in range(NH):
                            key = ("wo", p, m, h)
                            pe.wait_ge(free[bank_of[key]], at(g, key))
                            gemm3(pe, bank(key)[:, :], [woh[:, a_, m * P:(m + 1) * P] for a_ in range(2)],
                                  [wol[:, a_, m * P:(m + 1) * P] for a_ in range(2)],
                                  [ogh[:, a_, half(h)] for a_ in range(2)],
                                  [ogl[:, a_, half(h)] for a_ in range(2)]).then_inc(full[bank_of[key]], 1)
                    pe.wait_ge(full[bank_of[key]], at(g, key))
                    pe.sem_inc(pair_done, 1)

        @block.scalar
        def _(act):
            act.wait_ge(c_in, 48)
            with act.Fori(0, NQ) as g:
                for j, s_in in ((0, vw_in), (1, gw_in)):
                    act.wait_ge(s_in, g * 16 + 16)
                    act.wait_ge(pair_done, g * 2 + 1)
                    act.activation(vgh[:, j, :, :], vraw[:, :, :], ACT.Copy).then_inc(vg_hi, 1)
                for t in range(TB):
                    key = ("g", t)
                    act.wait_ge(full[bank_of[key]], at(g, key))
                    act.activation(gq[:, t, :, :].rearrange("p a d -> p (a d)"), bank(key)[:, :],
                                   ACT.Silu).then_inc(free[bank_of[key]], 1)
                act.wait_ge(free[3], at(g, ("g", TB - 1)) + 1)
                act.sem_inc(g_silu, TB)
                for p in range(2):
                    for h in range(NH):
                        act.wait_ge(clipped, g * 8 + (4 * p + 2 * h + 2))
                        act.activation(es[:, half(h)], sc[:, half(h)], ACT.Exp).then_inc(es_ready, 1)
                    for c in range(4):
                        a_, w = c // 2, c % 2
                        for h in range(NH):
                            key = ("qk", p, a_, w, h)
                            k = 8 * p + 2 * c + h
                            act.wait_ge(full[bank_of[key]], at(g, key))
                            act.wait_ge(times_sin, g * 16 + (k + 1))
                            act.activation(swap[0:64, h, :], bank(key)[64:128, :], ACT.Copy).then_inc(swapped, 1)
                            act.activation(swap[64:128, h, :], bank(key)[0:64, :], ACT.Copy).then_inc(swapped, 1)
                    for h in range(NH):
                        key = ("te", p, h)
                        act.wait_ge(full[bank_of[key]], at(g, key))
                        act.activation(estm[:, 4 * h:4 * h + 4, :].rearrange("p t m -> p (t m)"), bank(key)[:, :],
                                       ACT.Copy).then_inc(free[bank_of[key]], 1)
                        act.wait_ge(free[bank_of[key]], at(g, key) + 1)
                        act.sem_inc(tm_ready, 1)
                    for a_ in range(2):
                        for h in range(NH):
                            key = ("tk", p, a_, h)
                            act.wait_ge(full[bank_of[key]], at(g, key))
                            act.activation(ktm[:, a_, 4 * h:4 * h + 4, :].rearrange("p t m -> p (t m)"),
                                           bank(key)[:, :], ACT.Copy).then_inc(free[bank_of[key]], 1)
                            act.wait_ge(free[bank_of[key]], at(g, key) + 1)
                            act.sem_inc(tm_ready, 1)
                    for h in range(NH):
                        act.wait_ge(shifted, g * 4 + (2 * p + h + 1))
                        act.activation(qv[:, half(h)], qv[:, half(h)], ACT.Exp).then_inc(exped, 1)
                    for i in range(4):
                        key = ("o", p, i)
                        act.wait_ge(full[bank_of[key]], at(g, key))
                        act.activation(og[:, 2 * i:2 * i + 2, :, :].rearrange("p t a d -> p (t a d)"),
                                       bank(key)[:, :], ACT.Square).then_inc(squared, 1)
                    act.wait_ge(sumsq, g * 8 + (4 * p + 4))
                    act.activation(ss[:, :, :], ss[:, :, :], ACT.Sqrt, bias=core.eps5[:, :],
                                   scale=1.0 / DK).then_inc(rooted, 1)
                    for a_ in range(2):
                        for h in range(NH):
                            key = ("to", p, a_, h)
                            act.wait_ge(full[bank_of[key]], at(g, key))
                            act.activation(ogh[:, a_, half(h)], bank(key)[:, :], ACT.Copy).then_inc(oth, 1)

        @block.vector
        def _(dve):
            for b in range(8):
                dve.sem_inc(free[b], 1)
            dve.sem_inc(qk_ready, 2)
            dve.wait_ge(c_in, 48)
            dve.wait_ge(zeroed, 3)
            with dve.Fori(0, NQ) as g:
                dve.wait_ge(pair_done, g * 2 + 1)
                for t in range(TB):
                    key = ("v", t)
                    dve.wait_ge(full[bank_of[key]], at(g, key))
                    dve.tensor_copy(vq[:, t, :, :].rearrange("p a d -> p (a d)"),
                                    bank(key)[:, :]).then_inc(free[bank_of[key]], 1)
                dve.wait_ge(free[3], at(g, ("v", TB - 1)) + 1)
                dve.sem_inc(v_ready, TB)
                dve.wait_ge(sw_split, g * 3 + 3)
                for p in range(2):
                    dve.wait_ge(pair_done, g * 2 + (p + 1))
                    for h in range(NH):
                        key = ("s", p, h)
                        n = g * 8 + (4 * p + 2 * h)
                        dve.wait_ge(full[bank_of[key]], at(g, key))
                        dve.tensor_scalar(sc[:, half(h)], bank(key)[:, :], sbias[:, p:p + 1], 32.0, ALU.add,
                                          ALU.min).then_inc(clipped, 1)
                        dve.wait_ge(clipped, n + 1)
                        dve.sem_inc(free[bank_of[key]], 1)
                        dve.tensor_scalar(sc[:, half(h)], sc[:, half(h)], -32.0, None, ALU.max).then_inc(clipped, 1)
                    for c in range(4):
                        a_, w = c // 2, c % 2
                        for h in range(NH):
                            key = ("qk", p, a_, w, h)
                            k = 8 * p + 2 * c + h
                            dst = qt[:, a_, w, half(h)]
                            dve.wait_ge(swapped, g * 32 + (2 * k + 2))
                            dve.tensor_tensor(dst, bank(key)[:, :], tab[:, 0, half(h)], ALU.mult).then_inc(times_cos, 1)
                            dve.wait_ge(times_cos, g * 16 + (k + 1))
                            dve.sem_inc(free[bank_of[key]], 1)
                            dve.wait_ge(times_sin, g * 16 + (k + 3))
                            dve.tensor_tensor(dst, dst, t2[:, h, :], ALU.add).then_inc(qk_ready, 1)
                        if c == 0:
                            for h in range(NH):
                                n = g * 4 + (2 * p + h)
                                dve.wait_ge(es_ready, n + 1)
                                if h:
                                    dve.wait_ge(summed, n)
                                dve.tensor_tensor_scan(cs[:, half(h)], core.ones_r[:, 0:1].bitcast(F32)
                                                       .to_broadcast([P, HALF]), es[:, half(h)],
                                                       cs[:, HALF - 1:HALF] if h else 0.0, ALU.mult,
                                                       ALU.add).then_inc(summed, 1)
                            dve.wait_ge(summed, g * 4 + (2 * p + 2))
                            dve.reciprocal(enz[:, :], cs).then_inc(enz_ready, 1)
                    for a_ in range(2):
                        for h in range(NH):
                            key = ("at", p, a_, h)
                            dve.wait_ge(full[bank_of[key]], at(g, key))
                            dve.tensor_tensor(atw[:, 4 * h:4 * h + 4, a_, :],
                                              bank(key)[:, :].rearrange("p (t q) -> p t q", q=P),
                                              causal[:, :].unsqueeze(1).to_broadcast([P, 4, P]),
                                              ALU.mult).then_inc(at_ready, 1)
                            dve.wait_ge(at_ready, g * 8 + (4 * p + 2 * a_ + h + 1))
                            dve.sem_inc(free[bank_of[key]], 1)
                    for name_, st, ready, width in (("s1", s1, s1_ready, 64), ("s2", s2, s2_ready, None)):
                        for t in range(TB - 1):
                            key = (name_, p, t // 4)
                            if t % 4 == 0:
                                dve.wait_ge(full[bank_of[key]], at(g, key))
                            ps = bank(key)[:, (t % 4) * P:(t % 4 + 1) * P]
                            flat = lambda x: x.rearrange("p a m -> p (a m)") if name_ == "s1" else x
                            if t:
                                dve.wait_ge(ready, g * 14 + (7 * p + t))
                            dve.tensor_tensor(flat(st[:, t + 1]), flat(st[:, t]), ps, ALU.add).then_inc(ready, 1)
                            if t % 4 == 3 or t == TB - 2:
                                dve.wait_ge(ready, g * 14 + (7 * p + t + 1))
                                dve.sem_inc(free[bank_of[key]], 1)
                    dve.wait_ge(enz_ready, g * 2 + (p + 1))
                    for h in range(NH):
                        key = ("ok", p, h)
                        dve.wait_ge(full[bank_of[key]], at(g, key))
                        dve.scalar_tensor_tensor(oke[:, half(h)], bank(key)[:, :], float(DK) ** -0.5, enz[:, half(h)],
                                                 ALU.mult, ALU.mult).then_inc(oke_ready, 1)
                        dve.wait_ge(oke_ready, g * 4 + (2 * p + h + 1))
                        dve.sem_inc(free[bank_of[key]], 1)
                    n = g * 12 + 6 * p
                    for h in range(NH):
                        key = ("tok", p, h)
                        t = slice(4 * h, 4 * h + 4)
                        ps = bank(key)[:, :].rearrange("p (t a m) -> p t a m", a=2, m=64)
                        dve.wait_ge(full[bank_of[key]], at(g, key))
                        dve.tensor_reduce(mx[:, t, :], ps, AX.X, ALU.max).then_inc(soft, 1)
                        dve.wait_ge(soft, n + (h + 1))
                        dve.tensor_tensor(qv[:, half(h)].rearrange("p (t a m) -> p t a m", a=2, m=64), ps,
                                          mx[:, t, :].unsqueeze(3).to_broadcast([P, 4, 2, 64]),
                                          ALU.subtract).then_inc(shifted, 1)
                        dve.wait_ge(shifted, g * 4 + (2 * p + h + 1))
                        dve.sem_inc(free[bank_of[key]], 1)
                    dve.wait_ge(exped, g * 4 + (2 * p + 2))
                    q4 = qv.rearrange("p (t a m) -> p t a m", a=2, m=64)
                    dve.tensor_reduce(rs[:, :, :], q4, AX.X, ALU.add).then_inc(soft, 1)
                    dve.wait_ge(soft, n + 3)
                    dve.reciprocal(rs[:, :, :], rs[:, :, :]).then_inc(soft, 1)
                    dve.wait_ge(soft, n + 4)
                    for h in range(NH):
                        t = slice(4 * h, 4 * h + 4)
                        dve.tensor_tensor(q4[:, t], q4[:, t], rs[:, t, :].unsqueeze(3).to_broadcast([P, 4, 2, 64]),
                                          ALU.mult).then_inc(soft, 1)
                    for h in range(NH):
                        key = ("tq", p, h)
                        dve.wait_ge(full[bank_of[key]], at(g, key))
                        for a_ in range(2):
                            r = slice(64 * a_, 64 * a_ + 64)
                            dve.tensor_tensor(pb[r, 4 * h:4 * h + 4, a_, :],
                                              bank(key)[r, :].rearrange("p (t q) -> p t q", q=P),
                                              enz[r, half(h)].rearrange("p (t q) -> p t q", q=P),
                                              ALU.mult).then_inc(pb_ready, 1)
                        dve.wait_ge(pb_ready, g * 8 + (4 * p + 2 * h + 2))
                        dve.sem_inc(free[bank_of[key]], 1)
                    for i in range(4):
                        key = ("w2", p, i)
                        dve.wait_ge(full[bank_of[key]], at(g, key))
                        dve.tensor_tensor(atw[:, 2 * i:2 * i + 2, :, :].rearrange("p t a q -> p (t a) q"),
                                          bank(key)[:, :].rearrange("p (u q) -> p u q", q=P),
                                          causal[:, :].unsqueeze(1).to_broadcast([P, 4, P]),
                                          ALU.mult).then_inc(w2_ready, 1)
                        dve.wait_ge(w2_ready, g * 8 + (4 * p + i + 1))
                        dve.sem_inc(free[bank_of[key]], 1)
                    for i in range(4):
                        dve.wait_ge(squared, g * 8 + (4 * p + i + 1))
                        dve.tensor_reduce(ss[:, 2 * i:2 * i + 2, :], og[:, 2 * i:2 * i + 2, :, :], AX.X,
                                          ALU.add).then_inc(sumsq, 1)
                    dve.wait_ge(rooted, g * 2 + (p + 1))
                    dve.reciprocal(rs[:, :, :], ss[:, :, :]).then_inc(rooted_inv, 1)
                    dve.wait_ge(rooted_inv, g * 2 + (p + 1))
                    dve.wait_ge(g_ready, g * TB + TB)
                    for i in range(4):
                        key = ("o", p, i)
                        t = slice(2 * i, 2 * i + 2)
                        dve.tensor_tensor(og[:, t, :, :], bank(key)[:, :].rearrange("p (t a d) -> p t a d", a=2, d=DK),
                                          rs[:, t, :].unsqueeze(3).to_broadcast([P, 2, 2, DK]),
                                          ALU.mult).then_inc(scaled, 1)
                        dve.wait_ge(scaled, g * 8 + (4 * p + i + 1))
                        dve.sem_inc(free[bank_of[key]], 1)
                    for a_ in range(2):
                        for h in range(NH):
                            key = ("to", p, a_, h)
                            dve.wait_ge(oth, g * 8 + (4 * p + 2 * a_ + h + 1))
                            dve.tensor_tensor(ogl[:, a_, half(h)], bank(key)[:, :], ogh[:, a_, half(h)].bitcast(F32),
                                              ALU.subtract).then_inc(otl, 1)
                            dve.wait_ge(otl, g * 8 + (4 * p + 2 * a_ + h + 1))
                            dve.sem_inc(free[bank_of[key]], 1)
                    for m in range(DC):
                        for h in range(NH):
                            key = ("wo", p, m, h)
                            dve.wait_ge(full[bank_of[key]], at(g, key))
                            dve.tensor_tensor(core.x[:, m, half(h)], core.x[:, m, half(h)], bank(key)[:, :],
                                              ALU.add).then_inc(free[bank_of[key]], 1)
                    dve.wait_ge(free[bank_of[key]], at(g, key) + 1)


def layer3(nc, core, a):
    norm(nc, core, "n3a", core.x, True, core.eps5)
    decay_attention(nc, core, a["l3a_w"], a["l3a_cols"])
    norm(nc, core, "n3f", core.x, True, core.eps5)
    with nc.sbuf_tensor("l3_cwp", [P, T], BF16) as cwp:
        router(nc, core, "r3", "groups", 16, 4, a["l3_gate"], a["l3_ebias"], cwp)
        gated_ffn(nc, core, "f3", a["l3_w"], 17, True, cw_parts=cwp)


def layer2_attention(nc, core, a):
    norm(nc, core, "n2a", core.x, True, core.eps5)
    state_attention(nc, core, a)


def layer2(nc, core, a):
    norm(nc, core, "n2f", core.x, True, core.eps5)
    with nc.sbuf_tensor("l2_cwp", [P, T], BF16) as cwp:
        router(nc, core, "r2", "softmax_norm", 32, 4, a["l2_gate"], None, cwp)
        gated_ffn(nc, core, "f2", a["l2_w"], 24, True, cw_parts=cwp)


def layer0_attention(nc, core, a):
    norm(nc, core, "n0a", core.x, True, core.eps5)
    small_attention(nc, core, "a0", a, "l0a", core.x, a["l0a_tab"], a["l0a_bv"], True)


def small_attention(nc, core, name, a, key, dst, tables, v_bias, add_x):
    with nc.sbuf_tensor(name + "_on", [P, 4, T], F32) as on:
        with nc.sbuf_tensor(name + "_qk", [P, 4, T], F32) as qk, \
                nc.sbuf_tensor(name + "_v", [P, TB, 16, 32], F32) as v:
            v_ones = nc.alloc_semaphore(name + "_vone")
            with nc.Block() as block:
                @block.gpsimd
                def _(pool):
                    pool.memset(v[:, :, :, :], 1.0).then_inc(v_ones, 1)
                    pool.wait_ge(v_ones, 1)
            project(nc, core, name + "p", 4, a[key + "_w"], tables, qk, True, a[key + "_wv"], v_bias, v, 16, 16)
            attend(nc, core, name + "h", qk, 2, v, on, 0.25, True, 2, a[key + "_hm"], a["causal"])
        out_product(nc, core, name + "o", on, 4, a[key + "_wo"], a[key + "_bo"], dst, add_x)


def layer1_attention(nc, core, a):
    norm(nc, core, "n1a", core.x, True, core.eps5)
    with nc.sbuf_tensor("a1_qk", [P, 20, T], F32) as qk:
        with nc.sbuf_tensor("a1_v", [P, TB, 8, 64], F32) as v:
            project(nc, core, "a1p", 20, a["l1a_w"], a["l1a_tab"], qk, False, a["l1a_wv"], None, v, 8, 64)
            attend(nc, core, "a1h", qk, 16, v, qk, 0.125, False, 4, a["l1a_hm"], a["window"], a["l1a_sink"])
        out_product(nc, core, "a1o", qk, 16, a["l1a_wo"], a["zero_cols"], core.x, True)


def layer1_mlp(nc, core, a):
    with ExitStack() as ctx:
        sb = lambda n, shape, dt=F32: ctx.enter_context(nc.sbuf_tensor("l1f_" + n, shape, dt))
        r = sb("r", [P, DC, T])
        gains = sb("gains", [P, 2, DC])
        z_h = sb("z_h", [P, T], F32R)
        z_l = sb("z_l", [P, T], F32R)
        g_in = nc.alloc_semaphore("l1f_g")
        with nc.Block() as block:
            @block.sync
            def _(sp):
                sp.dma_start(gains[:, :, :], a["l1f_gains"]).then_inc(g_in, 16)
                sp.wait_ge(g_in, 16)
        norm(nc, core, "n1f", core.x, True, core.eps5, dst=r, split=False)
        norm(nc, core, "n1r", r, False, core.eps6, gain=gains[:, 0, :])
        with nc.sbuf_tensor("l1f_attn", [P, DC, T], F32) as attn:
            small_attention(nc, core, "a2", a, "l1f", attn, None, None, False)
            resplit(nc, core, "s1f", gains[:, 1, :])
            low_rank(nc, core, attn, a["l1f_a"], z_h, z_l)
        gated_ffn(nc, core, "f1", a["l1_w"], 8, False, z_h=z_h, z_l=z_l, extra=r)


def low_rank(nc, core, attn, a_dram, z_h, z_l):
    with ExitStack() as ctx:
        sem = lambda n: nc.alloc_semaphore("lr_" + n)
        sb = lambda n, shape, dt=F32: ctx.enter_context(nc.sbuf_tensor("lr_" + n, shape, dt))
        a_in, split, at_ready, ah_ready, tanh_ready, z_ready, zh_ready, zl_ready = map(
            sem, ("a", "sp", "at", "ah", "th", "z", "zh", "zl"))
        aw = sb("aw", [P, DC, P])
        awh = sb("awh", [P, DC, P], F32R)
        awl = sb("awl", [P, DC, P], F32R)
        th = sb("th", [P, T])
        z = sb("zf", [P, T])
        block = ctx.enter_context(nc.Block())

        @block.sync
        def _(sp):
            sp.dma_start(aw[:, :, :], a_dram).then_inc(a_in, 16)

        @block.tensor
        def _(pe):
            pe.wait_ge(a_in, 16)
            for h in range(NH):
                for c in range(DC):
                    mm = pe.matmul(core.bank[h][:, :], aw[:, c, :], attn[:, c, half(h)], start=c == 0, stop=c == DC - 1)
                mm.then_inc(at_ready, 1)
            pe.wait_ge(split, 2)
            for h in range(NH):
                gemm3(pe, core.bank[2 + h][:, :], [awh[:, k, :] for k in range(DC)], [awl[:, k, :] for k in range(DC)],
                      [core.xh[:, k, half(h)] for k in range(DC)],
                      [core.xl[:, k, half(h)] for k in range(DC)]).then_inc(ah_ready, 1)

        @block.scalar
        def _(act):
            for h in range(NH):
                act.wait_ge(at_ready, h + 1)
                act.activation(th[:, half(h)], core.bank[h][:, :], ACT.Tanh).then_inc(tanh_ready, 1)
            for h in range(NH):
                act.wait_ge(z_ready, h + 1)
                act.activation(z_h[:, half(h)], z[:, half(h)], ACT.Copy).then_inc(zh_ready, 1)

        @block.vector
        def _(dve):
            dve.wait_ge(a_in, 16)
            dve.tensor_copy(awh[:, :, :], aw[:, :, :]).then_inc(split, 1)
            dve.wait_ge(split, 1)
            dve.tensor_tensor(awl[:, :, :], aw[:, :, :], awh[:, :, :].bitcast(F32), ALU.subtract).then_inc(split, 1)
            for h in range(NH):
                dve.wait_ge(tanh_ready, h + 1)
                dve.wait_ge(ah_ready, h + 1)
                dve.scalar_tensor_tensor(z[:, half(h)], th[:, half(h)], 0.1, core.bank[2 + h][:, :], ALU.mult,
                                         ALU.mult).then_inc(z_ready, 1)
            for h in range(NH):
                dve.wait_ge(zh_ready, h + 1)
                dve.tensor_tensor(z_l[:, half(h)], z[:, half(h)], z_h[:, half(h)].bitcast(F32),
                                  ALU.subtract).then_inc(zl_ready, 1)


def layer0(nc, core, a):
    norm(nc, core, "n0f", core.x, True, core.eps5)
    with nc.sbuf_tensor("l0_cwp", [P, T], BF16) as cwp, nc.sbuf_tensor("l0_cwf", [P, T], F32) as cwf, \
            nc.sbuf_tensor("l0_b2", [P, D], F32) as b2:
        b2_in = nc.alloc_semaphore("l0_b2_in")
        with nc.Block() as block:
            @block.sync
            def _(sp):
                sp.dma_start(b2[:, :], a["l0_b2"]).then_inc(b2_in, 16)
                sp.wait_ge(b2_in, 16)
        router(nc, core, "r0", "softmax_bias", 16, 6, a["l0_gate"], a["l0_gbias"], cwp, cwf)
        gated_ffn(nc, core, "f0", a["l0_w"], 25, True, cw_parts=cwp, cw_f32=cwf, b2=b2)


def program(nc, a, stages=("0a", "0f", "1a", "1f", "2a", "2f", "3")):
    with ExitStack() as ctx:
        core = Core(nc, ctx)
        load_inputs(nc, core, a["x"], a["consts"])
        for s in stages:
            with nc.cleanup_on_exit():
                STAGES[s](nc, core, a)
        store_output(nc, core, a["out"])


STAGES = {"0a": layer0_attention, "0f": layer0, "1a": layer1_attention, "1f": layer1_mlp, "2a": layer2_attention,
          "2f": layer2, "3": layer3}


def by_feature(w):
    w = np.asarray(w)
    return np.ascontiguousarray(w.reshape(-1, P, w.shape[1]).transpose(1, 0, 2))


def ffn_weights(gate, up, down, b1, b3, owner, rows, kc=DC, gate_extra=None):
    hidden = gate.shape[1]
    n = -(-hidden // P)
    G, U, DN, B, S, cols = ffn_cols(kc)
    out = np.zeros((n, P, cols), np.float32)
    for c in range(n):
        lo, hi = c * P, min(hidden, (c + 1) * P)
        w = hi - lo
        for k in range(DC):
            out[c, :, G + k * P:G + k * P + w] = gate[k * P:(k + 1) * P, lo:hi]
            out[c, :, U + k * P:U + k * P + w] = up[k * P:(k + 1) * P, lo:hi]
        if gate_extra is not None:
            out[c, :gate_extra.shape[0], G + DC * P:G + DC * P + w] = gate_extra[:, lo:hi]
        out[c, :w, DN:DN + D] = down[lo:hi, :]
        if b1 is not None:
            out[c, :w, B] = b1[lo:hi]
            out[c, :w, B + 1] = b3[lo:hi]
        if owner is not None:
            for j in range(w):
                o = owner[lo + j]
                if o == 96:
                    out[c, 96, S + j] = 1.0
                else:
                    out[c, [o, 32 + o, 64 + o], S + j] = 1.0
    return out


def qk_chunk(w, bias):
    return np.concatenate([by_feature(w).reshape(P, DC * P), bias[:, None], np.roll(bias, 64)[:, None]], 1)


def rope_tables(angle, sign):
    s = np.sin(angle)
    s[:64] *= sign
    s[64:] *= -sign
    return np.ascontiguousarray(np.stack([np.cos(angle), s], 1).astype(np.float32))


def out_chunks(w):
    out = np.zeros((4, 4, 32, D), np.float32)
    out[:, :, :16] = w.reshape(4, 4, 16, D)
    return out.reshape(4, P, D)


def lay_out(inp):
    f = {k: np.asarray(v) for k, v in inp.items()}
    a = {}
    a["x"] = by_feature(f["L0_attn_x"][0].T)
    c = np.zeros((P, C_COLS), np.float32)
    c[:, C_ONES:C_ONES + P] = 1.0 / D
    c[:, C_IDENT:C_IDENT + P] = np.eye(P)
    a["consts"] = c
    a["zero_cols"] = np.zeros((P, DC), np.float32)
    k, q = np.arange(P)[:, None], np.arange(P)[None, :]
    m = np.zeros((P, 2, P + 4), np.float32)
    m[:, 0, :P][k > q] = -1e30
    m[:, 1, :P][k < q] = -1e30
    for j in range(4):
        m[32 * j + 16, 0, P + j] = 1.0
    a["causal"] = m
    m = np.zeros((P, 2, 2 * P), np.float32)
    c2 = np.arange(2 * P)[None, :]
    m[:, 0][(c2 >= k) & (c2 < k + 64)] = -1e30
    m[:, 1][(P + k - c2 >= 0) & (P + k - c2 < 64)] = -1e30
    a["window"] = m
    pos = np.arange(T, dtype=np.float32)
    r = np.arange(P)
    order = [np.array([(8 * g + (x % 64) // 8) * 16 + 2 * (x % 8) + x // 64 for x in r]) for g in range(2)]
    a["l0a_w"] = np.stack([qk_chunk(f[f"L0_attn_W{n}"].T[:, o], f[f"L0_attn_b{n}"][o]) for n in "qk" for o in order])
    a["l0a_wv"] = by_feature(f["L0_attn_Wv"].T)
    a["l0a_bv"] = f["L0_attn_bv"]
    freq = np.float32(10000.0) ** (-np.arange(0, 16, 2, dtype=np.float32) / np.float32(16))
    a["l0a_tab"] = rope_tables(pos[None, :] * freq[r % 8][:, None], -1.0)
    a["l0a_hm"] = ((r[:, None] % 64) // 8 == np.arange(8)).astype(np.float32)
    a["l0a_wo"] = out_chunks(f["L0_attn_Wo"].T)
    a["l0a_bo"] = np.ascontiguousarray(f["L0_attn_bo"].reshape(DC, P).T)
    w = f["L1_attn_W_qkv"]
    rows = lambda h0, h1: np.concatenate([h0 * 64 + np.arange(32), h1 * 64 + np.arange(32),
                                          h0 * 64 + 32 + np.arange(32), h1 * 64 + 32 + np.arange(32)])
    cols = [rows(8 * g + m, 8 * g + 4 + m) for g in range(4) for m in range(4)]
    cols += [2048 + rows(2 * g, 2 * g + 1) for g in range(4)]
    a["l1a_w"] = np.stack([qk_chunk(w[:, c], np.zeros(P, np.float32)) for c in cols])
    a["l1a_wv"] = by_feature(w[:, 2560:3072])
    freq = np.float32(1.0 / 1024.0) ** np.linspace(0.0, 1.0, 16, dtype=np.float32)
    freq = np.concatenate([freq, np.zeros(16, np.float32)])
    a["l1a_tab"] = rope_tables(pos[None, :] * freq[r % 32][:, None], 1.0)
    a["l1a_hm"] = ((r[:, None] % 64) // 32 == np.arange(2)).astype(np.float32)
    wo = f["L1_attn_W_out"]
    a["l1a_wo"] = np.stack([np.concatenate([wo[(8 * g + m) * 64:][:64], wo[(8 * g + 4 + m) * 64:][:64]])
                            for g in range(4) for m in range(4)])
    a["l1a_sink"] = np.ascontiguousarray(f["L1_attn_s"][0].reshape(4, 2, 4).transpose(0, 2, 1).reshape(32))
    a["l1f_w"] = np.stack([qk_chunk(f[f"L1_ffn_W{n}"].T[:, g * P:(g + 1) * P], np.zeros(P, np.float32))
                           for n in "qk" for g in range(2)])
    a["l1f_wv"] = by_feature(f["L1_ffn_Wv"].T)
    a["l1f_hm"] = (r[:, None] // 16 == np.arange(8)).astype(np.float32)
    a["l1f_wo"] = out_chunks(f["L1_ffn_Wo"].T)
    a["l1f_bo"] = np.zeros((P, DC), np.float32)
    a["l1f_gains"] = np.ascontiguousarray(np.stack([f[f"L1_ffn_ln{n}_w"].reshape(DC, P).T for n in (1, 2)], 1))
    aw = np.zeros((D, P), np.float32)
    aw[:, :16] = f["L1_ffn_A"]
    a["l1f_a"] = by_feature(aw)
    a["l1_w"] = ffn_weights(f["L1_ffn_W_in_base"].T, f["L1_ffn_W_up_base"].T, f["L1_ffn_W_down"].T, None, None, None,
                            0, kc=3, gate_extra=f["L1_ffn_B"])
    E, H = 16, 176
    g = np.concatenate([f["L0_ffn_w1"].reshape(E * H, D), f["L0_ffn_ws1"]]).T
    u = np.concatenate([f["L0_ffn_w3"].reshape(E * H, D), f["L0_ffn_ws3"]]).T
    dn = np.concatenate([f["L0_ffn_w2"].transpose(0, 2, 1).reshape(E * H, D), f["L0_ffn_ws2"].T])
    b1 = np.concatenate([f["L0_ffn_b1"].reshape(-1), f["L0_ffn_bs1"]])
    b3 = np.concatenate([f["L0_ffn_b3"].reshape(-1), f["L0_ffn_bs3"]])
    own = [e for e in range(E) for _ in range(H)] + [96] * 352
    a["l0_w"] = ffn_weights(g, u, dn, b1, b3, own, E)
    a["l0_gate"] = by_feature(f["L0_ffn_gate_w"].T)
    a["l0_gbias"] = f["L0_ffn_gate_b"]
    b2 = np.zeros((P, D), np.float32)
    b2[:E] = f["L0_ffn_b2"]
    b2[96] = f["L0_ffn_bs2"]
    a["l0_b2"] = b2
    ws1 = np.zeros((D, P), np.float32)
    ws1[:, :16] = f["L2_attn_Ws1"].T
    a["l2a_ws1"] = by_feature(ws1)
    ws2 = np.zeros((4, P, 2, P + 1), np.float32)
    ws2[:, :16, :, :P] = f["L2_attn_Ws2"].reshape(4, 2, P, 16).transpose(0, 3, 1, 2)
    ws2[:, :, :, P] = f["L2_attn_bs2"].reshape(4, 2, P).transpose(0, 2, 1)
    a["l2a_ws2"] = ws2
    chunk = lambda w, h: by_feature(w.T[:, h * P:(h + 1) * P]).reshape(P, DC * P)
    a["l2a_wqk"] = np.stack([chunk(f[f"L2_attn_W{n}"], h) for h in range(16) for n in "qk"])
    a["l2a_wvg"] = np.stack([by_feature(f[f"L2_attn_W{n}"].T[:, g * 512:(g + 1) * 512])
                             for g in range(4) for n in "vg"])
    a["l2a_wo"] = np.ascontiguousarray(f["L2_attn_Wo"].T.reshape(8, 2, P, D).transpose(0, 2, 1, 3))
    freq = np.float32(1.0) / np.float32(10000.0) ** (np.arange(0, 128, 2, dtype=np.float32) / np.float32(128))
    a["l2a_tab"] = rope_tables(pos[None, :] * freq[r % 64][:, None], -1.0)
    a["l2a_mask"] = (k <= q).astype(np.float32)
    a["l2a_gnw"] = f["L2_attn_g_norm_weight"]
    E, H = 32, 96
    gu = f["L2_ffn_gate_up_proj"]
    g = gu[:, :, :H].transpose(1, 0, 2).reshape(D, E * H)
    u = gu[:, :, H:].transpose(1, 0, 2).reshape(D, E * H)
    dn = f["L2_ffn_down_proj"].reshape(E * H, D)
    a["l2_w"] = ffn_weights(g, u, dn, None, None, [e for e in range(E) for _ in range(H)], E)
    a["l2_gate"] = by_feature(f["L2_ffn_gate"])
    a["l3a_w"] = by_feature(np.concatenate([f["L3_attn_Wv"], f["L3_attn_Wq"], f["L3_attn_Wg"], f["L3_attn_Wo"]], 1))
    vec = [np.repeat(f["L3_attn_beta"], 16), f["L3_attn_ln_g"], f["L3_attn_ln_b"]]
    a["l3a_cols"] = np.ascontiguousarray(np.stack([v.reshape(DC, P).T for v in vec], 1))
    E, H = 16, 128
    g = np.concatenate([f["L3_ffn_gate_proj"].reshape(E * H, D), f["L3_ffn_shared_gate"]]).T
    u = np.concatenate([f["L3_ffn_up_proj"].reshape(E * H, D), f["L3_ffn_shared_up"]]).T
    dn = np.concatenate([f["L3_ffn_down_proj"].transpose(0, 2, 1).reshape(E * H, D), f["L3_ffn_shared_down"].T])
    a["l3_w"] = ffn_weights(g, u, dn, None, None, [e for e in range(E) for _ in range(H)] + [96] * H, E)
    a["l3_gate"] = by_feature(f["L3_ffn_gate_weight"].T)
    a["l3_ebias"] = f["L3_ffn_expert_bias"]
    return a


def kernel(**inputs):
    import concourse.bacc as bacc
    from concourse.bass_utils import run_bass_kernel_spmd

    nc = bacc.Bacc("TRN2", target_bir_lowering=False, num_devices=1)
    arrays = {f"in_{k}_dram": np.ascontiguousarray(v) for k, v in lay_out(inputs).items()}
    a = {k[3:-5]: nc.dram_tensor(k, v.shape, mybir.dt.from_np(v.dtype), kind="ExternalInput").ap()
         for k, v in arrays.items()}
    a["out"] = nc.dram_tensor("out_0_dram", (P, DC, T), F32, kind="ExternalOutput").ap()
    program(nc, a)
    r = run_bass_kernel_spmd(nc, [arrays], core_ids=[0])
    got = r.results[0]["out_0_dram"]
    return np.ascontiguousarray(got.transpose(1, 0, 2).reshape(D, T).T)[None]
```

```python
import numpy as np
import concourse.bass as bass
from concourse import mybir
from contextlib import ExitStack

F32 = mybir.dt.float32
F32R = mybir.dt.float32r
BF16 = mybir.dt.bfloat16
ALU = mybir.AluOpType
ACT = mybir.ActivationFunctionType
AX = mybir.AxisListType

P = 128
T = 1024
D = 256
DC = D // P
HALF = 512
NH = T // HALF
TB = T // P
BIG = 3.0e38

C_ONES, C_IDENT, C_ZERO, C_ONE = 0, 128, 256, 384
C_MISC = 512
C_COLS = 1024


def half(h):
    return slice(h * HALF, (h + 1) * HALF)


class Core:

    def __init__(self, nc, ctx):
        self.nc = nc
        self.bank = [ctx.enter_context(nc.psum_tensor(f"bank{i}", [P, HALF], F32)) for i in range(8)]
        sb = lambda name, shape, dt=F32: ctx.enter_context(nc.sbuf_tensor(name, shape, dt))
        self.x = sb("x_resid", [P, DC, T])
        self.xn = sb("x_norm", [P, DC, T])
        self.xh = sb("x_norm_h", [P, DC, T], F32R)
        self.xl = sb("x_norm_l", [P, DC, T], F32R)
        self.mean_w = sb("mean_w", [P, P])
        self.ident = sb("ident", [P, P])
        self.zero_r = sb("zero_r", [P, P], F32R)
        self.ones_r = sb("ones_r", [P, P], F32R)
        self.ident_b = sb("ident_b", [P, P], BF16)
        self.eps5 = sb("eps5", [P, 1])
        self.eps6 = sb("eps6", [P, 1])

    def pool_copy(self, pool, dst, src):
        one = self.ones_r[:, 0:1].bitcast(F32)
        for _ in range(len(src.shape) - 2):
            one = one.unsqueeze(1)
        return pool.tensor_tensor(dst, src, one.to_broadcast(list(src.shape)), ALU.mult)


def load_inputs(nc, core, x_in, consts):
    x_loaded, c_loaded, made = map(nc.alloc_semaphore, ("x_loaded", "c_loaded", "c_made"))
    with nc.Block() as block:

        @block.sync
        def _(sp):
            sp.dma_start(core.x[:, :, :], x_in).then_inc(x_loaded, 16)
            sp.wait_ge(x_loaded, 16)

        @block.scalar
        def _(act):
            act.dma_start(core.mean_w[:, :], consts[:, C_ONES:C_ONES + P]).then_inc(c_loaded, 16)
            act.dma_start(core.ident[:, :], consts[:, C_IDENT:C_IDENT + P]).then_inc(c_loaded, 16)
            act.wait_ge(c_loaded, 32)

        @block.gpsimd
        def _(pool):
            pool.memset(core.eps5[:, :], 1e-5).then_inc(made, 1)
            pool.memset(core.eps6[:, :], 1e-6).then_inc(made, 1)
            pool.wait_ge(c_loaded, 32)
            pool.tensor_scalar(core.zero_r[:, :], core.ident[:, :], 0.0, None, ALU.mult).then_inc(made, 1)
            pool.tensor_scalar(core.ones_r[:, :], core.ident[:, :], 0.0, 1.0, ALU.mult, ALU.add).then_inc(made, 1)
            pool.tensor_copy(core.ident_b[:, :], core.ident[:, :]).then_inc(made, 1)
            pool.wait_ge(made, 5)


def store_output(nc, core, out):
    stored = nc.alloc_semaphore("stored")
    with nc.Block() as block:

        @block.sync
        def _(sp):
            sp.dma_start(out, core.x[:, :, :]).then_inc(stored, 16)
            sp.wait_ge(stored, 16)


def norm(nc, core, name, src, center, eps, dst=None, gain=None, split=True, shift=None):
    dst = core.xn if dst is None else dst
    with ExitStack() as ctx:
        sem = lambda n: nc.alloc_semaphore(f"{name}_{n}")
        sb = lambda n, shape, dt=F32: ctx.enter_context(nc.sbuf_tensor(f"{name}_{n}", shape, dt))
        mean_ready, xc_ready, sq_ready, var_ready, std_ready = map(sem, ("mean", "xc", "sq", "var", "std"))
        rstd_ready, spread, xn_ready, hi_ready, lo_ready, scaled = map(
            sem, ("rstd", "spread", "xn", "hi", "lo", "scaled"))
        sq = sb("sq", [P, DC, T])
        std = sb("std", [P, TB])
        rstd = sb("rstdv", [P, TB])
        xc = sb("xc_b", [P, DC, T]) if center else src
        block = ctx.enter_context(nc.Block())
        HB = TB // NH

        @block.tensor
        def _(pe):
            if center:
                for h in range(NH):
                    for c in range(DC):
                        mm = pe.matmul(core.bank[h][:, :], core.mean_w[:, :], src[:, c, half(h)],
                                       start=c == 0, stop=c == DC - 1)
                    mm.then_inc(mean_ready, 1)
            for h in range(NH):
                pe.wait_ge(sq_ready, h + 1)
                for b in range(HB):
                    t = h * HB + b
                    for c in range(DC):
                        mm = pe.matmul(core.bank[2 + h][:, b:b + 1], sq[:, c, t * P:(t + 1) * P],
                                       core.mean_w[:, 0:1], start=c == 0, stop=c == DC - 1)
                mm.then_inc(var_ready, 1)
            for h in range(NH):
                pe.wait_ge(rstd_ready, h + 1)
                for b in range(HB):
                    t = h * HB + b
                    mm = pe.matmul(core.bank[4 + h][:, b * P:(b + 1) * P], rstd[:, t:t + 1].to_broadcast([P, P]),
                                   core.ident[:, :], start=True, stop=True)
                mm.then_inc(spread, 1)

        @block.vector
        def _(dve):
            if center:
                for h in range(NH):
                    dve.wait_ge(mean_ready, h + 1)
                    for c in range(DC):
                        dve.tensor_tensor(xc[:, c, half(h)], src[:, c, half(h)], core.bank[h][:, :],
                                          ALU.subtract).then_inc(xc_ready, 1)
            for h in range(NH):
                dve.wait_ge(std_ready, h + 1)
                bl = slice(h * HB, (h + 1) * HB)
                dve.reciprocal(rstd[:, bl], std[:, bl]).then_inc(rstd_ready, 1)
            for h in range(NH):
                dve.wait_ge(spread, h + 1)
                if center:
                    dve.wait_ge(xc_ready, DC * (h + 1))
                for c in range(DC):
                    dve.tensor_tensor(dst[:, c, half(h)], xc[:, c, half(h)], core.bank[4 + h][:, :],
                                      ALU.mult).then_inc(xn_ready, 1)
                if shift is not None:
                    dve.wait_ge(xn_ready, DC * (h + 1))
                    for c in range(DC):
                        dve.tensor_scalar(dst[:, c, half(h)], dst[:, c, half(h)], gain[:, c:c + 1],
                                          shift[:, c:c + 1], ALU.mult, ALU.add).then_inc(scaled, 1)
            if split and gain is None:
                for h in range(NH):
                    dve.wait_ge(hi_ready, DC * (h + 1))
                    dve.tensor_tensor(core.xl[:, 1, half(h)], dst[:, 1, half(h)],
                                      core.xh[:, 1, half(h)].bitcast(F32), ALU.subtract).then_inc(lo_ready, 1)
            if split and gain is not None:
                for n in range(DC * NH):
                    h, c = n // DC, n % DC
                    dve.wait_ge(hi_ready, n + 1)
                    dve.scalar_tensor_tensor(core.xl[:, c, half(h)], dst[:, c, half(h)], gain[:, c:c + 1],
                                             core.xh[:, c, half(h)].bitcast(F32), ALU.mult,
                                             ALU.subtract).then_inc(lo_ready, 1)

        @block.gpsimd
        def _(pool):
            if split and gain is None:
                for h in range(NH):
                    pool.wait_ge(hi_ready, DC * h + 1)
                    pool.tensor_tensor(core.xl[:, 0, half(h)], dst[:, 0, half(h)],
                                       core.xh[:, 0, half(h)].bitcast(F32), ALU.subtract).then_inc(lo_ready, 1)

        @block.scalar
        def _(act):
            for h in range(NH):
                if center:
                    act.wait_ge(xc_ready, DC * (h + 1))
                act.activation(sq[:, :, half(h)], xc[:, :, half(h)], ACT.Square).then_inc(sq_ready, 1)
            for h in range(NH):
                act.wait_ge(var_ready, h + 1)
                act.activation(std[:, h * HB:(h + 1) * HB], core.bank[2 + h][:, 0:HB], ACT.Sqrt,
                               bias=eps[:, :]).then_inc(std_ready, 1)
            if split:
                for h in range(NH):
                    for c in range(DC):
                        act.wait_ge(xn_ready, DC * h + c + 1)
                        act.activation(core.xh[:, c, half(h)], dst[:, c, half(h)], ACT.Copy,
                                       scale=1.0 if gain is None else gain[:, c:c + 1]).then_inc(hi_ready, 1)


def resplit(nc, core, name, gain):
    hi_ready, lo_ready = nc.alloc_semaphore(f"{name}_hi"), nc.alloc_semaphore(f"{name}_lo")
    with nc.Block() as block:

        @block.scalar
        def _(act):
            for h in range(NH):
                for c in range(DC):
                    act.activation(core.xh[:, c, half(h)], core.xn[:, c, half(h)], ACT.Copy,
                                   scale=gain[:, c:c + 1]).then_inc(hi_ready, 1)

        @block.vector
        def _(dve):
            for h in range(NH):
                for c in range(DC):
                    dve.wait_ge(hi_ready, DC * h + c + 1)
                    dve.scalar_tensor_tensor(core.xl[:, c, half(h)], core.xn[:, c, half(h)], gain[:, c:c + 1],
                                             core.xh[:, c, half(h)].bitcast(F32), ALU.mult,
                                             ALU.subtract).then_inc(lo_ready, 1)


def ffn_cols(kc):
    g = 0
    u = kc * P
    d = u + DC * P
    b = d + D
    s = b + 2
    return g, u, d, b, s, s + P


def gated_ffn(nc, core, name, w_dram, n_chunks, routed, cw_parts=None, cw_f32=None, b2=None, z_h=None, z_l=None):
    kc = 3 if z_h is not None else DC
    G, U, DN, B, S, WCOLS = ffn_cols(kc)
    with ExitStack() as ctx:
        sem = lambda n: nc.alloc_semaphore(f"{name}_{n}")
        sb = lambda n, shape, dt=F32: ctx.enter_context(nc.sbuf_tensor(f"{name}_{n}", shape, dt))
        w_in = [sem("w_in0"), sem("w_in1")]
        raw_free, w_split, w_free = sem("raw_free"), sem("w_split"), sem("w_free")
        g_ready, u_ready, cwb_ready, y_done = sem("g"), sem("u"), sem("cwb"), sem("y")
        silu_ready, hh_ready, t_ready, h_ready, hl_ready = sem("silu"), sem("hh"), sem("t"), sem("h"), sem("hl")
        x_added = sem("x_added")
        zeroed = sem("zeroed")
        raw = sb("raw", [P, 2, WCOLS])
        wh = sb("wh", [P, 2, B], F32R)
        wl = sb("wl", [P, 2, B], F32R)
        bias = sb("bias", [P, 2, 2])
        sel = sb("sel", [P, 2, P], BF16)
        sg = sb("sg", [P, 2, HALF])
        tf = sb("tf", [P, 2, HALF])
        hf = sb("hf", [P, 2, HALF])
        hh = sb("hhi", [P, 2, HALF], F32R)
        hl = sb("hlo", [P, 2, HALF], F32R)
        acc = [[core.bank[2 * m + h] for h in range(NH)] for m in range(DC)]
        last = 2 * n_chunks
        block = ctx.enter_context(nc.Block())

        def chunks(eng, body):
            with eng.Fori(0, n_chunks // 2) as i:
                for slot in range(2):
                    body(i * 2 + slot, i, slot)
            if n_chunks % 2:
                body(n_chunks - 1, n_chunks // 2, 0)

        @block.sync
        def _(sp):
            def load(c, i, slot):
                sp.wait_ge(raw_free, c + 1)
                sp.dma_start(raw[:, slot, :], w_dram[c]).then_inc(w_in[slot], 16)
            chunks(sp, load)

        @block.gpsimd
        def _(pool):
            pool.sem_inc(raw_free, 2)
            pool.wait_ge(zeroed, 4)

            def split(c, i, slot):
                pool.wait_ge(w_in[slot], i * 16 + 16)
                pool.wait_ge(w_free, c + 1)
                core.pool_copy(pool, wh[:, slot, :], raw[:, slot, 0:B]).then_inc(w_split, 1)
                pool.tensor_copy(bias[:, slot, :], raw[:, slot, B:B + 2]).then_inc(w_split, 1)
                pool.tensor_copy(sel[:, slot, :], raw[:, slot, S:S + P]).then_inc(w_split, 1)
                pool.wait_ge(w_split, c * 4 + 3)
                pool.tensor_tensor(wl[:, slot, :], raw[:, slot, 0:B], wh[:, slot, :].bitcast(F32),
                                   ALU.subtract).then_inc(w_split, 1)
                pool.wait_ge(w_split, c * 4 + 4)
                pool.sem_inc(raw_free, 1)
            chunks(pool, split)

        @block.tensor
        def _(pe):
            def gemm(out, cols, n_k, slot, h, third):
                n = 0
                for k in range(n_k):
                    c0 = cols + k * P
                    xh = core.xh[:, k, half(h)] if k < DC else third[0][:, half(h)]
                    xl = core.xl[:, k, half(h)] if k < DC else third[1][:, half(h)]
                    for w, x in ((wh, xh), (wl, xh), (wh, xl)):
                        mm = pe.matmul(out[:, :], w[:, slot, c0:c0 + P], x, start=n == 0, stop=n == 3 * n_k - 1)
                        n += 1
                return mm

            def down(slot, h, par):
                for m in range(DC):
                    c0 = DN + m * P
                    for w, x in ((wh, hh), (wl, hh), (wh, hl)):
                        mm = pe.matmul(acc[m][h][:, :], w[:, slot, c0:c0 + P], x[:, par, :], start=False, stop=False,
                                       skip_group_check=True)
                return mm

            def products(c, i, slot):
                pe.wait_ge(w_split, c * 4 + 4)
                for h in range(NH):
                    k = c * 2 + h
                    gate, up = core.bank[4 + 2 * h], core.bank[5 + 2 * h]
                    pe.wait_ge(h_ready, k + 1)
                    gemm(gate, G, kc, slot, h, (z_h, z_l)).then_inc(g_ready, 1)
                    gemm(up, U, DC, slot, h, None).then_inc(u_ready, 1)
                    pe.wait_ge(hl_ready, k + 1)
                    down(slot if h else 1 - slot, 1 - h, 1 - h).then_inc(y_done, 1)
                    if routed:
                        pe.wait_ge(silu_ready, k + 1)
                        pe.matmul(gate[:, :], sel[:, slot, :], cw_parts[:, half(h)], start=True,
                                  stop=True).then_inc(cwb_ready, 1)
                    if h == 0:
                        pe.wait_ge(y_done, k + 2)
                        pe.sem_inc(w_free, 1)

            pe.wait_ge(zeroed, 4)
            for m in range(DC):
                for h in range(NH):
                    if b2 is None:
                        pe.matmul(acc[m][h][:, :], core.zero_r[:, :], core.xh[:, 0, half(h)], start=True, stop=False,
                                  skip_group_check=True)
                    else:
                        pe.matmul(acc[m][h][:, :], b2[:, m * P:(m + 1) * P], cw_f32[:, half(h)], start=True,
                                  stop=False, skip_group_check=True)
            pe.sem_inc(y_done, 1)
            pe.sem_inc(w_free, 1)
            chunks(pe, products)
            pe.wait_ge(hl_ready, last + 1)
            down((n_chunks - 1) % 2, 1, 1).then_inc(y_done, 1)

        @block.scalar
        def _(act):
            def rows(c, i, slot):
                act.wait_ge(w_split, c * 4 + 4)
                for h in range(NH):
                    k = c * 2 + h
                    act.wait_ge(g_ready, k + 1)
                    act.wait_ge(t_ready, k + 1)
                    act.activation(sg[:, h, :], core.bank[4 + 2 * h][:, :], ACT.Silu,
                                   bias=bias[:, slot, 0:1]).then_inc(silu_ready, 1)
                    act.wait_ge(h_ready, k + 3)
                    act.wait_ge(y_done, k + 1)
                    act.activation(hh[:, h, :], hf[:, h, :], ACT.Copy).then_inc(hh_ready, 1)
            act.activation(wh[:, 1, DN:DN + D], core.xn[:, 0, 0:D], ACT.Copy, scale=0.0).then_inc(zeroed, 1)
            act.activation(hh[:, 1, :], core.xn[:, 0, 0:HALF], ACT.Copy, scale=0.0).then_inc(zeroed, 1)
            act.wait_ge(zeroed, 4)
            chunks(act, rows)

        @block.vector
        def _(dve):
            dve.sem_inc(h_ready, 2)
            dve.sem_inc(t_ready, 2)
            dve.tensor_scalar(wl[:, 1, DN:DN + D], core.xn[:, 0, 0:D], 0.0, None, ALU.mult).then_inc(zeroed, 1)
            dve.tensor_scalar(hl[:, 1, :], core.xn[:, 0, 0:HALF], 0.0, None, ALU.mult).then_inc(zeroed, 1)
            dve.wait_ge(zeroed, 4)
            dve.sem_inc(hl_ready, 1)

            def rows(c, i, slot):
                for h in range(NH):
                    k = c * 2 + h
                    gate, up = core.bank[4 + 2 * h], core.bank[5 + 2 * h]
                    dve.wait_ge(u_ready, k + 1)
                    dve.wait_ge(silu_ready, k + 1)
                    if routed:
                        dve.wait_ge(h_ready, k + 1)
                        dve.scalar_tensor_tensor(tf[:, h, :], up[:, :], bias[:, slot, 1:2], sg[:, h, :], ALU.add,
                                                 ALU.mult).then_inc(t_ready, 1)
                        dve.wait_ge(t_ready, k + 3)
                        dve.wait_ge(cwb_ready, k + 1)
                        dve.wait_ge(y_done, k + 1)
                        dve.tensor_tensor(hf[:, h, :], tf[:, h, :], gate[:, :], ALU.mult).then_inc(h_ready, 1)
                    else:
                        dve.wait_ge(y_done, k + 1)
                        dve.scalar_tensor_tensor(hf[:, h, :], up[:, :], bias[:, slot, 1:2], sg[:, h, :], ALU.add,
                                                 ALU.mult).then_inc(h_ready, 1)
                        dve.sem_inc(t_ready, 1)
                    dve.wait_ge(hh_ready, k + 1)
                    dve.tensor_tensor(hl[:, h, :], hf[:, h, :], hh[:, h, :].bitcast(F32),
                                      ALU.subtract).then_inc(hl_ready, 1)
            chunks(dve, rows)
            dve.wait_ge(y_done, last + 2)
            for m in range(DC):
                for h in range(NH):
                    dve.tensor_tensor(core.x[:, m, half(h)], core.x[:, m, half(h)], acc[m][h][:, :],
                                      ALU.add).then_inc(x_added, 1)


def top_mask(dve, link, mask, work, top, values, n, k, tiles):
    link(*[dve.max(top[:, t, :], work[:, t, 0:max(n, 8)]) for t in range(tiles)])
    if k < 8:
        link(dve.memset(top[:, :, k:8], -BIG))
    link(*[dve.match_replace(work[:, t, :], top[:, t, :], work[:, t, :], BIG) for t in range(tiles)])
    link(dve.tensor_scalar(mask, work[:, :, 0:n], 2.9e38, None, ALU.is_ge))


def router(nc, core, name, kind, E, top_k, gate_w, bias_row, cw_parts, cw_f32=None, b2=None, b2_dram=None):
    with ExitStack() as ctx:
        sem = lambda n: nc.alloc_semaphore(f"{name}_{n}")
        sb = lambda n, shape, dt=F32: ctx.enter_context(nc.sbuf_tensor(f"{name}_{n}", shape, dt))
        w_loaded, b_loaded, b2_loaded = sem("w"), sem("b"), sem("b2")
        logits_ready, shifted, exp_ready, cw_ready, cwt_ready, chain, made, copied = map(
            sem, ("lg", "sh", "ex", "cw", "cwt", "chain", "made", "copied"))
        gw = sb("gw", [P, DC, E])
        br = sb("br", [P, E])
        lg = sb("lg_s", [P, TB, E])
        pr = sb("pr", [P, TB, E])
        work = sb("work", [P, TB, E + 8])
        mask = sb("mask", [P, TB, E])
        col = sb("col", [P, TB])
        top = sb("top", [P, TB, 8])
        part_b = sb("part_b", [P, TB, E], BF16)
        parts = sb("parts", [P, TB, P])
        N_G = 4
        gs = sb("gs", [P, 4, TB, N_G])
        gwork = sb("gwork", [P, TB, 16])
        gmask = sb("gmask", [P, TB, N_G])
        block = ctx.enter_context(nc.Block())
        wide = lambda c: c.unsqueeze(2).to_broadcast([P, TB, E])
        logits = core.bank[0][:, 0:TB * E].rearrange("p (t e) -> p t e", e=E)

        @block.sync
        def _(sp):
            sp.dma_start(gw[:, :, :], gate_w).then_inc(w_loaded, 16)
            if bias_row is not None:
                sp.dma_start(br[:, :], bias_row.partition_broadcast(P)).then_inc(b_loaded, 16)
            if b2 is not None:
                sp.dma_start(b2[:, :], b2_dram).then_inc(b2_loaded, 16)
                sp.wait_ge(b2_loaded, 16)

        @block.gpsimd
        def _(pool):
            pool.memset(parts[:, :, :], 0.0).then_inc(made, 1)
            pool.wait_ge(made, 1)
            pool.memset(parts[:, :, 96:97], 1.0).then_inc(made, 1)

        @block.tensor
        def _(pe):
            pe.wait_ge(w_loaded, 16)
            for t in range(TB):
                for c in range(DC):
                    mm = pe.matmul(logits[:, t, :], core.xn[:, c, t * P:(t + 1) * P], gw[:, c, :],
                                   start=c == 0, stop=c == DC - 1)
            mm.then_inc(logits_ready, 1)
            pe.wait_ge(cw_ready, 1)
            for t in range(TB):
                mm = pe.transpose(core.bank[2 + t // 4][:, (t % 4) * P:(t % 4 + 1) * P], parts[:, t, :],
                                  core.ident[:, :])
                if t % 4 == 3:
                    mm.then_inc(cwt_ready, 1)

        @block.scalar
        def _(act):
            if kind == "groups":
                act.wait_ge(logits_ready, 1)
                act.activation(pr[:, :, :], logits, ACT.Sigmoid).then_inc(exp_ready, 1)
            else:
                act.wait_ge(shifted, 1)
                act.activation(pr[:, :, :], lg[:, :, :], ACT.Exp).then_inc(exp_ready, 1)
            if cw_f32 is not None:
                for h in range(NH):
                    act.wait_ge(copied, h + 1)
                    act.activation(cw_f32[:, half(h)], core.bank[2 + h][:, :], ACT.Copy).then_inc(made, 1)

        @block.vector
        def _(dve):
            n = [0]

            def link(*steps):
                for ins in steps:
                    ins.then_inc(chain, 1)
                n[0] += len(steps)
                dve.wait_ge(chain, n[0])

            if kind != "groups":
                dve.wait_ge(logits_ready, 1)
                link(dve.tensor_reduce(col[:, :], logits, AX.X, ALU.max))
                dve.tensor_tensor(lg[:, :, :], logits, wide(col[:, :]), ALU.subtract).then_inc(shifted, 1)
            dve.wait_ge(exp_ready, 1)
            if kind != "groups":
                link(dve.tensor_reduce(col[:, :], pr[:, :, :], AX.X, ALU.add))
                link(dve.reciprocal(col[:, :], col[:, :]))
                link(dve.tensor_tensor(pr[:, :, :], pr[:, :, :], wide(col[:, :]), ALU.mult))
            link(dve.memset(work[:, :, E:E + 8], -BIG))
            if bias_row is not None:
                dve.wait_ge(b_loaded, 16)
                link(dve.tensor_tensor(work[:, :, 0:E], pr[:, :, :], br[:, :].unsqueeze(1).to_broadcast([P, TB, E]),
                                       ALU.add))
            else:
                link(dve.tensor_copy(work[:, :, 0:E], pr[:, :, :]))
            if kind == "groups":
                v = work[:, :, 0:E].rearrange("p t (g j) -> p t g j", j=E // N_G)
                big, small, big2, small2 = (gs[:, j, :, :] for j in range(4))
                link(dve.tensor_tensor(big, v[:, :, :, 0], v[:, :, :, 1], ALU.max))
                link(dve.tensor_tensor(small, v[:, :, :, 0], v[:, :, :, 1], ALU.min))
                link(dve.tensor_tensor(big2, v[:, :, :, 2], v[:, :, :, 3], ALU.max))
                link(dve.tensor_tensor(small2, v[:, :, :, 2], v[:, :, :, 3], ALU.min))
                link(dve.tensor_tensor(small, small, small2, ALU.max))
                link(dve.tensor_tensor(small2, big, big2, ALU.min))
                link(dve.tensor_tensor(small, small, small2, ALU.max))
                link(dve.tensor_tensor(big, big, big2, ALU.max))
                link(dve.memset(gwork[:, :, :], -BIG))
                link(dve.tensor_tensor(gwork[:, :, 0:N_G], big, small, ALU.add))
                top_mask(dve, link, gmask[:, :, :], gwork, top, None, N_G, 2, TB)
                gm = gmask[:, :, :].unsqueeze(3).to_broadcast([P, TB, N_G, E // N_G])
                m4 = mask[:, :, :].rearrange("p t (g j) -> p t g j", j=E // N_G)
                link(dve.tensor_scalar(gmask[:, :, :], gmask[:, :, :], -1.0, 1.0e30, ALU.add, ALU.mult))
                link(dve.tensor_copy(m4, gm))
                link(dve.tensor_tensor(work[:, :, 0:E], work[:, :, 0:E], mask[:, :, :], ALU.add))
            top_mask(dve, link, mask[:, :, :], work, top, None, E, top_k, TB)
            link(dve.tensor_tensor(pr[:, :, :], pr[:, :, :], mask[:, :, :], ALU.mult))
            if kind != "softmax_bias":
                link(dve.tensor_reduce(col[:, :], pr[:, :, :], AX.X, ALU.add))
                if kind == "groups":
                    link(dve.tensor_scalar(col[:, :], col[:, :], 1e-20, None, ALU.add))
                link(dve.reciprocal(col[:, :], col[:, :]))
                if kind == "groups":
                    link(dve.tensor_scalar(col[:, :], col[:, :], 2.5, None, ALU.mult))
                link(dve.tensor_tensor(pr[:, :, :], pr[:, :, :], wide(col[:, :]), ALU.mult))
            dve.wait_ge(made, 2)
            for j in range(3):
                part = parts[:, :, 32 * j:32 * j + E]
                link(dve.tensor_copy(part_b[:, :, :], pr[:, :, :]))
                ins = dve.tensor_copy(part, part_b[:, :, :])
                if j < 2:
                    link(ins)
                    link(dve.tensor_tensor(pr[:, :, :], pr[:, :, :], part, ALU.subtract))
                else:
                    ins.then_inc(cw_ready, 1)
            for h in range(NH):
                dve.wait_ge(cwt_ready, h + 1)
                dve.tensor_copy(cw_parts[:, half(h)], core.bank[2 + h][:, :]).then_inc(copied, 1)


def load_split(block_engines, raw, wh, wl, srcs, in_sems, hi_sem, lo_sem, lo_engine):
    sp, act, low = block_engines
    if sp is not None:
        for j, (cols, src) in enumerate(srcs):
            sp.dma_start(raw[:, :, cols], src).then_inc(in_sems[j], 16)
    if act is not None:
        for j, (cols, src) in enumerate(srcs):
            act.wait_ge(in_sems[j], 16)
            act.activation(wh[:, :, cols], raw[:, :, cols], ACT.Copy).then_inc(hi_sem, 1)
    if low is not None:
        for j, (cols, src) in enumerate(srcs):
            low.wait_ge(hi_sem, j + 1)
            low.tensor_tensor(wl[:, :, cols], raw[:, :, cols], wh[:, :, cols].bitcast(F32),
                              ALU.subtract).then_inc(lo_sem, 1)


def gemm3(pe, out, wh, wl, xh, xl, first=True, last=True):
    n, total = 0, 3 * len(wh)
    for k in range(len(wh)):
        for w, x in ((wh[k], xh[k]), (wl[k], xh[k]), (wh[k], xl[k])):
            mm = pe.matmul(out, w, x, start=first and n == 0, stop=last and n == total - 1)
            n += 1
    return mm


def decay_attention(nc, core, w_dram, cols_dram):
    with ExitStack() as outer:
        sbo = lambda n, shape, dt=F32: outer.enter_context(nc.sbuf_tensor(f"l3a_{n}", shape, dt))
        wh = sbo("wh", [P, DC, 4 * D], F32R)
        wl = sbo("wl", [P, DC, 4 * D], F32R)
        cols = sbo("cols", [P, 3, DC])
        lam = sbo("lam", [P, DC])
        y = sbo("y", [P, DC, T])
        gate = sbo("gate", [P, DC, T])
        V, Q, G, O = (j * D for j in range(4))
        with ExitStack() as ctx:
            sem = lambda n: nc.alloc_semaphore(f"l3a_{n}")
            raw = ctx.enter_context(nc.sbuf_tensor("l3a_raw", [P, DC, 4 * D], F32))
            states = ctx.enter_context(nc.sbuf_tensor("l3a_states", [P, DC, T], F32))
            w_in = [sem(f"w_in{j}") for j in range(4)]
            hi, lo, cols_in, lam_ready, v_ready, q_ready, g_ready = map(
                sem, ("hi", "lo", "cols", "lam", "v", "q", "g"))
            state_ready, y_ready, gate_ready = sem("st"), sem("yr"), sem("gr")
            srcs = [(slice(j * D, (j + 1) * D), w_dram[:, :, j * D:(j + 1) * D]) for j in range(4)]
            block = ctx.enter_context(nc.Block())

            @block.sync
            def _(sp):
                load_split((sp, None, None), raw, wh, wl, srcs, w_in, hi, lo, None)
                sp.dma_start(cols[:, :, :], cols_dram).then_inc(cols_in, 16)

            @block.scalar
            def _(act):
                load_split((None, act, None), raw, wh, wl, srcs, w_in, hi, lo, None)
                act.wait_ge(cols_in, 16)
                act.activation(lam[:, :], cols[:, 0, :], ACT.Sigmoid).then_inc(lam_ready, 1)
                for n in range(DC * NH):
                    m, h = n // NH, n % NH
                    act.wait_ge(g_ready, n + 1)
                    act.activation(gate[:, m, half(h)], core.bank[4 + n][:, :], ACT.Silu).then_inc(gate_ready, 1)

            @block.gpsimd
            def _(pool):
                load_split((None, None, pool), raw, wh, wl, srcs, w_in, hi, lo, None)

            @block.tensor
            def _(pe):
                def project(part, banks, ready):
                    for n in range(DC * NH):
                        m, h = n // NH, n % NH
                        w = slice(part + m * P, part + (m + 1) * P)
                        gemm3(pe, core.bank[banks(n)][:, :], [wh[:, k, w] for k in range(DC)],
                              [wl[:, k, w] for k in range(DC)], [core.xh[:, k, half(h)] for k in range(DC)],
                              [core.xl[:, k, half(h)] for k in range(DC)]).then_inc(ready, 1)
                pe.wait_ge(lo, 1)
                project(V, lambda n: n, v_ready)
                pe.wait_ge(lo, 2)
                project(Q, lambda n: 4 + n, q_ready)
                pe.wait_ge(lo, 3)
                pe.wait_ge(y_ready, DC * NH)
                project(G, lambda n: 4 + n, g_ready)

            @block.vector
            def _(dve):
                dve.wait_ge(lam_ready, 1)
                for n in range(DC * NH):
                    m, h = n // NH, n % NH
                    dve.wait_ge(v_ready, n + 1)
                    if h:
                        dve.wait_ge(state_ready, n)
                    dve.tensor_tensor_scan(states[:, m, half(h)], lam[:, m:m + 1].to_broadcast([P, HALF]),
                                           core.bank[n][:, :],
                                           states[:, m, HALF - 1:HALF] if h else 0.0,
                                           ALU.mult, ALU.add).then_inc(state_ready, 1)
                for n in range(DC * NH):
                    m, h = n // NH, n % NH
                    dve.wait_ge(q_ready, n + 1)
                    dve.wait_ge(state_ready, n + 1)
                    dve.tensor_tensor(y[:, m, half(h)], core.bank[4 + n][:, :], states[:, m, half(h)],
                                      ALU.mult).then_inc(y_ready, 1)

        norm(nc, core, "l3a_ln", y, True, core.eps5, dst=y, gain=cols[:, 1, :], shift=cols[:, 2, :], split=False)

        with ExitStack() as ctx:
            sem = lambda n: nc.alloc_semaphore(f"l3o_{n}")
            yg, yh, yl, out_ready, added = map(sem, ("yg", "yh", "yl", "out", "add"))
            block = ctx.enter_context(nc.Block())

            @block.vector
            def _(dve):
                for h in range(NH):
                    for c in range(DC):
                        dve.tensor_tensor(y[:, c, half(h)], y[:, c, half(h)], gate[:, c, half(h)],
                                          ALU.mult).then_inc(yg, 1)
                    for c in range(DC):
                        dve.wait_ge(yh, DC * h + c + 1)
                        dve.tensor_tensor(core.xl[:, c, half(h)], y[:, c, half(h)], core.xh[:, c, half(h)].bitcast(F32),
                                          ALU.subtract).then_inc(yl, 1)
                add_banks(dve, core, out_ready, added)

            @block.scalar
            def _(act):
                for h in range(NH):
                    for c in range(DC):
                        act.wait_ge(yg, DC * h + c + 1)
                        act.activation(core.xh[:, c, half(h)], y[:, c, half(h)], ACT.Copy).then_inc(yh, 1)

            @block.tensor
            def _(pe):
                for h in range(NH):
                    pe.wait_ge(yl, DC * (h + 1))
                    for m in range(DC):
                        w = slice(O + m * P, O + (m + 1) * P)
                        gemm3(pe, core.bank[DC * h + m][:, :], [wh[:, k, w] for k in range(DC)],
                              [wl[:, k, w] for k in range(DC)], [core.xh[:, k, half(h)] for k in range(DC)],
                              [core.xl[:, k, half(h)] for k in range(DC)]).then_inc(out_ready, 1)


def add_banks(dve, core, ready, added):
    for h in range(NH):
        for m in range(DC):
            dve.wait_ge(ready, DC * h + m + 1)
            dve.tensor_tensor(core.x[:, m, half(h)], core.x[:, m, half(h)], core.bank[DC * h + m][:, :],
                              ALU.add).then_inc(added, 1)


def project(nc, core, name, n_chunks, w_dram, tables, out, bias, v_w, v_bias, v_out, v_heads, v_dim,
            fills=()):
    rope = tables is not None
    WC = DC * P
    NV = v_heads * v_dim
    with ExitStack() as ctx:
        sem = lambda n: nc.alloc_semaphore(f"{name}_{n}")
        sb = lambda n, shape, dt=F32: ctx.enter_context(nc.sbuf_tensor(f"{name}_{n}", shape, dt))
        SLOTS = 4
        w_in = [sem(f"w_in{j}") for j in range(SLOTS)]
        vw_in, tab_in, vb_in = sem("vw_in"), sem("tab_in"), sem("vb_in")
        w_hi = sem("w_hi")
        raw_free, w_split, v_split, ps_ready, swapped, turned, sin_done, out_done = map(
            sem, ("raw_free", "w_split", "v_split", "ps", "sw", "cos", "sin", "out"))
        v_ready, v_read, filled = sem("v_ready"), sem("v_read"), sem("filled")
        raw = sb("raw", [P, SLOTS, WC + 2])
        wh = sb("wh", [P, SLOTS, WC], F32R)
        wl = sb("wl", [P, SLOTS, WC], F32R)
        bcol = sb("bcol", [P, SLOTS, 2])
        vraw = sb("vraw", [P, DC, NV])
        vh = sb("vh", [P, DC, NV], F32R)
        vl = sb("vl", [P, DC, NV], F32R)
        if rope:
            tab = sb("tab", [P, 2, T])
            swap = sb("swap", [P, 2, HALF])
            t1 = sb("t1", [P, 2, HALF])
            t2 = sb("t2", [P, 2, HALF])
        if v_bias is not None:
            vb = sb("vb", [P, NV])
        block = ctx.enter_context(nc.Block())
        ROUNDS = n_chunks // SLOTS

        def chunks(eng, body):
            with eng.Fori(0, ROUNDS) as i:
                for slot in range(SLOTS):
                    body(i * SLOTS + slot, i, slot)

        def with_splits_ahead(eng, split, body):
            split(0, 0, 0)
            split(1, 0, 1)
            if ROUNDS > 1:
                with eng.Fori(0, ROUNDS - 1) as i:
                    for slot in range(SLOTS):
                        ahead = slot + 2
                        split(i * SLOTS + ahead, i + ahead // SLOTS, ahead % SLOTS)
                        body(i * SLOTS + slot, i, slot)
            for c in range(n_chunks - SLOTS, n_chunks):
                if c + 2 < n_chunks:
                    split(c + 2, ROUNDS - 1, (c + 2) % SLOTS)
                body(c, ROUNDS - 1, c % SLOTS)

        def split_low(eng, c, i, slot):
            eng.wait_ge(ps_ready, c * 2 + 2)
            eng.wait_ge(out_done, c * 2 + 2)
            eng.wait_ge(w_in[slot], i * 16 + 16)
            eng.tensor_copy(bcol[:, slot, :], raw[:, slot, WC:WC + 2]).then_inc(w_split, 1)
            eng.wait_ge(w_hi, c + 1)
            eng.tensor_tensor(wl[:, slot, :], raw[:, slot, 0:WC], wh[:, slot, :].bitcast(F32),
                              ALU.subtract).then_inc(w_split, 1)
            eng.wait_ge(w_split, c * 2 + 2)
            eng.sem_inc(raw_free, 1)

        @block.sync
        def _(sp):
            def load(c, i, slot):
                sp.wait_ge(raw_free, c + 1)
                sp.dma_start(raw[:, slot, :], w_dram[c]).then_inc(w_in[slot], 16)
            chunks(sp, load)

        @block.gpsimd
        def _(pool):
            pool.sem_inc(raw_free, SLOTS)
            pool.sem_inc(sin_done, 2)

            def times_sin(c, i, slot):
                for h in range(NH):
                    k = c * 2 + h
                    pool.wait_ge(out_done, k + 7)
                    pool.wait_ge(swapped, k * 2 + 2)
                    pool.tensor_tensor(t2[:, h, :], swap[:, h, :], tab[:, 1, half(h)],
                                       ALU.mult).then_inc(sin_done, 1)

            def split(c, i, slot):
                pool.wait_ge(ps_ready, c * 2 + 2)
                pool.wait_ge(w_in[slot], i * 16 + 16)
                core.pool_copy(pool, wh[:, slot, :], raw[:, slot, 0:WC]).then_inc(w_hi, 1)
                split_low(pool, c, i, slot)

            if rope:
                pool.wait_ge(tab_in, 16)
                chunks(pool, times_sin)
            else:
                chunks(pool, split)

        @block.tensor
        def _(pe):
            pe.sem_inc(ps_ready, 2 * SLOTS)

            def product(c, i, slot):
                pe.wait_ge(w_split, c * 2 + 2)
                for h in range(NH):
                    k = c * 2 + h
                    pe.wait_ge(out_done, k + 1)
                    gemm3(pe, core.bank[2 * slot + h][:, :], [wh[:, slot, j * P:(j + 1) * P] for j in range(DC)],
                          [wl[:, slot, j * P:(j + 1) * P] for j in range(DC)],
                          [core.xh[:, j, half(h)] for j in range(DC)],
                          [core.xl[:, j, half(h)] for j in range(DC)]).then_inc(ps_ready, 1)
            chunks(pe, product)
            pe.wait_ge(v_split, 2)
            pe.wait_ge(out_done, 2 * n_chunks + 4)
            for t in range(TB):
                tok = slice(t * P, (t + 1) * P)
                if t >= 4:
                    pe.wait_ge(v_read, t - 3)
                gemm3(pe, core.bank[t % 4][:, 0:NV], [core.xh[:, j, tok] for j in range(DC)],
                      [core.xl[:, j, tok] for j in range(DC)], [vh[:, j, :] for j in range(DC)],
                      [vl[:, j, :] for j in range(DC)]).then_inc(v_ready, 1)

        @block.scalar
        def _(act):
            def evacuate(c, i, slot):
                act.wait_ge(w_split, c * 2 + 2)
                for h in range(NH):
                    k = c * 2 + h
                    act.wait_ge(ps_ready, k + 9)
                    bank = core.bank[2 * slot + h]
                    if rope:
                        act.wait_ge(sin_done, k + 1)
                        act.activation(swap[0:64, h, :], bank[64:128, :], ACT.Identity,
                                       bias=bcol[0:64, slot, 1:2]).then_inc(swapped, 1)
                        act.activation(swap[64:128, h, :], bank[0:64, :], ACT.Identity,
                                       bias=bcol[64:128, slot, 1:2]).then_inc(swapped, 1)
                    else:
                        act.activation(out[:, c, half(h)], bank[:, :], ACT.Identity,
                                       bias=bcol[:, slot, 0:1]).then_inc(out_done, 1)
            def split_high(c, i, slot):
                act.wait_ge(ps_ready, c * 2 + 2)
                act.wait_ge(w_in[slot], i * 16 + 16)
                act.activation(wh[:, slot, :], raw[:, slot, 0:WC], ACT.Copy).then_inc(w_hi, 1)

            act.dma_start(vraw[:, :, :], v_w).then_inc(vw_in, 16)
            if rope:
                act.dma_start(tab[:, :, :], tables).then_inc(tab_in, 16)
            if v_bias is not None:
                act.dma_start(vb[:, :], v_bias.partition_broadcast(P)).then_inc(vb_in, 16)
            if not rope:
                act.sem_inc(out_done, 8)
            for memory, value in fills[:1]:
                act.activation(memory, value, ACT.Copy).then_inc(filled, 1)
            act.wait_ge(vw_in, 16)
            act.activation(vh[:, :, :], vraw[:, :, :], ACT.Copy).then_inc(v_split, 1)
            if rope:
                with_splits_ahead(act, split_high, evacuate)
            else:
                chunks(act, evacuate)
            for memory, value in fills[1:]:
                act.activation(memory, value, ACT.Copy).then_inc(filled, 1)

        @block.vector
        def _(dve):
            dve.wait_ge(v_split, 1)
            dve.tensor_tensor(vl[:, :, :], vraw[:, :, :], vh[:, :, :].bitcast(F32), ALU.subtract).then_inc(v_split, 1)
            if rope:
                dve.sem_inc(out_done, 8)
                dve.wait_ge(tab_in, 16)

                def turn(c, i, slot):
                    dve.wait_ge(w_split, c * 2 + 2)
                    for h in range(NH):
                        k = c * 2 + h
                        dve.wait_ge(ps_ready, k + 9)
                        dve.wait_ge(swapped, k * 2 + 2)
                        dve.wait_ge(out_done, k + 7)
                        dve.scalar_tensor_tensor(t1[:, h, :], core.bank[2 * slot + h][:, :], bcol[:, slot, 0:1],
                                                 tab[:, 0, half(h)], ALU.add, ALU.mult).then_inc(turned, 1)
                    for h in range(NH):
                        k = c * 2 + h
                        dve.wait_ge(turned, k + 1)
                        dve.wait_ge(sin_done, k + 3)
                        dve.tensor_tensor(out[:, c, half(h)], t1[:, h, :], t2[:, h, :], ALU.add).then_inc(out_done, 1)
                with_splits_ahead(dve, lambda c, i, slot: split_low(dve, c, i, slot), turn)
            if v_bias is not None:
                dve.wait_ge(vb_in, 16)
            for t in range(TB):
                dve.wait_ge(v_ready, t + 1)
                ps = core.bank[t % 4][:, 0:NV].rearrange("p (h d) -> p h d", d=v_dim)
                if v_bias is None:
                    dve.tensor_copy(v_out[:, t, :, 0:v_dim], ps).then_inc(v_read, 1)
                else:
                    dve.tensor_tensor(v_out[:, t, :, 0:v_dim], ps, vb[:, :].rearrange("p (h d) -> p h d", d=v_dim),
                                      ALU.add).then_inc(v_read, 1)


def attend_plan(per, n_batches, tiles, segs, window, tail, nxt):
    n_s, n_a = len(tiles), len(segs)
    slots = n_s * per
    prep0, prep_step, a_from, a_to = (0, 2, 2, slots - 6) if window else (1, 7, 8, slots - 4)
    plan = []
    late = []
    for b in range(n_batches):
        more = b + 1 < n_batches or nxt
        queue = [("A", b + 1, a, i) for a in range(per) for i in range(n_a)] if more else []
        done = 0
        due = {}
        at = lambda slot, ev: due.setdefault(slot, []).append(ev)
        if b:
            at(per, ("OU", b - 1, 1))
            at(per + 2, ("DEN", b - 1))
            at(per + 6, ("R", b - 1, 0))
            at(per + 8, ("R", b - 1, 1))
        half0 = sum(h == 0 for h, _ in tiles)
        at((half0 + 1) * per, ("OU", b, 0))
        if window and b == n_batches - 2 and nxt:
            at(2, ("KP", 0))
            at(14, ("KP", 1))
        if more:
            for a in range(per):
                at(prep0 + prep_step * a, ("Q", b + 1, a))
        for n in range(slots):
            i, a = n // per, n % per
            plan.append(("S", b, i, a))
            if n >= a_from and more:
                want = min(len(queue), -(-len(queue) * (n - a_from + 1) // (a_to - a_from)))
                while done < want:
                    plan.append(queue[done])
                    if queue[done][3] == n_a - 1:
                        plan.append(("X", b + 1, queue[done][2]))
                        at(n + 3, ("M", b + 1, queue[done][2]))
                    done += 1
            if a == per - 1:
                plan += late
                late = [("V", b, i, x) for x in range(per)]
            plan += due.pop(n, [])
        assert not due and done == len(queue)
    if nxt:
        plan.append(("KC",))
    plan += late
    if nxt:
        plan.append(("VC",))
    b = n_batches - 1
    plan += [("OU", b, 1), ("DEN", b), ("R", b, 0), ("R", b, 1)]
    return plan


def attend(nc, core, name, qk, n_q, k_dram, v, on, scale, causal, groups, spread_dram, masks_dram, sink=None, staging=None):
    HEADS = 8
    per = 4 if causal else 2
    NB = HEADS // per
    vw = P // per
    R0 = 96 if causal else 64
    tiles = [(h, kb) for h in range(NH) for kb in range(TB) if not causal or kb * P < (h + 1) * HALF]
    segs = [(qb, s) for qb in range(TB) for s in range(NH) if not causal or s * HALF < (qb + 1) * P]
    NS, NA = len(tiles), len(segs)
    SL = NS * per
    GT = SL * NB
    NP = 12
    first = [("A", 0, a, i) for a in range(per) for i in range(NA)]
    start = ([] if causal else [("KP", 0), ("KP", 1)]) + [("VC",), ("Q", 0, 0)]
    for a in range(per):
        start += first[a * NA:a * NA + NA // 2]
        if a + 1 < per:
            start.append(("Q", 0, a + 1))
        start += first[a * NA + NA // 2:(a + 1) * NA] + [("X", 0, a), ("M", 0, a)]
    start.append(("KC",))
    plan = attend_plan(per, NB, tiles, segs, not causal, None, True)
    last_plan = attend_plan(per, NB, tiles, segs, not causal, None, False)

    RING = (0, 1, 6, 7)
    def ring_uses(events):
        order = [ev for ev in events if ev[0] in ("A", "M", "DEN", "R")]
        return {ev: u for u, ev in enumerate(order)}, -(-len(order) // len(RING)) * len(RING)
    start_ring, U0 = ring_uses(start)
    ring, NU = ring_uses(plan)
    last_ring, NL = ring_uses(last_plan)

    with ExitStack() as ctx:
        credit = {}

        def sem(n, start_at=0):
            s = nc.alloc_semaphore(f"{name}_{n}")
            credit[s.name] = start_at
            return s

        def wait(eng, s, count):
            eng.wait_ge(s, count + credit[s.name])

        def give(eng, *sems):
            for s in sems:
                if credit[s.name]:
                    eng.sem_inc(s, credit[s.name])

        sb = lambda n, shape, dt=F32: ctx.enter_context(nc.sbuf_tensor(f"{name}_{n}", shape, dt))
        c_in, prep, mseg_set = sem("c_in"), sem("prep"), sem("mseg_set")
        q_in = [sem(f"q_in{a}") for a in range(per)]
        kn_in = sem("kn_in")
        q_hi, k_hi, parts = sem("q_hi", 0), sem("k_hi", 0), sem("parts", 0)
        kn_steps, kc, v_copied = sem("kn_steps"), sem("kc"), sem("v_copied")
        a_ready, a_read = sem("a_ready"), sem("a_read", len(RING))
        m_steps, m_rows, m_copied = sem("m_steps"), sem("m_rows", per if causal else 0), sem("m_copied")
        s_ready, p_ready, av_done = sem("s_ready", 1), sem("p_ready", 2), sem("av_done", NP)
        ou_done, on_done, r_steps = sem("ou_done", 2), sem("on_done", 2), sem("r_steps", 3)
        sum_done, den_done, sinks = sem("sum_done", NP), sem("den_done", 1), sem("sinks", per)
        MW = P if causal else 2 * P
        spread = sb("spread", [P, TB])
        mk = sb("mk", [P, 2, MW], BF16)
        qa1 = sb("qa1", [P, per, T], F32R) if causal else core.xl
        QA = lambda par, a: qa1[:, a, :] if par else (core.xh if a < 2 else core.xl)[:, a % 2, :]
        mseg = sb("mseg", [P, per, TB, NH])
        mrow = sb("mrow", [P, per, TB])
        negm = sb("negm", [P, per, P - R0], F32R)
        prob = sb("prob", [P, NP, HALF])
        den = sb("den", [P, TB, per])
        if causal:
            mk_raw = sb("mk_raw", [P, 2, MW])
            vs = sb("vs", [P, TB, HEADS * vw])
            ks = sb("ks", [P, 2, per, T], F32R)
            st_q, st_k = staging[:, 0, :, :], staging[:, 1, :, :]
            ou = sb("ou", [P, T])
            rx = sb("rx", [P, TB, per, vw])
            m_row = sb("m_row", [P, per, P])
            pick = sb("pick", [P, per])
        else:
            st_q = sb("st_q", [P, 2, T])
            ql = sb("ql", [P, 2, 2, T], F32R)
            kn = sb("kn", [P, 2, T], F32R)
            k2 = sb("k2", [P, 2, T], F32R)
            k1 = sb("k1", [P, 2, T], F32R)
            st_k = qk[:, n_q + 3, :]
            vs = core.xn[:, 0, :].rearrange("p (t a) -> p t a", t=TB)
            rx = core.xn[:, 1, :].rearrange("p (t a d) -> p t a d", t=TB, a=per)
            acc = qk[:, n_q:n_q + 2, :]
            ou = qk[:, n_q + 2, :]
            mk_raw = qk[:, n_q, 0:2 * MW].rearrange("p (u m) -> p u m", u=2)
            sk = sb("sk", [P, groups * HEADS])
            sk8 = sb("sk8", [P, groups * HEADS])
            esink = sb("esink", [P, 2, per, TB])
            one_col = sb("one_col", [P, 1])
        block = ctx.enter_context(nc.Block())

        def cols(i):
            h, kb = tiles[i]
            q0 = max(kb * P, h * HALF) if causal else h * HALF
            return h, kb, q0, q0 - h * HALF, (h + 1) * HALF - q0

        def spread_rows(eng, dst, rows):
            return eng.tensor_tensor(dst[R0:P].rearrange("p (t q) -> p t q", q=P),
                                     rows[R0:P].unsqueeze(1).to_broadcast([P - R0, TB, P]),
                                     spread[R0:P, :].unsqueeze(2).to_broadcast([P - R0, TB, P]),
                                     ALU.mult).then_inc(m_rows, 1)

        def unused(uses):
            return -len(uses) % len(RING)

        def groups_of(eng, body):
            body(None, start, start_ring, 0, True)
            with eng.Fori(0, groups - 1) as g:
                body(g, plan, ring, g * NU + U0, True)
            body(groups - 1, last_plan, last_ring, (groups - 1) * NU + U0, False)

        def batch_no(g, b):
            return b if g is None else g * NB + b

        def next_group(g):
            return 0 if g is None else g + 1

        @block.sync
        def _(sp):
            def constants():
                sp.dma_start(spread[:, :], spread_dram).then_inc(c_in, 16)
                sp.dma_start(mk_raw[:, :, :], masks_dram[:, :, 0:MW]).then_inc(c_in, 16)
                if causal:
                    sp.dma_start(pick[:, :], masks_dram[:, 0, MW:MW + per]).then_inc(c_in, 16)
                else:
                    sp.dma_start(sk[:, :], sink.partition_broadcast(P)).then_inc(c_in, 16)

            def stage(g, b):
                n = batch_no(g, b)
                gq = next_group(g) if b in (0, NB) else g
                for a in range(per):
                    if causal:
                        if g is not None:
                            wait(sp, parts, n * (2 * per) + (2 * a + 2 - 2 * per))
                        j = (b % NB) * per + a
                        for st, c in ((st_q, gq), (st_k, gq + n_q)):
                            src = qk[:, bass.ds(c, 1), :] if not isinstance(c, int) else qk[:, c:c + 1, :]
                            for slot in range(3):
                                for u in range(2):
                                    r = 32 * slot + 8 * u
                                    sp.dma_start(st[r:r + 8, a:a + 1, :],
                                                 src[64 * u + 8 * j:64 * u + 8 * j + 8]).then_inc(q_in[a], 16)
                    else:
                        if g is not None:
                            sp.wait_ge(parts, n * per + (a + 1 - per))
                        c = gq * NB + b % NB
                        src = qk[:, bass.ds(c, 1), :] if not isinstance(c, int) else qk[:, c:c + 1, :]
                        for r in range(4):
                            r0 = 64 * (r % 2) + 32 * a
                            sp.dma_start(st_q[32 * r:32 * r + 32, a:a + 1, :],
                                         src[r0:r0 + 32]).then_inc(q_in[a], 16)

            def next_keys(g, a):
                G = next_group(g)
                if a:
                    sp.wait_ge(kn_steps, G * 4 + 2)
                elif g is not None:
                    sp.wait_ge(kc, g * 2 + 2)
                for r in range(4):
                    r0 = 64 * (r % 2) + 32 * a
                    sp.dma_start(st_k[32 * r:32 * r + 32], k_dram[G, r0:r0 + 32, :]).then_inc(kn_in, 16)

            def body(g, events, uses, u0, nxt):
                if g is None:
                    constants()
                    if not causal:
                        next_keys(g, 0)
                    stage(g, 0)
                    if not causal:
                        next_keys(g, 1)
                    return
                for b in range(NB):
                    if b + 1 < NB or nxt:
                        stage(g, b + 1)
                    if b in (0, NB - 2) and nxt and not causal:
                        next_keys(g, 0 if b == 0 else 1)
            groups_of(sp, body)

        @block.gpsimd
        def _(pool):
            pool.wait_ge(c_in, 48)
            pool.tensor_scalar(mk[:, :, :], mk_raw[:, :, :], 1.0, None, ALU.mult).then_inc(prep, 1)
            pool.memset(negm[:, :, :].bitcast(F32), 0.0).then_inc(prep, 1)
            if not causal:
                pool.tensor_scalar(sk8[:, :], sk[:, :], 1.0 / scale, None, ALU.mult).then_inc(prep, 1)
                pool.memset(one_col[:, :], 1.0).then_inc(prep, 1)
                pool.wait_ge(prep, 4)
                ones = core.ones_r[64:128, 0:1].bitcast(F32).unsqueeze(1).to_broadcast([64, 2, T])
                pool.tensor_tensor(k1[64:128, :, :], ones, ones, ALU.mult).then_inc(prep, 1)
            give(pool, sum_done, m_rows)

            def body(g, events, uses, u0, nxt):
                for ev in events:
                    if ev[0] == "Q" and causal:
                        b, a = ev[1:]
                        n = batch_no(g, b) * per + a
                        for rows, dst, st, hi in ((slice(64, 96), QA(b % 2, a), st_q, q_hi),
                                                  (slice(32, 64), ks[:, b % 2, a, :], st_k, k_hi)):
                            pool.wait_ge(hi, n + 1)
                            pool.tensor_tensor(dst[rows], st[rows, a, :], dst[rows].bitcast(F32),
                                               ALU.subtract).then_inc(parts, 1)
                    elif ev[0] == "M" and causal:
                        b, a = ev[1:]
                        pool.wait_ge(m_copied, batch_no(g, b) * per + (a + 1))
                        spread_rows(pool, QA(b % 2, a), m_row[:, a, :])
                    elif ev[0] == "S" and not causal:
                        b, i, a = ev[1:]
                        h, kb = tiles[i]
                        n = b * SL + i * per + a
                        v_ = g * GT + n
                        out = acc[:, a, half(h)]
                        if kb == 0:
                            continue
                        if kb == 1:
                            wait(pool, den_done, g * NB + b)
                            wait(pool, p_ready, v_ + 1)
                            pool.tensor_tensor(out, prob[:, (n - per) % NP, :], prob[:, n % NP, :],
                                               ALU.add).then_inc(sum_done, 3 if a else 1)
                        else:
                            wait(pool, sum_done, v_ - 1)
                            wait(pool, p_ready, v_ + 1)
                            pool.tensor_tensor(out, out, prob[:, n % NP, :], ALU.add).then_inc(sum_done, 1)
            groups_of(pool, body)

        @block.tensor
        def _(pe):
            pe.wait_ge(prep, 2 if causal else 5)
            give(pe, s_ready, av_done, den_done)

            def body(g, events, uses, u0, nxt):
                for ev in events:
                    kind = ev[0]
                    if ev in uses:
                        u = uses[ev]
                        u_ = u0 + u
                        ps = core.bank[RING[u % len(RING)]]
                        wait(pe, a_read, u_ + 1 - len(RING))
                    if kind == "A":
                        b, a, i = ev[1:]
                        qb, s = segs[i]
                        n = batch_no(g, b) * per + a
                        if i == 0:
                            if causal:
                                pe.wait_ge(parts, n * 2 + 2)
                            else:
                                pe.wait_ge(q_hi, n + 1)
                                if b in (0, NB):
                                    pe.wait_ge(kn_steps, next_group(g) * 4 + 4)
                        key = ks[:, b % 2, a, :] if causal else (kn if b in (0, NB) else k2)[:, a, :]
                        end = min((qb + 1) * P, (s + 1) * HALF) if causal else (s + 1) * HALF
                        m0 = qb * P if causal else (qb - 1) * P
                        lo, hi = max(m0, s * HALF), min((qb + 1) * P, end)
                        mm = pe.matmul(ps[:, 0:end - s * HALF], QA(b % 2, a)[:, qb * P:(qb + 1) * P],
                                       key[:, s * HALF:end], start=True, stop=lo >= hi)
                        if lo < hi:
                            mm = pe.matmul(ps[:, lo - s * HALF:hi - s * HALF], core.ident_b[:, :],
                                           mk[:, 1, lo - m0:hi - m0], start=False, stop=True)
                        mm.then_inc(a_ready, 1)
                    elif kind == "M":
                        b, a = ev[1:]
                        pe.wait_ge(m_steps, batch_no(g, b) * (2 * per) + (2 * a + 2))
                        pe.matmul(ps[R0:P, 0:P], negm[:, a, :].bitcast(F32), core.ident[:, :], start=True, stop=True,
                                  tile_position=(0, R0)).then_inc(a_ready, 1)
                    elif kind == "S":
                        b, i, a = ev[1:]
                        h, kb, q0, c0, w = cols(i)
                        n = b * SL + i * per + a
                        bank = core.bank[2 + n % 2]
                        keys = slice(kb * P, (kb + 1) * P)
                        if i == 0:
                            wait(pe, m_rows, batch_no(g, b) * per + (a + 1))
                            if not causal:
                                pe.wait_ge(parts, batch_no(g, b) * per + (a + 1))
                                if b == 0:
                                    pe.wait_ge(kc, g * 2 + 2)
                        wait(pe, p_ready, g * GT + (n - 1))
                        lo, hi = max(kb * P, q0), min(kb * P + MW, q0 + w)
                        qs = slice(q0, q0 + w)
                        if causal:
                            mm = pe.matmul(bank[:, c0:c0 + w], ks[:, b % 2, a, keys], QA(b % 2, a)[:, qs],
                                           start=True, stop=lo >= hi)
                        else:
                            pe.matmul(bank[:, c0:c0 + w], k2[:, a, keys], QA(b % 2, a)[:, qs], start=True, stop=False)
                            mm = pe.matmul(bank[:, c0:c0 + w], k1[:, a, keys], ql[:, b % 2, a, qs], start=False,
                                           stop=lo >= hi)
                        if lo < hi:
                            mm = pe.matmul(bank[:, lo - h * HALF:hi - h * HALF], core.ident_b[:, :],
                                           mk[:, 0, lo - kb * P:hi - kb * P], start=False, stop=True)
                        mm.then_inc(s_ready, 1)
                    elif kind == "V":
                        b, i, a = ev[1:]
                        h, kb, q0, c0, w = cols(i)
                        n = b * SL + i * per + a
                        if a == 0 and kb == 0:
                            if b == 0 and h == 0:
                                pe.wait_ge(v_copied, g + 1)
                            wait(pe, ou_done, g * (2 * NB) + (2 * b + h - 1))
                        wait(pe, p_ready, g * GT + (n + 1))
                        vcol = (b * per + a if causal else a) * vw
                        pe.matmul(core.bank[4 + h][vw * a:vw * a + vw, c0:c0 + w], vs[:, kb, vcol:vcol + vw],
                                  prob[:, n % NP, 0:w], start=kb == 0,
                                  stop=kb == (4 * h + 3 if causal else TB - 1), skip_group_check=True,
                                  tile_position=(0, vw * a)).then_inc(av_done, 1)
                    elif kind == "DEN":
                        b = ev[1]
                        if causal:
                            wait(pe, ou_done, g * (2 * NB) + (2 * b + 2))
                            for qb in range(TB):
                                mm = pe.matmul(ps[:, qb * per:(qb + 1) * per], ou[:, qb * P:(qb + 1) * P],
                                               pick[:, :], start=True, stop=True)
                        else:
                            wait(pe, sum_done, g * GT + (b + 1) * SL)
                            for qb in range(TB):
                                for a in range(per):
                                    mm = pe.matmul(ps[:, qb * per + a:qb * per + a + 1],
                                                   acc[:, a, qb * P:(qb + 1) * P], one_col[:, :], start=True,
                                                   stop=True)
                        mm.then_inc(a_ready, 1)
                        if not causal:
                            pe.wait_ge(a_ready, u_ + 1)
                            pe.sem_inc(den_done, 1)
                    elif kind == "R":
                        b, h = ev[1:]
                        if h == 0:
                            wait(pe, r_steps, g * (3 * NB) + (3 * b + 3))
                        for j in range(4):
                            mm = pe.transpose(ps[:, j * P:(j + 1) * P],
                                              rx[:, 4 * h + j, :, :].rearrange("p a d -> p (a d)"), core.ident[:, :])
                        mm.then_inc(a_ready, 1)
                if unused(uses):
                    pe.wait_ge(a_ready, u0 + len(uses))
                    pe.sem_inc(a_ready, unused(uses))
            groups_of(pe, body)

        @block.scalar
        def _(act):
            act.wait_ge(prep, 2 if causal else 4)
            give(act, p_ready, ou_done, sinks)

            def body(g, events, uses, u0, nxt):
                for ev in events:
                    kind = ev[0]
                    if kind == "Q":
                        b, a = ev[1:]
                        n = batch_no(g, b)
                        if causal:
                            act.wait_ge(q_in[a], n * 192 + 192)
                            if g is not None:
                                wait(act, s_ready, n * SL - SL)
                            act.activation(QA(b % 2, a), st_q[:, a, :], ACT.Copy).then_inc(q_hi, 1)
                        else:
                            act.wait_ge(q_in[a], n * 64 + 64)
                            if g is not None:
                                wait(act, s_ready, n * SL - SL)
                            act.activation(QA(b % 2, a), st_q[:, a, :], ACT.Copy).then_inc(q_hi, 1)
                    elif kind == "S":
                        b, i, a = ev[1:]
                        h, kb, q0, c0, w = cols(i)
                        n = b * SL + i * per + a
                        v_ = g * GT + n
                        if n == 0 and GT % NP:
                            wait(act, av_done, g * GT)
                            if not causal:
                                wait(act, sum_done, g * GT)
                        wait(act, av_done, v_ + (1 - NP))
                        if not causal:
                            wait(act, sum_done, v_ + (1 - NP))
                        wait(act, s_ready, v_ + 1)
                        act.activation(prob[:, n % NP, 0:w], core.bank[2 + n % 2][:, c0:c0 + w], ACT.Exp,
                                       scale=scale).then_inc(p_ready, 1)
                    elif kind == "M" and causal:
                        b, a = ev[1:]
                        n = batch_no(g, b) * per + a
                        act.wait_ge(a_ready, u0 + uses[ev] + 1)
                        wait(act, m_rows, n + 1 - per)
                        act.activation(m_row[R0:P, a, :], core.bank[RING[uses[ev] % len(RING)]][R0:P, 0:P],
                                       ACT.Copy).then_inc(m_copied, 1)
                    elif kind == "M":
                        b, a = ev[1:]
                        n = batch_no(g, b)
                        act.wait_ge(m_steps, n * (2 * per) + (2 * a + 2))
                        if g is not None:
                            wait(act, r_steps, n * 3 - 3)
                        act.activation(esink[:, b % 2, a, :], negm[:, a, 0:TB].bitcast(F32), ACT.Exp,
                                       bias=sk[:, a:a + 1] if g is None else sk[:, bass.ds(n * per + a, 1)],
                                       scale=scale).then_inc(sinks, 1)
                    elif kind == "OU":
                        b, h = ev[1:]
                        wait(act, av_done, g * GT + b * SL + (SL if h else sum(x == 0 for x, _ in tiles) * per))
                        wait(act, on_done, g * (2 * NB) + (2 * b + h - 1))
                        act.activation(ou[:, half(h)], core.bank[4 + h][:, :], ACT.Copy).then_inc(ou_done, 1)
                    elif kind == "KC" and not causal:
                        G = next_group(g)
                        if g is not None:
                            wait(act, s_ready, G * GT)
                        act.wait_ge(kn_steps, G * 4 + 4)
                        act.activation(k1[0:64, :, :], kn[0:64, :, :].bitcast(F32), ACT.Copy).then_inc(kc, 1)
                    elif kind == "VC":
                        G = next_group(g)
                        if g is not None:
                            wait(act, av_done, G * GT)
                        n_v = HEADS if causal else 2
                        src = v[:, :, 0:n_v, :] if g is None else v[:, :, bass.ds(G * n_v, n_v), :]
                        act.activation(vs.rearrange("p t (a d) -> p t a d", d=vw), src,
                                       ACT.Copy).then_inc(v_copied, 1)
            groups_of(act, body)

        @block.vector
        def _(dve):
            dve.wait_ge(prep, 2 if causal else 4)
            dve.memset(mseg[:, :, :, :], -BIG).then_inc(mseg_set, 1)
            dve.wait_ge(mseg_set, 1)
            give(dve, a_read, on_done, r_steps)

            def body(g, events, uses, u0, nxt):
                for ev in events:
                    kind = ev[0]
                    if ev in uses:
                        u = uses[ev]
                        u_ = u0 + u
                        ps = core.bank[RING[u % len(RING)]]
                        dve.wait_ge(a_ready, u_ + 1)
                    if kind == "Q":
                        b, a = ev[1:]
                        n = batch_no(g, b)
                        if causal:
                            dve.wait_ge(q_in[a], n * 192 + 192)
                            if g is not None:
                                wait(dve, s_ready, n * SL - SL)
                            dve.tensor_copy(ks[:, b % 2, a, :], st_k[:, a, :]).then_inc(k_hi, 1)
                        else:
                            dve.wait_ge(q_hi, n * per + (a + 1))
                            dve.tensor_tensor(ql[0:64, b % 2, a, :], st_q[0:64, a, :],
                                              QA(b % 2, a)[0:64].bitcast(F32), ALU.subtract).then_inc(parts, 1)
                    elif kind == "KP":
                        a = ev[1]
                        G = next_group(g)
                        dve.wait_ge(kn_in, G * 128 + (64 * a + 64))
                        dve.tensor_copy(kn[:, a, :], st_k).then_inc(kn_steps, 1)
                        dve.wait_ge(kn_steps, G * 4 + (2 * a + 1))
                        dve.tensor_tensor(kn[64:128, a, :], st_k[64:128], kn[64:128, a, :].bitcast(F32),
                                          ALU.subtract).then_inc(kn_steps, 1)
                    elif kind == "KC" and not causal:
                        G = next_group(g)
                        if g is not None:
                            wait(dve, s_ready, G * GT)
                        dve.tensor_copy(k2[:, :, :], kn[:, :, :].bitcast(F32)).then_inc(kc, 1)
                    elif kind == "A":
                        b, a, i = ev[1:]
                        qb, s = segs[i]
                        end = min((qb + 1) * P, (s + 1) * HALF) if causal else (s + 1) * HALF
                        dve.tensor_reduce(mseg[:, a, qb, s:s + 1], ps[:, 0:end - s * HALF], AX.X,
                                          ALU.max).then_inc(a_read, 1)
                        last_read = u_
                    elif kind == "X":
                        b, a = ev[1:]
                        n = batch_no(g, b)
                        wait(dve, a_read, last_read + 1)
                        dve.tensor_reduce(mrow[:, a, :], mseg[:, a, :, :], AX.X, ALU.max).then_inc(m_steps, 1)
                        dve.wait_ge(m_steps, n * (2 * per) + (2 * a + 1))
                        out = negm[:, a, 0:TB]
                        if causal:
                            dve.tensor_scalar(out, mrow[:, a, :], -1.0, None, ALU.mult).then_inc(m_steps, 1)
                        else:
                            wait(dve, sinks, n * per + (a + 1 - per))
                            s8 = sk8[:, a:a + 1] if g is None else sk8[:, bass.ds(n * per + a, 1)]
                            dve.tensor_scalar(out, mrow[:, a, :], s8, -1.0, ALU.max, ALU.mult).then_inc(m_steps, 1)
                    elif kind == "M":
                        b, a = ev[1:]
                        if causal:
                            dve.wait_ge(m_copied, batch_no(g, b) * per + (a + 1))
                            wait(dve, a_read, u_)
                        else:
                            spread_rows(dve, ql[:, b % 2, a, :], ps[:, 0:P])
                            dve.wait_ge(m_rows, batch_no(g, b) * per + (a + 1))
                        dve.sem_inc(a_read, 1)
                    elif kind == "DEN":
                        b = ev[1]
                        base = g * (3 * NB) + 3 * b
                        sums = ps[:, 0:TB * per].rearrange("p (t a) -> p t a", a=per)
                        if causal:
                            dve.tensor_copy(den[:, :, :], sums).then_inc(r_steps, 1)
                        else:
                            wait(dve, sinks, g * (NB * per) + (b + 1) * per)
                            dve.tensor_tensor(den[:, :, :], sums, esink[:, b % 2, :, :].rearrange("p a t -> p t a"),
                                              ALU.add).then_inc(r_steps, 1)
                        wait(dve, r_steps, base + 1)
                        dve.sem_inc(a_read, 1)
                        dve.reciprocal(den[:, :, :], den[:, :, :]).then_inc(r_steps, 1)
                        wait(dve, r_steps, base + 2)
                        dve.tensor_copy(rx if not causal else rx[:, :, :, :],
                                        den[:, :, :].unsqueeze(3).to_broadcast([P, TB, per, vw])
                                        ).then_inc(r_steps, 1)
                    elif kind == "R":
                        b, h = ev[1:]
                        done = g * (2 * NB) + (2 * b + h)
                        c = g * NB + b
                        dst = (on[:, c:c + 1, half(h)] if isinstance(c, int) else on[:, bass.ds(c, 1), half(h)]
                               ).rearrange("p a t -> p (a t)")
                        wait(dve, ou_done, done + 1)
                        dve.tensor_tensor(dst, ou[:, half(h)], ps[:, :], ALU.mult).then_inc(on_done, 1)
                        wait(dve, on_done, done + 1)
                        dve.sem_inc(a_read, 1)
                if unused(uses):
                    wait(dve, a_read, u0 + len(uses))
                    dve.sem_inc(a_read, unused(uses))
            groups_of(dve, body)


def out_product(nc, core, name, on, n_chunks, w_dram, bias, dst, add_x):
    with ExitStack() as ctx:
        sem = lambda n: nc.alloc_semaphore(f"{name}_{n}")
        sb = lambda n, shape, dt=F32: ctx.enter_context(nc.sbuf_tensor(f"{name}_{n}", shape, dt))
        w_in = [sem("w_in0"), sem("w_in1")]
        raw_free, w_split, oh_ready, ol_ready, y_done, added, b_in = map(
            sem, ("raw_free", "w_split", "oh", "ol", "y", "added", "b_in"))
        raw = sb("raw", [P, 2, D])
        wh = sb("wh", [P, 2, D], F32R)
        wl = sb("wl", [P, 2, D], F32R)
        oh = sb("ohi", [P, 2, T], F32R)
        ol = sb("olo", [P, 2, T], F32R)
        bc = sb("bc", [P, DC])
        block = ctx.enter_context(nc.Block())

        def chunks(eng, body):
            with eng.Fori(0, n_chunks // 2) as i:
                for slot in range(2):
                    body(i * 2 + slot, i, slot)

        @block.sync
        def _(sp):
            sp.dma_start(bc[:, :], bias).then_inc(b_in, 16)

            def load(c, i, slot):
                sp.wait_ge(raw_free, c + 1)
                sp.dma_start(raw[:, slot, :], w_dram[c]).then_inc(w_in[slot], 16)
            chunks(sp, load)

        @block.gpsimd
        def _(pool):
            pool.sem_inc(raw_free, 2)

            def split(c, i, slot):
                pool.wait_ge(y_done, c + 1)
                pool.wait_ge(w_in[slot], i * 16 + 16)
                pool.wait_ge(b_in, 16)
                core.pool_copy(pool, wh[:, slot, :], raw[:, slot, :]).then_inc(w_split, 1)
                pool.wait_ge(w_split, c * 2 + 1)
                pool.tensor_tensor(wl[:, slot, :], raw[:, slot, :], wh[:, slot, :].bitcast(F32),
                                   ALU.subtract).then_inc(w_split, 1)
                pool.wait_ge(w_split, c * 2 + 2)
                pool.sem_inc(raw_free, 1)
            chunks(pool, split)

        @block.scalar
        def _(act):
            def high(c, i, slot):
                act.wait_ge(y_done, c + 1)
                src = on[:, bass.ds(c, 1), :].rearrange("p a t -> p (a t)")
                act.activation(oh[:, slot, :], src, ACT.Copy).then_inc(oh_ready, 1)
            chunks(act, high)

        @block.vector
        def _(dve):
            def low(c, i, slot):
                dve.wait_ge(oh_ready, c + 1)
                src = on[:, bass.ds(c, 1), :].rearrange("p a t -> p (a t)")
                dve.tensor_tensor(ol[:, slot, :], src, oh[:, slot, :].bitcast(F32), ALU.subtract).then_inc(ol_ready, 1)
            chunks(dve, low)
            dve.wait_ge(b_in, 16)
            dve.wait_ge(y_done, n_chunks + 2)
            for m in range(DC):
                for h in range(NH):
                    ps = core.bank[DC * h + m][:, :]
                    if add_x:
                        dve.scalar_tensor_tensor(dst[:, m, half(h)], ps, bc[:, m:m + 1], dst[:, m, half(h)], ALU.add,
                                                 ALU.add).then_inc(added, 1)
                    else:
                        dve.tensor_scalar(dst[:, m, half(h)], ps, bc[:, m:m + 1], None, ALU.add).then_inc(added, 1)

        @block.tensor
        def _(pe):
            for m in range(DC):
                for h in range(NH):
                    pe.matmul(core.bank[DC * h + m][:, :], core.zero_r[:, :], core.xh[:, 0, half(h)], start=True,
                              stop=False, skip_group_check=True)
            pe.sem_inc(y_done, 2)

            def product(c, i, slot):
                pe.wait_ge(w_split, c * 2 + 2)
                pe.wait_ge(ol_ready, c + 1)
                for m in range(DC):
                    for h in range(NH):
                        for w, x in ((wh, oh), (wl, oh), (wh, ol)):
                            mm = pe.matmul(core.bank[DC * h + m][:, :], w[:, slot, m * P:(m + 1) * P],
                                           x[:, slot, half(h)], start=False, stop=False, skip_group_check=True)
                mm.then_inc(y_done, 1)
            chunks(pe, product)


def low_state(nc, core, w_dram, t_h, t_l):
    with ExitStack() as ctx:
        sem = lambda n: nc.alloc_semaphore("ls_" + n)
        sb = lambda n, shape, dt=F32: ctx.enter_context(nc.sbuf_tensor("ls_" + n, shape, dt))
        w_in, split, ready, hi, lo = map(sem, ("w", "sp", "rd", "hi", "lo"))
        w = sb("wt", [P, DC, P])
        wh = sb("wth", [P, DC, P], F32R)
        wl = sb("wtl", [P, DC, P], F32R)
        block = ctx.enter_context(nc.Block())

        @block.sync
        def _(sp):
            sp.dma_start(w[:, :, :], w_dram).then_inc(w_in, 16)

        @block.tensor
        def _(pe):
            pe.wait_ge(split, 2)
            for h in range(NH):
                gemm3(pe, core.bank[h][:, :], [wh[:, k, :] for k in range(DC)], [wl[:, k, :] for k in range(DC)],
                      [core.xh[:, k, half(h)] for k in range(DC)],
                      [core.xl[:, k, half(h)] for k in range(DC)]).then_inc(ready, 1)

        @block.scalar
        def _(act):
            for h in range(NH):
                act.wait_ge(ready, h + 1)
                act.activation(t_h[:, half(h)], core.bank[h][:, :], ACT.Copy).then_inc(hi, 1)

        @block.vector
        def _(dve):
            dve.wait_ge(w_in, 16)
            dve.tensor_copy(wh[:, :, :], w[:, :, :]).then_inc(split, 1)
            dve.wait_ge(split, 1)
            dve.tensor_tensor(wl[:, :, :], w[:, :, :], wh[:, :, :].bitcast(F32), ALU.subtract).then_inc(split, 1)
            for h in range(NH):
                dve.wait_ge(hi, h + 1)
                dve.tensor_tensor(t_l[:, half(h)], core.bank[h][:, :], t_h[:, half(h)].bitcast(F32),
                                  ALU.subtract).then_inc(lo, 1)


def state_attention(nc, core, a):
    NQ = 4
    DK = 128
    uses = [(("v", t), t % 4) for t in range(TB)] + [(("g", t), t % 4) for t in range(TB)]
    scores = lambda p: [(("s", p, h), h) for h in range(NH)]
    first_q = lambda p: [(("qk", p, 0, 0, h), 4 + h) for h in range(NH)]
    for p in range(2):
        if p == 0:
            uses += scores(0) + first_q(0)
        uses += [(("qk", p, a_, w, h), 4 + 2 * w + h) for a_ in range(2) for w in range(2) for h in range(NH)
                 if a_ or w]
        uses += [(("te", p, h), h) for h in range(NH)]
        for a_ in range(2):
            uses += [(("tk", p, a_, h), (2, 4)[a_] + h) for h in range(NH)]
            uses += [(("at", p, a_, h), (0, 6)[a_] + h) for h in range(NH)]
        uses += [(("s1", p, h), 2 + h) for h in range(NH)]
        uses += [(("ok", p, h), h) for h in range(NH)]
        uses += [(("tok", p, h), 2 + h) for h in range(NH)]
        uses += [(("s2", p, h), 4 + h) for h in range(NH)]
        uses += [(("tq", p, h), 6 + h) for h in range(NH)]
        uses += [(("w2", p, i), (0, 1, 4, 5)[i]) for i in range(4)]
        uses += [(("o", p, i), (2, 3, 6, 7)[i]) for i in range(4)]
        if p == 0:
            uses += scores(1) + first_q(1)
        uses += [(("to", p, a_, h), (2, 6)[a_] + h) for h in range(NH) for a_ in range(2)]
        uses += [(("wo", p, m, h), (2, 6)[m] + h) for h in range(NH) for m in range(DC)]
    bank_of = dict(uses)
    count = [0] * 8
    nth = {}
    for key, b in uses:
        nth[key] = count[b]
        count[b] += 1

    with ExitStack() as ctx:
        sem = lambda n: nc.alloc_semaphore("l2a_" + n)
        sb = lambda n, shape, dt=F32: ctx.enter_context(nc.sbuf_tensor("l2a_" + n, shape, dt))
        t_h = sb("t_h", [P, T], F32R)
        t_l = sb("t_l", [P, T], F32R)
        low_state(nc, core, a["l2a_ws1"], t_h, t_l)
        full = [sem(f"bank_full{b}") for b in range(8)]
        free = [sem(f"bank_free{b}") for b in range(8)]
        c_in, vw_in, gw_in, sw_in, wo_in = map(sem, ("c_in", "vw_in", "gw_in", "sw_in", "wo_in"))
        qkw_in = [sem("qkw_in0"), sem("qkw_in1")]
        vraw_free, qkraw_free, swraw_free, woraw_free = map(sem, ("vraw_free", "qkraw_free", "swraw_free", "woraw_free"))
        vg_hi, vg_lo, sw_split, qkw_split, wo_split = map(sem, ("vg_hi", "vg_lo", "sw_split", "qkw_split", "wo_split"))
        v_ready, g_silu, clipped, es_ready, summed, enz_ready = map(
            sem, ("v_ready", "g_silu", "clipped", "es", "summed", "enz"))
        swapped, times_cos, times_sin, qk_ready = map(sem, ("swapped", "cos", "sin", "qk"))
        tm_ready, at_ready, s1_ready, s2_ready, oke_ready = map(sem, ("tm", "at", "s1", "s2", "oke"))
        shifted, exped, soft, pb_ready, w2_ready = map(sem, ("shifted", "exped", "soft", "pb", "w2"))
        squared, sumsq, rooted, gated = map(sem, ("squared", "sumsq", "rooted", "gated"))
        oth, otl, pair_done, rooted_inv, zeroed = map(sem, ("oth", "otl", "pair_done", "rooted_inv", "zeroed"))

        tab = sb("tab", [P, 2, T])
        causal = sb("causal", [P, P])
        gnw = sb("gnw", [P, 1])
        vraw = sb("vraw", [P, DC, 512])
        vgh = sb("vgh", [P, 2, DC, 512], F32R)
        vgl = sb("vgl", [P, 2, DC, 512], F32R)
        swraw = sb("swraw", [P, 2, P + 1])
        swh = sb("swh", [P, 2, P], F32R)
        swl = sb("swl", [P, 2, P], F32R)
        sbias = sb("sbias", [P, 2])
        qkraw = sb("qkraw", [P, 2, DC * P])
        qkwh = sb("qkwh", [P, 4, DC * P], F32R)
        qkwl = sb("qkwl", [P, 4, DC * P], F32R)
        woraw = sb("woraw", [P, 2, D])
        woh = sb("woh", [P, 2, D], F32R)
        wol = sb("wol", [P, 2, D], F32R)
        vq = sb("vq", [P, TB, 4, DK])
        gq = sb("gq", [P, TB, 4, DK])
        qt = sb("qt", [P, 2, 2, T])
        ktm = sb("ktm", [P, 2, TB, P])
        es = sb("es_", [P, T])
        estm = sb("estm", [P, TB, P])
        enz = sb("enz_", [P, T])
        atw = sb("atw", [P, TB, 2, P])
        s1 = sb("s1_", [P, TB, 2, 64])
        s2 = sb("s2_", [P, TB, DK])
        pb = sb("pb_", [P, TB, 2, P])
        og = sb("og", [P, TB, 2, DK])
        cs = og[:, 0:4, :, :].rearrange("p t a d -> p (t a d)")
        sc = og[:, 4:8, :, :].rearrange("p t a d -> p (t a d)")
        oke = core.xn[:, 0, :]
        qv = core.xn[:, 1, :]
        swap = core.xn[:, 0, :].rearrange("p (h t) -> p h t", h=NH)
        t2 = core.xn[:, 1, :].rearrange("p (h t) -> p h t", h=NH)
        ogh = sb("ogh", [P, 2, T], F32R)
        ogl = sb("ogl", [P, 2, T], F32R)
        mx = sb("mx", [P, TB, 2])
        rs = sb("rs", [P, TB, 2])
        ss = sb("ss", [P, TB, 2])
        block = ctx.enter_context(nc.Block())

        def at(g, key):
            return g * count[bank_of[key]] + (nth[key] + 1)

        def bank(key):
            return core.bank[bank_of[key]]

        @block.sync
        def _(sp):
            sp.dma_start(tab[:, :, :], a["l2a_tab"]).then_inc(c_in, 16)
            sp.dma_start(causal[:, :], a["l2a_mask"]).then_inc(c_in, 16)
            sp.dma_start(gnw[:, :], a["l2a_gnw"]).then_inc(c_in, 16)
            with sp.Fori(0, NQ) as g:
                for j, s_in in ((0, vw_in), (1, gw_in)):
                    sp.wait_ge(vraw_free, g * 2 + (j + 1))
                    sp.dma_start(vraw[:, :, :], a["l2a_wvg"][g * 2 + j]).then_inc(s_in, 16)
                sp.wait_ge(swraw_free, g + 1)
                sp.dma_start(swraw[:, :, :], a["l2a_ws2"][g]).then_inc(sw_in, 16)
                for c in range(8):
                    sp.wait_ge(qkraw_free, g * 8 + (c + 1))
                    sp.dma_start(qkraw[:, c % 2, :], a["l2a_wqk"][g * 8 + c]).then_inc(qkw_in[c % 2], 16)
                    if c % 4 == 3:
                        sp.wait_ge(woraw_free, g * 2 + (c // 4 + 1))
                        sp.dma_start(woraw[:, :, :], a["l2a_wo"][g * 2 + c // 4]).then_inc(wo_in, 16)

        @block.gpsimd
        def _(pool):
            pool.sem_inc(vraw_free, 1)
            pool.sem_inc(swraw_free, 1)
            pool.sem_inc(qkraw_free, 2)
            pool.sem_inc(woraw_free, 1)
            pool.sem_inc(times_sin, 2)
            pool.memset(pb[:, :, :, :], 0.0).then_inc(zeroed, 1)
            pool.memset(s1[:, 0, :, :], 0.0).then_inc(zeroed, 1)
            pool.memset(s2[:, 0, :], 0.0).then_inc(zeroed, 1)
            pool.wait_ge(c_in, 48)
            with pool.Fori(0, NQ) as g:
                for j in range(2):
                    pool.wait_ge(vg_hi, g * 2 + (j + 1))
                    pool.tensor_tensor(vgl[:, j, :, :], vraw[:, :, :], vgh[:, j, :, :].bitcast(F32),
                                       ALU.subtract).then_inc(vg_lo, 1)
                    pool.wait_ge(vg_lo, g * 2 + (j + 1))
                    pool.sem_inc(vraw_free, 1)
                pool.wait_ge(sw_in, g * 16 + 16)
                pool.wait_ge(pair_done, g * 2 + 1)
                pool.wait_ge(c_in, 48)
                core.pool_copy(pool, swh[:, :, :], swraw[:, :, 0:P]).then_inc(sw_split, 1)
                pool.tensor_copy(sbias[:, :], swraw[:, :, P]).then_inc(sw_split, 1)
                pool.wait_ge(sw_split, g * 3 + 2)
                pool.tensor_tensor(swl[:, :, :], swraw[:, :, 0:P], swh[:, :, :].bitcast(F32),
                                   ALU.subtract).then_inc(sw_split, 1)
                pool.wait_ge(sw_split, g * 3 + 3)
                pool.sem_inc(swraw_free, 1)

                def split_qk(c):
                    if c >= 4:
                        last = ("qk", 0, (c - 4) // 2, c % 2, 1)
                        pool.wait_ge(full[bank_of[last]], at(g, last))
                    pool.wait_ge(qkw_in[c % 2], g * 64 + 16 * (c // 2 + 1))
                    pool.wait_ge(c_in, 48)
                    core.pool_copy(pool, qkwh[:, c % 4, :], qkraw[:, c % 2, :]).then_inc(qkw_split, 1)
                    pool.wait_ge(qkw_split, g * 16 + (2 * c + 1))
                    pool.tensor_tensor(qkwl[:, c % 4, :], qkraw[:, c % 2, :], qkwh[:, c % 4, :].bitcast(F32),
                                       ALU.subtract).then_inc(qkw_split, 1)
                    pool.wait_ge(qkw_split, g * 16 + (2 * c + 2))
                    pool.sem_inc(qkraw_free, 1)

                for c in range(4):
                    split_qk(c)
                for c in range(8):
                    for h in range(NH):
                        k = 2 * c + h
                        pool.wait_ge(qk_ready, g * 16 + (k + 1))
                        pool.wait_ge(swapped, g * 32 + (2 * k + 2))
                        pool.tensor_tensor(t2[:, h, :], swap[:, h, :], tab[:, 1, half(h)],
                                           ALU.mult).then_inc(times_sin, 1)
                    if c == 3:
                        for e in range(4, 8):
                            split_qk(e)
                    if c % 4 == 3:
                        p = c // 4
                        pool.wait_ge(wo_in, g * 32 + 16 * (p + 1))
                        pool.wait_ge(pair_done, g * 2 + (p + 1))
                        pool.wait_ge(c_in, 48)
                        core.pool_copy(pool, woh[:, :, :], woraw[:, :, :]).then_inc(wo_split, 1)
                        pool.wait_ge(wo_split, g * 4 + (2 * p + 1))
                        pool.tensor_tensor(wol[:, :, :], woraw[:, :, :], woh[:, :, :].bitcast(F32),
                                           ALU.subtract).then_inc(wo_split, 1)
                        pool.wait_ge(wo_split, g * 4 + (2 * p + 2))
                        pool.sem_inc(woraw_free, 1)

        @block.tensor
        def _(pe):
            pe.sem_inc(pair_done, 1)
            pe.wait_ge(c_in, 48)
            pe.wait_ge(zeroed, 3)
            with pe.Fori(0, NQ) as g:
                for j, kind in enumerate("vg"):
                    pe.wait_ge(vg_lo, g * 2 + (j + 1))
                    for t in range(TB):
                        key = (kind, t)
                        tok = slice(t * P, (t + 1) * P)
                        pe.wait_ge(free[bank_of[key]], at(g, key))
                        gemm3(pe, bank(key)[:, :], [core.xh[:, k, tok] for k in range(DC)],
                              [core.xl[:, k, tok] for k in range(DC)], [vgh[:, j, k, :] for k in range(DC)],
                              [vgl[:, j, k, :] for k in range(DC)]).then_inc(full[bank_of[key]], 1)
                pe.wait_ge(sw_split, g * 3 + 3)

                def slot_scores(p):
                    for h in range(NH):
                        key = ("s", p, h)
                        pe.wait_ge(free[bank_of[key]], at(g, key))
                        gemm3(pe, bank(key)[:, :], [swh[:, p, :]], [swl[:, p, :]], [t_h[:, half(h)]],
                              [t_l[:, half(h)]]).then_inc(full[bank_of[key]], 1)

                def project(p, c):
                    a_, w = c // 2, c % 2
                    pe.wait_ge(qkw_split, g * 16 + (8 * p + 2 * c + 2))
                    for h in range(NH):
                        key = ("qk", p, a_, w, h)
                        pe.wait_ge(free[bank_of[key]], at(g, key))
                        gemm3(pe, bank(key)[:, :], [qkwh[:, c, k * P:(k + 1) * P] for k in range(DC)],
                              [qkwl[:, c, k * P:(k + 1) * P] for k in range(DC)],
                              [core.xh[:, k, half(h)] for k in range(DC)],
                              [core.xl[:, k, half(h)] for k in range(DC)]).then_inc(full[bank_of[key]], 1)

                slot_scores(0)
                project(0, 0)
                for p in range(2):
                    for c in range(1, 4):
                        project(p, c)
                    for h in range(NH):
                        key = ("te", p, h)
                        pe.wait_ge(es_ready, g * 4 + (2 * p + h + 1))
                        pe.wait_ge(free[bank_of[key]], at(g, key))
                        for b in range(4):
                            t = 4 * h + b
                            mm = pe.transpose(bank(key)[:, b * P:(b + 1) * P], es[:, t * P:(t + 1) * P],
                                              core.ident[:, :])
                        mm.then_inc(full[bank_of[key]], 1)
                    for a_ in range(2):
                        for h in range(NH):
                            key = ("tk", p, a_, h)
                            pe.wait_ge(qk_ready, g * 16 + (8 * p + 4 * a_ + 2 + h + 3))
                            pe.wait_ge(free[bank_of[key]], at(g, key))
                            for b in range(4):
                                t = 4 * h + b
                                mm = pe.transpose(bank(key)[:, b * P:(b + 1) * P],
                                                  qt[:, a_, 1, t * P:(t + 1) * P], core.ident[:, :])
                            mm.then_inc(full[bank_of[key]], 1)
                        for h in range(NH):
                            key = ("at", p, a_, h)
                            pe.wait_ge(free[bank_of[key]], at(g, key))
                            for b in range(4):
                                tok = slice((4 * h + b) * P, (4 * h + b + 1) * P)
                                mm = pe.matmul(bank(key)[:, b * P:(b + 1) * P], qt[:, a_, 1, tok], qt[:, a_, 0, tok],
                                               start=True, stop=True)
                            mm.then_inc(full[bank_of[key]], 1)
                    pe.wait_ge(tm_ready, g * 12 + (6 * p + 6))
                    for h in range(NH):
                        key = ("s1", p, h)
                        pe.wait_ge(free[bank_of[key]], at(g, key))
                        for t in range(4 * h, min(4 * h + 4, TB - 1)):
                            for a_ in range(2):
                                c0 = (t % 4) * P + 64 * a_
                                mm = pe.matmul(bank(key)[:, c0:c0 + 64], ktm[:, a_, t, :],
                                               estm[:, t, 64 * a_:64 * a_ + 64], start=True, stop=True)
                        mm.then_inc(full[bank_of[key]], 1)
                    for h in range(NH):
                        key = ("ok", p, h)
                        pe.wait_ge(free[bank_of[key]], at(g, key))
                        pe.wait_ge(at_ready, g * 8 + (4 * p + 4))
                        pe.wait_ge(s1_ready, g * 14 + (7 * p + (3 if h == 0 else 7)))
                        for t in range(4 * h, 4 * h + 4):
                            for a_ in range(2):
                                out = bank(key)[64 * a_:64 * a_ + 64, (t % 4) * P:(t % 4 + 1) * P]
                                mm = pe.matmul(out, estm[:, t, 64 * a_:64 * a_ + 64], atw[:, t, a_, :],
                                               start=True, stop=t == 0, tile_position=(0, 64 * a_))
                                if t:
                                    mm = pe.matmul(out, s1[:, t, a_, :], qt[:, a_, 0, t * P:(t + 1) * P],
                                                   start=False, stop=True, tile_position=(0, 64 * a_))
                        mm.then_inc(full[bank_of[key]], 1)
                    for h in range(NH):
                        key = ("tok", p, h)
                        pe.wait_ge(oke_ready, g * 4 + (2 * p + h + 1))
                        pe.wait_ge(free[bank_of[key]], at(g, key))
                        for b in range(4):
                            t = 4 * h + b
                            mm = pe.transpose(bank(key)[:, b * P:(b + 1) * P], oke[:, t * P:(t + 1) * P],
                                              core.ident[:, :])
                        mm.then_inc(full[bank_of[key]], 1)
                    for h in range(NH):
                        key = ("s2", p, h)
                        pe.wait_ge(v_ready, g * TB + TB)
                        pe.wait_ge(free[bank_of[key]], at(g, key))
                        for t in range(4 * h, min(4 * h + 4, TB - 1)):
                            for a_ in range(2):
                                mm = pe.matmul(bank(key)[64 * a_:64 * a_ + 64, (t % 4) * P:(t % 4 + 1) * P],
                                               estm[:, t, 64 * a_:64 * a_ + 64], vq[:, t, 2 * p + a_, :],
                                               start=True, stop=True, tile_position=(0, 64 * a_))
                        mm.then_inc(full[bank_of[key]], 1)
                    for h in range(NH):
                        key = ("tq", p, h)
                        pe.wait_ge(soft, g * 16 + (8 * p + 5 + 3 * h))
                        pe.wait_ge(free[bank_of[key]], at(g, key))
                        for b in range(4):
                            t = 4 * h + b
                            mm = pe.transpose(bank(key)[:, b * P:(b + 1) * P], qv[:, t * P:(t + 1) * P],
                                              core.ident[:, :])
                        mm.then_inc(full[bank_of[key]], 1)
                    for i in range(4):
                        key = ("w2", p, i)
                        pe.wait_ge(pb_ready, g * 8 + (4 * p + 2 * (i // 2) + 2))
                        pe.wait_ge(free[bank_of[key]], at(g, key))
                        for t in (2 * i, 2 * i + 1):
                            mm = pe.matmul(bank(key)[:, (t % 2) * 256:(t % 2 + 1) * 256], es[:, t * P:(t + 1) * P],
                                           pb[:, t, :, :].rearrange("p a t -> p (a t)"), start=True, stop=True)
                        mm.then_inc(full[bank_of[key]], 1)
                    for i in range(4):
                        key = ("o", p, i)
                        pe.wait_ge(w2_ready, g * 8 + (4 * p + i + 1))
                        pe.wait_ge(s2_ready, g * 14 + (7 * p + 2 * i + 1))
                        pe.wait_ge(free[bank_of[key]], at(g, key))
                        for t in (2 * i, 2 * i + 1):
                            for a_ in range(2):
                                out = bank(key)[:, (t % 2) * 256 + a_ * P:(t % 2) * 256 + (a_ + 1) * P]
                                mm = pe.matmul(out, atw[:, t, a_, :], vq[:, t, 2 * p + a_, :], start=True, stop=t == 0)
                                if t:
                                    mm = pe.matmul(out, pb[:, t, a_, :], s2[:, t, :], start=False, stop=True)
                        mm.then_inc(full[bank_of[key]], 1)
                    if p == 0:
                        slot_scores(1)
                        project(1, 0)
                    for h in range(NH):
                        for a_ in range(2):
                            key = ("to", p, a_, h)
                            pe.wait_ge(gated, g * 32 + (16 * p + 8 * h + 8))
                            pe.wait_ge(free[bank_of[key]], at(g, key))
                            for b in range(4):
                                mm = pe.transpose(bank(key)[:, b * P:(b + 1) * P], og[:, 4 * h + b, a_, :],
                                                  core.ident[:, :])
                            mm.then_inc(full[bank_of[key]], 1)
                    pe.wait_ge(wo_split, g * 4 + (2 * p + 2))
                    for h in range(NH):
                        for m in range(DC):
                            key = ("wo", p, m, h)
                            pe.wait_ge(otl, g * 8 + (4 * p + 2 * h + 2))
                            pe.wait_ge(free[bank_of[key]], at(g, key))
                            gemm3(pe, bank(key)[:, :], [woh[:, a_, m * P:(m + 1) * P] for a_ in range(2)],
                                  [wol[:, a_, m * P:(m + 1) * P] for a_ in range(2)],
                                  [ogh[:, a_, half(h)] for a_ in range(2)],
                                  [ogl[:, a_, half(h)] for a_ in range(2)]).then_inc(full[bank_of[key]], 1)
                    pe.wait_ge(full[bank_of[key]], at(g, key))
                    pe.sem_inc(pair_done, 1)

        @block.scalar
        def _(act):
            act.wait_ge(c_in, 48)
            with act.Fori(0, NQ) as g:
                for j, s_in in ((0, vw_in), (1, gw_in)):
                    act.wait_ge(s_in, g * 16 + 16)
                    act.activation(vgh[:, j, :, :], vraw[:, :, :], ACT.Copy).then_inc(vg_hi, 1)
                act.wait_ge(pair_done, g * 2 + 1)
                for t in range(TB):
                    key = ("g", t)
                    act.wait_ge(full[bank_of[key]], at(g, key))
                    act.activation(gq[:, t, :, :].rearrange("p a d -> p (a d)"), bank(key)[:, :],
                                   ACT.Silu).then_inc(free[bank_of[key]], 1)
                act.wait_ge(free[3], at(g, ("g", TB - 1)) + 1)
                act.sem_inc(g_silu, TB)
                for p in range(2):
                    for h in range(NH):
                        act.wait_ge(clipped, g * 8 + (4 * p + 2 * h + 2))
                        act.activation(es[:, half(h)], sc[:, half(h)], ACT.Exp).then_inc(es_ready, 1)
                    for c in range(4):
                        a_, w = c // 2, c % 2
                        for h in range(NH):
                            key = ("qk", p, a_, w, h)
                            k = 8 * p + 2 * c + h
                            act.wait_ge(full[bank_of[key]], at(g, key))
                            act.wait_ge(times_sin, g * 16 + (k + 1))
                            act.activation(swap[0:64, h, :], bank(key)[64:128, :], ACT.Copy).then_inc(swapped, 1)
                            act.activation(swap[64:128, h, :], bank(key)[0:64, :], ACT.Copy).then_inc(swapped, 1)
                    for h in range(NH):
                        key = ("te", p, h)
                        act.wait_ge(full[bank_of[key]], at(g, key))
                        act.activation(estm[:, 4 * h:4 * h + 4, :].rearrange("p t m -> p (t m)"), bank(key)[:, :],
                                       ACT.Copy).then_inc(free[bank_of[key]], 1)
                        act.wait_ge(free[bank_of[key]], at(g, key) + 1)
                        act.sem_inc(tm_ready, 1)
                    for a_ in range(2):
                        for h in range(NH):
                            key = ("tk", p, a_, h)
                            act.wait_ge(full[bank_of[key]], at(g, key))
                            act.activation(ktm[:, a_, 4 * h:4 * h + 4, :].rearrange("p t m -> p (t m)"),
                                           bank(key)[:, :], ACT.Copy).then_inc(free[bank_of[key]], 1)
                            act.wait_ge(free[bank_of[key]], at(g, key) + 1)
                            act.sem_inc(tm_ready, 1)
                    for h in range(NH):
                        act.wait_ge(shifted, g * 4 + (2 * p + h + 1))
                        act.activation(qv[:, half(h)], qv[:, half(h)], ACT.Exp).then_inc(exped, 1)
                    for i in range(4):
                        key = ("o", p, i)
                        act.wait_ge(full[bank_of[key]], at(g, key))
                        act.activation(og[:, 2 * i:2 * i + 2, :, :].rearrange("p t a d -> p (t a d)"),
                                       bank(key)[:, :], ACT.Square).then_inc(squared, 1)
                    act.wait_ge(sumsq, g * 8 + (4 * p + 4))
                    act.activation(ss[:, :, :], ss[:, :, :], ACT.Sqrt, bias=core.eps5[:, :],
                                   scale=1.0 / DK).then_inc(rooted, 1)
                    for h in range(NH):
                        for a_ in range(2):
                            key = ("to", p, a_, h)
                            act.wait_ge(full[bank_of[key]], at(g, key))
                            act.activation(ogh[:, a_, half(h)], bank(key)[:, :], ACT.Copy,
                                           scale=gnw[:, :]).then_inc(oth, 1)

        @block.vector
        def _(dve):
            for b in range(8):
                dve.sem_inc(free[b], 1)
            dve.sem_inc(qk_ready, 2)
            dve.wait_ge(c_in, 48)
            dve.wait_ge(zeroed, 3)
            with dve.Fori(0, NQ) as g:
                dve.wait_ge(pair_done, g * 2 + 1)
                for t in range(TB):
                    key = ("v", t)
                    dve.wait_ge(full[bank_of[key]], at(g, key))
                    dve.tensor_copy(vq[:, t, :, :].rearrange("p a d -> p (a d)"),
                                    bank(key)[:, :]).then_inc(free[bank_of[key]], 1)
                dve.wait_ge(free[3], at(g, ("v", TB - 1)) + 1)
                dve.sem_inc(v_ready, TB)
                dve.wait_ge(sw_split, g * 3 + 3)
                for p in range(2):
                    dve.wait_ge(pair_done, g * 2 + (p + 1))
                    for h in range(NH):
                        key = ("s", p, h)
                        n = g * 8 + (4 * p + 2 * h)
                        dve.wait_ge(full[bank_of[key]], at(g, key))
                        dve.tensor_scalar(sc[:, half(h)], bank(key)[:, :], sbias[:, p:p + 1], 32.0, ALU.add,
                                          ALU.min).then_inc(clipped, 1)
                        dve.wait_ge(clipped, n + 1)
                        dve.sem_inc(free[bank_of[key]], 1)
                        dve.tensor_scalar(sc[:, half(h)], sc[:, half(h)], -32.0, None, ALU.max).then_inc(clipped, 1)
                    def add_products(c, h):
                        k = 8 * p + 2 * c + h
                        dst = qt[:, c // 2, c % 2, half(h)]
                        dve.wait_ge(times_sin, g * 16 + (k + 3))
                        dve.tensor_tensor(dst, dst, t2[:, h, :], ALU.add).then_inc(qk_ready, 1)

                    for c in range(4):
                        a_, w = c // 2, c % 2
                        for h in range(NH):
                            key = ("qk", p, a_, w, h)
                            k = 8 * p + 2 * c + h
                            dve.wait_ge(swapped, g * 32 + (2 * k + 2))
                            dve.tensor_tensor(qt[:, a_, w, half(h)], bank(key)[:, :], tab[:, 0, half(h)],
                                              ALU.mult).then_inc(times_cos, 1)
                            dve.wait_ge(times_cos, g * 16 + (k + 1))
                            dve.sem_inc(free[bank_of[key]], 1)
                            if c or h:
                                add_products(c if h else c - 1, 1 - h)
                        if c == 0:
                            for h in range(NH):
                                n = g * 4 + (2 * p + h)
                                dve.wait_ge(es_ready, n + 1)
                                if h:
                                    dve.wait_ge(summed, n)
                                dve.tensor_tensor_scan(cs[:, half(h)], core.ones_r[:, 0:1].bitcast(F32)
                                                       .to_broadcast([P, HALF]), es[:, half(h)],
                                                       cs[:, HALF - 1:HALF] if h else 0.0, ALU.mult,
                                                       ALU.add).then_inc(summed, 1)
                    add_products(3, 1)

                    def invert(h):
                        dve.wait_ge(summed, g * 4 + (2 * p + h + 1))
                        dve.reciprocal(enz[:, half(h)], cs[:, half(h)]).then_inc(enz_ready, 1)

                    for a_ in range(2):
                        if a_ == 0:
                            invert(0)
                        for h in range(NH):
                            key = ("at", p, a_, h)
                            dve.wait_ge(full[bank_of[key]], at(g, key))
                            dve.tensor_tensor(atw[:, 4 * h:4 * h + 4, a_, :],
                                              bank(key)[:, :].rearrange("p (t q) -> p t q", q=P),
                                              causal[:, :].unsqueeze(1).to_broadcast([P, 4, P]),
                                              ALU.mult).then_inc(at_ready, 1)
                            dve.wait_ge(at_ready, g * 8 + (4 * p + 2 * a_ + h + 1))
                            dve.sem_inc(free[bank_of[key]], 1)
                    def add_states(name_, st, ready, h):
                        for t in range(4 * h, min(4 * h + 4, TB - 1)):
                            key = (name_, p, t // 4)
                            if t % 4 == 0:
                                dve.wait_ge(full[bank_of[key]], at(g, key))
                            ps = bank(key)[:, (t % 4) * P:(t % 4 + 1) * P]
                            flat = lambda x: x.rearrange("p a m -> p (a m)") if name_ == "s1" else x
                            if t:
                                dve.wait_ge(ready, g * 14 + (7 * p + t))
                            dve.tensor_tensor(flat(st[:, t + 1]), flat(st[:, t]), ps, ALU.add).then_inc(ready, 1)
                            if t % 4 == 3 or t == TB - 2:
                                dve.wait_ge(ready, g * 14 + (7 * p + t + 1))
                                dve.sem_inc(free[bank_of[key]], 1)
                    for h in range(NH):
                        add_states("s1", s1, s1_ready, h)
                    invert(1)
                    dve.wait_ge(enz_ready, g * 4 + (2 * p + 2))
                    for h in range(NH):
                        key = ("ok", p, h)
                        dve.wait_ge(full[bank_of[key]], at(g, key))
                        dve.scalar_tensor_tensor(oke[:, half(h)], bank(key)[:, :], float(DK) ** -0.5, enz[:, half(h)],
                                                 ALU.mult, ALU.mult).then_inc(oke_ready, 1)
                        dve.wait_ge(oke_ready, g * 4 + (2 * p + h + 1))
                        dve.sem_inc(free[bank_of[key]], 1)
                    n = g * 16 + 8 * p
                    for h in range(NH):
                        key = ("tok", p, h)
                        t = slice(4 * h, 4 * h + 4)
                        ps = bank(key)[:, :].rearrange("p (t a m) -> p t a m", a=2, m=64)
                        dve.wait_ge(full[bank_of[key]], at(g, key))
                        dve.tensor_reduce(mx[:, t, :], ps, AX.X, ALU.max).then_inc(soft, 1)
                        dve.wait_ge(soft, n + (h + 1))
                        dve.tensor_tensor(qv[:, half(h)].rearrange("p (t a m) -> p t a m", a=2, m=64), ps,
                                          mx[:, t, :].unsqueeze(3).to_broadcast([P, 4, 2, 64]),
                                          ALU.subtract).then_inc(shifted, 1)
                        dve.wait_ge(shifted, g * 4 + (2 * p + h + 1))
                        dve.sem_inc(free[bank_of[key]], 1)
                    q4 = qv.rearrange("p (t a m) -> p t a m", a=2, m=64)
                    for h in range(NH):
                        t = slice(4 * h, 4 * h + 4)
                        dve.wait_ge(exped, g * 4 + (2 * p + h + 1))
                        dve.tensor_reduce(rs[:, t, :], q4[:, t], AX.X, ALU.add).then_inc(soft, 1)
                        dve.wait_ge(soft, n + (3 * h + 3))
                        dve.reciprocal(rs[:, t, :], rs[:, t, :]).then_inc(soft, 1)
                        dve.wait_ge(soft, n + (3 * h + 4))
                        dve.tensor_tensor(q4[:, t], q4[:, t], rs[:, t, :].unsqueeze(3).to_broadcast([P, 4, 2, 64]),
                                          ALU.mult).then_inc(soft, 1)
                    for h in range(NH):
                        key = ("tq", p, h)
                        dve.wait_ge(full[bank_of[key]], at(g, key))
                        for a_ in range(2):
                            r = slice(64 * a_, 64 * a_ + 64)
                            dve.tensor_tensor(pb[r, 4 * h:4 * h + 4, a_, :],
                                              bank(key)[r, :].rearrange("p (t q) -> p t q", q=P),
                                              enz[r, half(h)].rearrange("p (t q) -> p t q", q=P),
                                              ALU.mult).then_inc(pb_ready, 1)
                        dve.wait_ge(pb_ready, g * 8 + (4 * p + 2 * h + 2))
                        dve.sem_inc(free[bank_of[key]], 1)
                    for i in range(4):
                        key = ("w2", p, i)
                        if i % 2 == 0:
                            add_states("s2", s2, s2_ready, i // 2)
                        dve.wait_ge(full[bank_of[key]], at(g, key))
                        dve.tensor_tensor(atw[:, 2 * i:2 * i + 2, :, :].rearrange("p t a q -> p (t a) q"),
                                          bank(key)[:, :].rearrange("p (u q) -> p u q", q=P),
                                          causal[:, :].unsqueeze(1).to_broadcast([P, 4, P]),
                                          ALU.mult).then_inc(w2_ready, 1)
                        dve.wait_ge(w2_ready, g * 8 + (4 * p + i + 1))
                        dve.sem_inc(free[bank_of[key]], 1)
                    for i in range(4):
                        dve.wait_ge(squared, g * 8 + (4 * p + i + 1))
                        dve.tensor_reduce(ss[:, 2 * i:2 * i + 2, :], og[:, 2 * i:2 * i + 2, :, :], AX.X,
                                          ALU.add).then_inc(sumsq, 1)
                    dve.wait_ge(rooted, g * 2 + (p + 1))
                    dve.reciprocal(rs[:, :, :], ss[:, :, :]).then_inc(rooted_inv, 1)
                    dve.wait_ge(rooted_inv, g * 2 + (p + 1))
                    dve.wait_ge(g_silu, g * TB + TB)
                    for i in range(4):
                        key = ("o", p, i)
                        for t in (2 * i, 2 * i + 1):
                            for a_ in range(2):
                                c0 = (t % 2) * 256 + a_ * P
                                dve.scalar_tensor_tensor(og[:, t, a_, :], bank(key)[:, c0:c0 + DK], rs[:, t, a_:a_ + 1],
                                                         gq[:, t, 2 * p + a_, :], ALU.mult,
                                                         ALU.mult).then_inc(gated, 1)
                        dve.wait_ge(gated, g * 32 + (16 * p + 4 * i + 4))
                        dve.sem_inc(free[bank_of[key]], 1)
                    for h in range(NH):
                        for a_ in range(2):
                            key = ("to", p, a_, h)
                            dve.wait_ge(oth, g * 8 + (4 * p + 2 * h + a_ + 1))
                            dve.scalar_tensor_tensor(ogl[:, a_, half(h)], bank(key)[:, :], gnw[:, :],
                                                     ogh[:, a_, half(h)].bitcast(F32), ALU.mult,
                                                     ALU.subtract).then_inc(otl, 1)
                            dve.wait_ge(otl, g * 8 + (4 * p + 2 * h + a_ + 1))
                            dve.sem_inc(free[bank_of[key]], 1)
                    for h in range(NH):
                        for m in range(DC):
                            key = ("wo", p, m, h)
                            dve.wait_ge(full[bank_of[key]], at(g, key))
                            dve.tensor_tensor(core.x[:, m, half(h)], core.x[:, m, half(h)], bank(key)[:, :],
                                              ALU.add).then_inc(free[bank_of[key]], 1)
                    dve.wait_ge(free[bank_of[key]], at(g, key) + 1)


def layer3(nc, core, a):
    norm(nc, core, "n3a", core.x, True, core.eps5)
    decay_attention(nc, core, a["l3a_w"], a["l3a_cols"])
    norm(nc, core, "n3f", core.x, True, core.eps5)
    with nc.sbuf_tensor("l3_cwp", [P, T], BF16) as cwp:
        router(nc, core, "r3", "groups", 16, 4, a["l3_gate"], a["l3_ebias"], cwp)
        gated_ffn(nc, core, "f3", a["l3_w"], 17, True, cw_parts=cwp)


def layer2_attention(nc, core, a):
    norm(nc, core, "n2a", core.x, True, core.eps5)
    state_attention(nc, core, a)


def layer2(nc, core, a):
    norm(nc, core, "n2f", core.x, True, core.eps5)
    with nc.sbuf_tensor("l2_cwp", [P, T], BF16) as cwp:
        router(nc, core, "r2", "softmax_norm", 32, 4, a["l2_gate"], None, cwp)
        gated_ffn(nc, core, "f2", a["l2_w"], 24, True, cw_parts=cwp)


def layer0_attention(nc, core, a):
    norm(nc, core, "n0a", core.x, True, core.eps5)
    with nc.sbuf_tensor("a0_on", [P, 4, T], F32) as on:
        small_attention(nc, core, "a0", a, "l0a", on, core.x, a["l0a_tab"], a["l0a_bv"], True)


def small_attention(nc, core, name, a, key, on, dst, tables, v_bias, add_x):
    with nc.sbuf_tensor(name + "_qk", [P, 4, T], F32) as qk, \
            nc.sbuf_tensor(name + "_v", [P, TB, 16, 32], F32) as v, \
            nc.sbuf_tensor(name + "_staging", [P, 2, 4, T], F32) as staging:
        one = core.ones_r[:, 0:1].bitcast(F32).unsqueeze(1)
        zero = core.zero_r[:, 0:1].bitcast(F32).unsqueeze(1)
        fills = [(v[:, :, :, 16:32], one.unsqueeze(1).to_broadcast([P, TB, 16, 16])),
                 (staging[:, 0, :, :], zero.to_broadcast([P, 4, T])),
                 (staging[:, 1, :, :], one.to_broadcast([P, 4, T]))]
        project(nc, core, name + "p", 4, a[key + "_w"], tables, qk, True, a[key + "_wv"], v_bias, v, 16, 16, fills)
        attend(nc, core, name + "h", qk, 2, None, v, on, 0.25, True, 2, a["spread"], a["causal"], staging=staging)
    out_product(nc, core, name + "o", on, 4, a[key + "_wo"], a[key + "_bo"], dst, add_x)


def layer1_attention(nc, core, a):
    norm(nc, core, "n1a", core.x, True, core.eps5)
    with nc.sbuf_tensor("a1_qk", [P, 20, T], F32) as qk:
        with nc.sbuf_tensor("a1_v", [P, TB, 8, 64], F32) as v:
            project(nc, core, "a1p", 20, a["l1a_w"], a["l1a_tab"], qk, False, a["l1a_wv"], None, v, 8, 64)
            keys = nc.dram_tensor("l1_keys", (4, P, T), F32).ap()
            keys_out = nc.alloc_semaphore("l1a_keys_out")
            with nc.Block() as block:
                @block.sync
                def _(sp):
                    for c in range(4):
                        sp.dma_start(keys[c], qk[:, 16 + c, :]).then_inc(keys_out, 16)
                    sp.wait_ge(keys_out, 64)
            attend(nc, core, "a1h", qk, 16, keys, v, qk, 0.125, False, 4, a["spread"], a["window"], a["l1a_sink"])
        out_product(nc, core, "a1o", qk, 16, a["l1a_wo"], a["zero_cols"], core.x, True)


def layer1_mlp(nc, core, a):
    with nc.sbuf_tensor("l1f_gains", [P, 2, DC], F32) as gains:
        g_in, r_added = nc.alloc_semaphore("l1f_g"), nc.alloc_semaphore("l1f_r")
        with nc.Block() as block:
            @block.sync
            def _(sp):
                sp.dma_start(gains[:, :, :], a["l1f_gains"]).then_inc(g_in, 16)
                sp.wait_ge(g_in, 16)
        with nc.sbuf_tensor("l1f_r", [P, DC, T], F32) as r:
            norm(nc, core, "n1f", core.x, True, core.eps5, dst=r, split=False)
            norm(nc, core, "n1r", r, False, core.eps6, gain=gains[:, 0, :])
            with nc.Block() as block:
                @block.vector
                def _(dve):
                    dve.tensor_tensor(core.x[:, :, :], core.x[:, :, :], r[:, :, :], ALU.add).then_inc(r_added, 1)
        with nc.sbuf_tensor("a2_on", [P, 4, T], F32) as on:
            attn = on[:, 0:DC, :]
            small_attention(nc, core, "a2", a, "l1f", on, attn, None, None, False)
            resplit(nc, core, "s1f", gains[:, 1, :])
            with nc.sbuf_tensor("l1f_z_h", [P, T], F32R) as z_h, nc.sbuf_tensor("l1f_z_l", [P, T], F32R) as z_l:
                low_rank(nc, core, attn, a["l1f_a"], z_h, z_l)
                gated_ffn(nc, core, "f1", a["l1_w"], 8, False, z_h=z_h, z_l=z_l)


def low_rank(nc, core, attn, a_dram, z_h, z_l):
    with ExitStack() as ctx:
        sem = lambda n: nc.alloc_semaphore("lr_" + n)
        sb = lambda n, shape, dt=F32: ctx.enter_context(nc.sbuf_tensor("lr_" + n, shape, dt))
        a_in, split, at_ready, ah_ready, tanh_ready, z_ready, zh_ready, zl_ready = map(
            sem, ("a", "sp", "at", "ah", "th", "z", "zh", "zl"))
        aw = sb("aw", [P, DC, P])
        awh = sb("awh", [P, DC, P], F32R)
        awl = sb("awl", [P, DC, P], F32R)
        th = sb("th", [P, T])
        z = sb("zf", [P, T])
        block = ctx.enter_context(nc.Block())

        @block.sync
        def _(sp):
            sp.dma_start(aw[:, :, :], a_dram).then_inc(a_in, 16)

        @block.tensor
        def _(pe):
            pe.wait_ge(a_in, 16)
            for h in range(NH):
                for c in range(DC):
                    mm = pe.matmul(core.bank[h][:, :], aw[:, c, :], attn[:, c, half(h)], start=c == 0, stop=c == DC - 1)
                mm.then_inc(at_ready, 1)
            pe.wait_ge(split, 2)
            for h in range(NH):
                gemm3(pe, core.bank[2 + h][:, :], [awh[:, k, :] for k in range(DC)], [awl[:, k, :] for k in range(DC)],
                      [core.xh[:, k, half(h)] for k in range(DC)],
                      [core.xl[:, k, half(h)] for k in range(DC)]).then_inc(ah_ready, 1)

        @block.scalar
        def _(act):
            for h in range(NH):
                act.wait_ge(at_ready, h + 1)
                act.activation(th[:, half(h)], core.bank[h][:, :], ACT.Tanh).then_inc(tanh_ready, 1)
            for h in range(NH):
                act.wait_ge(z_ready, h + 1)
                act.activation(z_h[:, half(h)], z[:, half(h)], ACT.Copy).then_inc(zh_ready, 1)

        @block.vector
        def _(dve):
            dve.wait_ge(a_in, 16)
            dve.tensor_copy(awh[:, :, :], aw[:, :, :]).then_inc(split, 1)
            dve.wait_ge(split, 1)
            dve.tensor_tensor(awl[:, :, :], aw[:, :, :], awh[:, :, :].bitcast(F32), ALU.subtract).then_inc(split, 1)
            for h in range(NH):
                dve.wait_ge(tanh_ready, h + 1)
                dve.wait_ge(ah_ready, h + 1)
                dve.scalar_tensor_tensor(z[:, half(h)], th[:, half(h)], 0.1, core.bank[2 + h][:, :], ALU.mult,
                                         ALU.mult).then_inc(z_ready, 1)
            for h in range(NH):
                dve.wait_ge(zh_ready, h + 1)
                dve.tensor_tensor(z_l[:, half(h)], z[:, half(h)], z_h[:, half(h)].bitcast(F32),
                                  ALU.subtract).then_inc(zl_ready, 1)


def layer0(nc, core, a):
    norm(nc, core, "n0f", core.x, True, core.eps5)
    with nc.sbuf_tensor("l0_cwp", [P, T], BF16) as cwp, nc.sbuf_tensor("l0_cwf", [P, T], F32) as cwf, \
            nc.sbuf_tensor("l0_b2", [P, D], F32) as b2:
        router(nc, core, "r0", "softmax_bias", 16, 6, a["l0_gate"], a["l0_gbias"], cwp, cwf, b2, a["l0_b2"])
        gated_ffn(nc, core, "f0", a["l0_w"], 25, True, cw_parts=cwp, cw_f32=cwf, b2=b2)


def program(nc, a, stages=("0a", "0f", "1a", "1f", "2a", "2f", "3")):
    with ExitStack() as ctx:
        core = Core(nc, ctx)
        load_inputs(nc, core, a["x"], a["consts"])
        for s in stages:
            with nc.cleanup_on_exit():
                STAGES[s](nc, core, a)
        store_output(nc, core, a["out"])


STAGES = {"0a": layer0_attention, "0f": layer0, "1a": layer1_attention, "1f": layer1_mlp, "2a": layer2_attention,
          "2f": layer2, "3": layer3}


def by_feature(w):
    w = np.asarray(w)
    return np.ascontiguousarray(w.reshape(-1, P, w.shape[1]).transpose(1, 0, 2))


def ffn_weights(gate, up, down, b1, b3, owner, rows, kc=DC, gate_extra=None):
    hidden = gate.shape[1]
    n = -(-hidden // P)
    G, U, DN, B, S, cols = ffn_cols(kc)
    out = np.zeros((n, P, cols), np.float32)
    for c in range(n):
        lo, hi = c * P, min(hidden, (c + 1) * P)
        w = hi - lo
        for k in range(DC):
            out[c, :, G + k * P:G + k * P + w] = gate[k * P:(k + 1) * P, lo:hi]
            out[c, :, U + k * P:U + k * P + w] = up[k * P:(k + 1) * P, lo:hi]
        if gate_extra is not None:
            out[c, :gate_extra.shape[0], G + DC * P:G + DC * P + w] = gate_extra[:, lo:hi]
        out[c, :w, DN:DN + D] = down[lo:hi, :]
        if b1 is not None:
            out[c, :w, B] = b1[lo:hi]
            out[c, :w, B + 1] = b3[lo:hi]
        if owner is not None:
            for j in range(w):
                o = owner[lo + j]
                if o == 96:
                    out[c, 96, S + j] = 1.0
                else:
                    out[c, [o, 32 + o, 64 + o], S + j] = 1.0
    return out


def qk_chunk(w, bias):
    return np.concatenate([by_feature(w).reshape(P, DC * P), bias[:, None], np.roll(bias, 64)[:, None]], 1)


def rope_tables(angle, sign):
    s = np.sin(angle)
    s[:64] *= sign
    s[64:] *= -sign
    return np.ascontiguousarray(np.stack([np.cos(angle), s], 1).astype(np.float32))


def out_chunks(w):
    out = np.zeros((4, 4, 32, D), np.float32)
    out[:, :, :16] = w.reshape(4, 4, 16, D)
    return out.reshape(4, P, D)


def lay_out(inp):
    f = {k: np.asarray(v) for k, v in inp.items()}
    a = {}
    a["x"] = by_feature(f["L0_attn_x"][0].T)
    c = np.zeros((P, C_COLS), np.float32)
    c[:, C_ONES:C_ONES + P] = 1.0 / D
    c[:, C_IDENT:C_IDENT + P] = np.eye(P)
    a["consts"] = c
    a["zero_cols"] = np.zeros((P, DC), np.float32)
    k, q = np.arange(P)[:, None], np.arange(P)[None, :]
    m = np.zeros((P, 2, P + 4), np.float32)
    m[:, 0, :P][k > q] = -1e30
    m[:, 1, :P][k < q] = -1e30
    for j in range(4):
        m[32 * j + 16, 0, P + j] = 1.0
    a["causal"] = m
    m = np.zeros((P, 2, 2 * P), np.float32)
    c2 = np.arange(2 * P)[None, :]
    m[:, 0][(c2 >= k) & (c2 < k + 64)] = -1e30
    m[:, 1][(P + k - c2 >= 0) & (P + k - c2 < 64)] = -1e30
    a["window"] = m
    pos = np.arange(T, dtype=np.float32)
    r = np.arange(P)
    order = [np.array([(8 * g + (x % 64) // 8) * 16 + 2 * (x % 8) + x // 64 for x in r]) for g in range(2)]
    a["l0a_w"] = np.stack([qk_chunk(f[f"L0_attn_W{n}"].T[:, o], f[f"L0_attn_b{n}"][o]) for n in "qk" for o in order])
    a["l0a_wv"] = by_feature(f["L0_attn_Wv"].T)
    a["l0a_bv"] = f["L0_attn_bv"]
    freq = np.float32(10000.0) ** (-np.arange(0, 16, 2, dtype=np.float32) / np.float32(16))
    a["l0a_tab"] = rope_tables(pos[None, :] * freq[r % 8][:, None], -1.0)
    a["spread"] = (r[:, None] % 32 == np.arange(TB)).astype(np.float32)
    a["l0a_wo"] = out_chunks(f["L0_attn_Wo"].T)
    a["l0a_bo"] = np.ascontiguousarray(f["L0_attn_bo"].reshape(DC, P).T)
    w = f["L1_attn_W_qkv"]
    rows = lambda h0, h1: np.concatenate([h0 * 64 + np.arange(32), h1 * 64 + np.arange(32),
                                          h0 * 64 + 32 + np.arange(32), h1 * 64 + 32 + np.arange(32)])
    cols = [rows(8 * g + m, 8 * g + 4 + m) for g in range(4) for m in range(4)]
    cols += [2048 + rows(2 * g, 2 * g + 1) for g in range(4)]
    a["l1a_w"] = np.stack([qk_chunk(w[:, c], np.zeros(P, np.float32)) for c in cols])
    a["l1a_wv"] = by_feature(w[:, 2560:3072])
    freq = np.float32(1.0 / 1024.0) ** np.linspace(0.0, 1.0, 16, dtype=np.float32)
    freq = np.concatenate([freq, np.zeros(16, np.float32)])
    a["l1a_tab"] = rope_tables(pos[None, :] * freq[r % 32][:, None], 1.0)
    wo = f["L1_attn_W_out"]
    a["l1a_wo"] = np.stack([np.concatenate([wo[(8 * g + m) * 64:][:64], wo[(8 * g + 4 + m) * 64:][:64]])
                            for g in range(4) for m in range(4)])
    a["l1a_sink"] = np.ascontiguousarray(f["L1_attn_s"][0].reshape(4, 2, 4).transpose(0, 2, 1).reshape(32))
    a["l1f_w"] = np.stack([qk_chunk(f[f"L1_ffn_W{n}"].T[:, o], np.zeros(P, np.float32)) for n in "qk" for o in order])
    a["l1f_wv"] = by_feature(f["L1_ffn_Wv"].T)
    a["l1f_wo"] = out_chunks(f["L1_ffn_Wo"].T)
    a["l1f_bo"] = np.zeros((P, DC), np.float32)
    a["l1f_gains"] = np.ascontiguousarray(np.stack([f[f"L1_ffn_ln{n}_w"].reshape(DC, P).T for n in (1, 2)], 1))
    aw = np.zeros((D, P), np.float32)
    aw[:, :16] = f["L1_ffn_A"]
    a["l1f_a"] = by_feature(aw)
    a["l1_w"] = ffn_weights(f["L1_ffn_W_in_base"].T, f["L1_ffn_W_up_base"].T, f["L1_ffn_W_down"].T, None, None, None,
                            0, kc=3, gate_extra=f["L1_ffn_B"])
    E, H = 16, 176
    g = np.concatenate([f["L0_ffn_w1"].reshape(E * H, D), f["L0_ffn_ws1"]]).T
    u = np.concatenate([f["L0_ffn_w3"].reshape(E * H, D), f["L0_ffn_ws3"]]).T
    dn = np.concatenate([f["L0_ffn_w2"].transpose(0, 2, 1).reshape(E * H, D), f["L0_ffn_ws2"].T])
    b1 = np.concatenate([f["L0_ffn_b1"].reshape(-1), f["L0_ffn_bs1"]])
    b3 = np.concatenate([f["L0_ffn_b3"].reshape(-1), f["L0_ffn_bs3"]])
    own = [e for e in range(E) for _ in range(H)] + [96] * 352
    a["l0_w"] = ffn_weights(g, u, dn, b1, b3, own, E)
    a["l0_gate"] = by_feature(f["L0_ffn_gate_w"].T)
    a["l0_gbias"] = f["L0_ffn_gate_b"]
    b2 = np.zeros((P, D), np.float32)
    for j in range(3):
        b2[32 * j:32 * j + E] = f["L0_ffn_b2"]
    b2[96] = f["L0_ffn_bs2"]
    a["l0_b2"] = b2
    ws1 = np.zeros((D, P), np.float32)
    ws1[:, :16] = f["L2_attn_Ws1"].T
    a["l2a_ws1"] = by_feature(ws1)
    ws2 = np.zeros((4, P, 2, P + 1), np.float32)
    ws2[:, :16, :, :P] = f["L2_attn_Ws2"].reshape(4, 2, P, 16).transpose(0, 3, 1, 2)
    ws2[:, :, :, P] = f["L2_attn_bs2"].reshape(4, 2, P).transpose(0, 2, 1)
    a["l2a_ws2"] = ws2
    chunk = lambda w, h: by_feature(w.T[:, h * P:(h + 1) * P]).reshape(P, DC * P)
    a["l2a_wqk"] = np.stack([chunk(f[f"L2_attn_W{n}"], h) for h in range(16) for n in "qk"])
    a["l2a_wvg"] = np.stack([by_feature(f[f"L2_attn_W{n}"].T[:, g * 512:(g + 1) * 512])
                             for g in range(4) for n in "vg"])
    a["l2a_wo"] = np.ascontiguousarray(f["L2_attn_Wo"].T.reshape(8, 2, P, D).transpose(0, 2, 1, 3))
    freq = np.float32(1.0) / np.float32(10000.0) ** (np.arange(0, 128, 2, dtype=np.float32) / np.float32(128))
    a["l2a_tab"] = rope_tables(pos[None, :] * freq[r % 64][:, None], -1.0)
    a["l2a_mask"] = (k <= q).astype(np.float32)
    a["l2a_gnw"] = f["L2_attn_g_norm_weight"].reshape(P, 1)
    E, H = 32, 96
    gu = f["L2_ffn_gate_up_proj"]
    g = gu[:, :, :H].transpose(1, 0, 2).reshape(D, E * H)
    u = gu[:, :, H:].transpose(1, 0, 2).reshape(D, E * H)
    dn = f["L2_ffn_down_proj"].reshape(E * H, D)
    a["l2_w"] = ffn_weights(g, u, dn, None, None, [e for e in range(E) for _ in range(H)], E)
    a["l2_gate"] = by_feature(f["L2_ffn_gate"])
    a["l3a_w"] = by_feature(np.concatenate([f["L3_attn_Wv"], f["L3_attn_Wq"], f["L3_attn_Wg"], f["L3_attn_Wo"]], 1))
    vec = [np.repeat(f["L3_attn_beta"], 16), f["L3_attn_ln_g"], f["L3_attn_ln_b"]]
    a["l3a_cols"] = np.ascontiguousarray(np.stack([v.reshape(DC, P).T for v in vec], 1))
    E, H = 16, 128
    g = np.concatenate([f["L3_ffn_gate_proj"].reshape(E * H, D), f["L3_ffn_shared_gate"]]).T
    u = np.concatenate([f["L3_ffn_up_proj"].reshape(E * H, D), f["L3_ffn_shared_up"]]).T
    dn = np.concatenate([f["L3_ffn_down_proj"].transpose(0, 2, 1).reshape(E * H, D), f["L3_ffn_shared_down"].T])
    a["l3_w"] = ffn_weights(g, u, dn, None, None, [e for e in range(E) for _ in range(H)] + [96] * H, E)
    a["l3_gate"] = by_feature(f["L3_ffn_gate_weight"].T)
    a["l3_ebias"] = f["L3_ffn_expert_bias"]
    return a


def kernel(**inputs):
    import concourse.bacc as bacc
    from concourse.bass_utils import run_bass_kernel_spmd

    nc = bacc.Bacc("TRN2", target_bir_lowering=False, num_devices=1)
    arrays = {f"in_{k}_dram": np.ascontiguousarray(v) for k, v in lay_out(inputs).items()}
    a = {k[3:-5]: nc.dram_tensor(k, v.shape, mybir.dt.from_np(v.dtype), kind="ExternalInput").ap()
         for k, v in arrays.items()}
    a["out"] = nc.dram_tensor("out_0_dram", (P, DC, T), F32, kind="ExternalOutput").ap()
    program(nc, a)
    r = run_bass_kernel_spmd(nc, [arrays], core_ids=[0])
    got = r.results[0]["out_0_dram"]
    return np.ascontiguousarray(got.transpose(1, 0, 2).reshape(D, T).T)[None]
```
